# Optimizing a Trainium2 kernel written in Bass

```python
import numpy as np
import jax
import jax.numpy as jnp

def _softmax(x, axis=-1):
    return jax.nn.softmax(x, axis=axis)

def _gelu(x):
    return jax.nn.gelu(x, approximate=True)

def _silu(x):
    return jax.nn.silu(x)

def _sigmoid(x):
    return jax.nn.sigmoid(x)

def _layernorm(x, axis=-1, eps=1e-05):
    m = jnp.mean(x, axis=axis, keepdims=True)
    v = jnp.var(x, axis=axis, keepdims=True)
    return (x - m) / jnp.sqrt(v + eps)

def _scatter_add(tgt, idx, src, axis=0):
    return tgt.at[idx].add(src)

def _segment_sum(src, seg, n):
    return jax.ops.segment_sum(src, seg, n)
kernel_name = 'mk_seq_postln_d2_jaxref_r8_eebf5f'

def setup_inputs(seed: int=0):
    np.random.seed(seed)
    _w = jnp.asarray

    def _L0_attn_setup():
        import jax, jax.numpy as jnp
        import numpy as np
        B, T, C, I = (4, 512, 128, 512)

        def rmsnorm(x, w, eps=1e-06):
            return x * jax.lax.rsqrt(jnp.mean(x * x, axis=-1, keepdims=True) + eps) * w

        def shift(h):
            return jnp.pad(h, ((0, 0), (1, 0), (0, 0)))[:, :-1]

        def wkv_scan(k, v, w, u):
            ew = jnp.exp(jnp.clip(w, -20.0, 20.0))

            def step(carry, kv):
                a, b = carry
                kt, vt = kv
                ekt = jnp.exp(jnp.clip(u + kt, -20.0, 20.0))
                out = (a + ekt * vt) / (b + ekt + 1e-08)
                ek = jnp.exp(jnp.clip(kt, -20.0, 20.0))
                return ((ew * a + ek * vt, ew * b + ek), out)
            init = (jnp.zeros((k.shape[0], k.shape[2]), jnp.float32), jnp.zeros((k.shape[0], k.shape[2]), jnp.float32))
            _, out = jax.lax.scan(step, init, (k.swapaxes(0, 1), v.swapaxes(0, 1)))
            return out.swapaxes(0, 1)
        key = jax.random.key(seed)
        ks = jax.random.split(key, 16)
        s = 1.0 / np.sqrt(C)
        si = 1.0 / np.sqrt(I)
        return {'x': jax.random.normal(ks[0], (B, T, C), jnp.float32), 'ln1_w': jnp.ones((C,), jnp.float32), 'ln2_w': jnp.ones((C,), jnp.float32), 'time_decay': jax.random.normal(ks[1], (C,), jnp.float32) * 0.1 - 5.0, 'time_first': jax.random.normal(ks[2], (C,), jnp.float32) * 0.01, 'time_mix_k': jnp.full((C,), 0.5, jnp.float32), 'time_mix_v': jnp.full((C,), 0.5, jnp.float32), 'time_mix_r': jnp.full((C,), 0.5, jnp.float32), 'W_key': jax.random.normal(ks[3], (C, C), jnp.float32) * s, 'W_value': jax.random.normal(ks[4], (C, C), jnp.float32) * s, 'W_recept': jax.random.normal(ks[5], (C, C), jnp.float32) * s, 'W_out': jax.random.normal(ks[6], (C, C), jnp.float32) * s, 'time_mix_k2': jnp.full((C,), 0.5, jnp.float32), 'time_mix_r2': jnp.full((C,), 0.5, jnp.float32), 'W_key2': jax.random.normal(ks[7], (C, I), jnp.float32) * s, 'W_value2': jax.random.normal(ks[8], (I, C), jnp.float32) * si, 'W_recept2': jax.random.normal(ks[9], (C, C), jnp.float32) * s}
    _L0_attn_in = _L0_attn_setup()

    def _L0_ffn_setup():
        import jax, jax.numpy as jnp
        import numpy as np
        E = 8
        K = 2
        CAP_FACTOR = 1.0
        key = jax.random.key(seed)
        k0, k1, k2, k3 = jax.random.split(key, 4)
        B, S, M, H = (4, 256, 128, 512)
        x = jax.random.normal(k0, (B, S, M), jnp.float32)
        wg = jax.random.normal(k1, (M, E), jnp.float32) * 0.02
        w1 = jax.random.normal(k2, (E, M, H), jnp.float32) * 0.02
        b1 = jnp.zeros((E, H), jnp.float32)
        w2 = jax.random.normal(k3, (E, H, M), jnp.float32) * 0.02
        b2 = jnp.zeros((E, M), jnp.float32)
        return {'x': x, 'wg': wg, 'w1': w1, 'b1': b1, 'w2': w2, 'b2': b2}
    _L0_ffn_in = _L0_ffn_setup()

    def _L1_attn_setup():
        import jax, jax.numpy as jnp
        import numpy as np
        import math
        B, L, DIM = (2, 256, 128)
        HEADS = 16
        DH = DIM // HEADS
        M_IALSH = 2
        U_IALSH = 0.75
        NEG = -10000.0

        def _ialsh_mask(qkh, hash_a):
            norms = jnp.linalg.norm(qkh, axis=-1, keepdims=True)
            max_norm = jnp.max(norms, axis=2, keepdims=True)
            xk = qkh * (U_IALSH / jnp.maximum(max_norm, 1e-12))
            nk2 = jnp.sum(xk * xk, axis=-1, keepdims=True)
            P = jnp.concatenate([xk, 0.5 - nk2, 0.5 - nk2 * nk2], axis=-1)
            q_unit = qkh / jnp.maximum(norms, 1e-12)
            zeros = jnp.zeros_like(nk2)
            Q = jnp.concatenate([q_unit, zeros, zeros], axis=-1)
            hq = Q @ hash_a >= 0.0
            hk = P @ hash_a >= 0.0
            same = hq[..., :, None] == hk[..., None, :]
            return jnp.where(same, 0.0, NEG).astype(qkh.dtype)
        key = jax.random.key(seed)
        k0, k1, k2, k3 = jax.random.split(key, 4)
        return {'hidden_states': jax.random.normal(k0, (B, L, DIM), jnp.float32), 'qk_w': jax.random.normal(k1, (DIM, DIM), jnp.float32) * 0.02, 'qk_b': jnp.zeros((DIM,), jnp.float32), 'v_w': jax.random.normal(k2, (DIM, DIM), jnp.float32) * 0.02, 'v_b': jnp.zeros((DIM,), jnp.float32), 'hash_a': jax.random.normal(k3, (DH + M_IALSH,), jnp.float32)}
    _L1_attn_in = _L1_attn_setup()

    def _L1_ffn_setup():
        import jax, jax.numpy as jnp
        import numpy as np
        NUM_EXPERTS = 8
        HIDDEN = 128
        FFN = 512
        BATCH = 2
        SEQ = 256
        key = jax.random.key(seed)
        k_x, k_g, k_u, k_d = jax.random.split(key, 4)
        scale_in = 1.0 / np.sqrt(HIDDEN)
        scale_mid = 1.0 / np.sqrt(FFN)
        return {'hidden_states': jax.random.normal(k_x, (BATCH, SEQ, HIDDEN), dtype=jnp.float32), 'Wg': jax.random.normal(k_g, (NUM_EXPERTS, HIDDEN, FFN), dtype=jnp.float32) * scale_in, 'Wu': jax.random.normal(k_u, (NUM_EXPERTS, HIDDEN, FFN), dtype=jnp.float32) * scale_in, 'Wd': jax.random.normal(k_d, (NUM_EXPERTS, FFN, HIDDEN), dtype=jnp.float32) * scale_mid}
    _L1_ffn_in = _L1_ffn_setup()
    _d = {'L0_attn_x': _L0_attn_in['x'], 'L0_attn_ln1_w': _L0_attn_in['ln1_w'], 'L0_attn_ln2_w': _L0_attn_in['ln2_w'], 'L0_attn_time_decay': _L0_attn_in['time_decay'], 'L0_attn_time_first': _L0_attn_in['time_first'], 'L0_attn_time_mix_k': _L0_attn_in['time_mix_k'], 'L0_attn_time_mix_v': _L0_attn_in['time_mix_v'], 'L0_attn_time_mix_r': _L0_attn_in['time_mix_r'], 'L0_attn_W_key': _L0_attn_in['W_key'], 'L0_attn_W_value': _L0_attn_in['W_value'], 'L0_attn_W_recept': _L0_attn_in['W_recept'], 'L0_attn_W_out': _L0_attn_in['W_out'], 'L0_attn_time_mix_k2': _L0_attn_in['time_mix_k2'], 'L0_attn_time_mix_r2': _L0_attn_in['time_mix_r2'], 'L0_attn_W_key2': _L0_attn_in['W_key2'], 'L0_attn_W_value2': _L0_attn_in['W_value2'], 'L0_attn_W_recept2': _L0_attn_in['W_recept2'], 'L0_ffn_wg': _L0_ffn_in['wg'], 'L0_ffn_w1': _L0_ffn_in['w1'], 'L0_ffn_b1': _L0_ffn_in['b1'], 'L0_ffn_w2': _L0_ffn_in['w2'], 'L0_ffn_b2': _L0_ffn_in['b2'], 'L1_attn_qk_w': _L1_attn_in['qk_w'], 'L1_attn_qk_b': _L1_attn_in['qk_b'], 'L1_attn_v_w': _L1_attn_in['v_w'], 'L1_attn_v_b': _L1_attn_in['v_b'], 'L1_attn_hash_a': _L1_attn_in['hash_a'], 'L1_ffn_Wg': _L1_ffn_in['Wg'], 'L1_ffn_Wu': _L1_ffn_in['Wu'], 'L1_ffn_Wd': _L1_ffn_in['Wd']}
    _x0 = _d['L0_attn_x']
    _d['L0_attn_x'] = jax.random.normal(jax.random.fold_in(jax.random.key(seed), 1), (2, 1024, 128), dtype=_x0.dtype)
    del _x0
    return _d

def reference(L0_attn_x, L0_attn_ln1_w, L0_attn_ln2_w, L0_attn_time_decay, L0_attn_time_first, L0_attn_time_mix_k, L0_attn_time_mix_v, L0_attn_time_mix_r, L0_attn_W_key, L0_attn_W_value, L0_attn_W_recept, L0_attn_W_out, L0_attn_time_mix_k2, L0_attn_time_mix_r2, L0_attn_W_key2, L0_attn_W_value2, L0_attn_W_recept2, L0_ffn_wg, L0_ffn_w1, L0_ffn_b1, L0_ffn_w2, L0_ffn_b2, L1_attn_qk_w, L1_attn_qk_b, L1_attn_v_w, L1_attn_v_b, L1_attn_hash_a, L1_ffn_Wg, L1_ffn_Wu, L1_ffn_Wd):

    def _L0_attn_ref(x, ln1_w, ln2_w, time_decay, time_first, time_mix_k, time_mix_v, time_mix_r, W_key, W_value, W_recept, W_out, time_mix_k2, time_mix_r2, W_key2, W_value2, W_recept2):
        import jax, jax.numpy as jnp
        import numpy as np
        B, T, C, I = (4, 512, 128, 512)

        def rmsnorm(x, w, eps=1e-06):
            return x * jax.lax.rsqrt(jnp.mean(x * x, axis=-1, keepdims=True) + eps) * w

        def shift(h):
            return jnp.pad(h, ((0, 0), (1, 0), (0, 0)))[:, :-1]

        def wkv_scan(k, v, w, u):
            ew = jnp.exp(jnp.clip(w, -20.0, 20.0))

            def step(carry, kv):
                a, b = carry
                kt, vt = kv
                ekt = jnp.exp(jnp.clip(u + kt, -20.0, 20.0))
                out = (a + ekt * vt) / (b + ekt + 1e-08)
                ek = jnp.exp(jnp.clip(kt, -20.0, 20.0))
                return ((ew * a + ek * vt, ew * b + ek), out)
            init = (jnp.zeros((k.shape[0], k.shape[2]), jnp.float32), jnp.zeros((k.shape[0], k.shape[2]), jnp.float32))
            _, out = jax.lax.scan(step, init, (k.swapaxes(0, 1), v.swapaxes(0, 1)))
            return out.swapaxes(0, 1)
        h = rmsnorm(x, ln1_w)
        sh = shift(h)
        xk = h * time_mix_k + sh * (1 - time_mix_k)
        xv = h * time_mix_v + sh * (1 - time_mix_v)
        xr = h * time_mix_r + sh * (1 - time_mix_r)
        k = xk @ W_key
        v = xv @ W_value
        r = jax.nn.sigmoid(xr @ W_recept)
        w = -jnp.exp(time_decay)
        u = time_first
        wkv = wkv_scan(k.astype(jnp.float32), v.astype(jnp.float32), w, u).astype(x.dtype)
        x = x + r * wkv @ W_out
        h = rmsnorm(x, ln2_w)
        sh = shift(h)
        xk = h * time_mix_k2 + sh * (1 - time_mix_k2)
        xr = h * time_mix_r2 + sh * (1 - time_mix_r2)
        k2 = jnp.square(jax.nn.relu(xk @ W_key2))
        r2 = jax.nn.sigmoid(xr @ W_recept2)
        return x + r2 * (k2 @ W_value2)

    def _L0_ffn_ref(x, wg, w1, b1, w2, b2):
        import jax, jax.numpy as jnp
        import numpy as np
        E = 8
        K = 2
        CAP_FACTOR = 1.0
        B, S, M = x.shape
        N = B * S
        capacity = int(CAP_FACTOR * K * N // E)
        xt = x.reshape(N, M)
        logits = xt @ wg
        scores = jax.nn.softmax(logits, axis=-1)
        topv, topi = jax.lax.top_k(scores, K)
        topv = topv / jnp.sum(topv, axis=-1, keepdims=True)
        masks = jax.nn.one_hot(topi.T, E, dtype=jnp.int32)
        flat = masks.reshape(K * N, E)
        locs = jnp.cumsum(flat, axis=0) - 1
        pos = jnp.sum(locs * flat, axis=-1).reshape(K, N).T
        valid = pos < capacity
        gate = topv * valid.astype(topv.dtype)
        pos_c = jnp.where(valid, pos, 0)
        xk = xt[:, None, :] * valid[..., None].astype(xt.dtype)
        disp = jnp.zeros((E, capacity, M), xt.dtype)
        disp = disp.at[topi, pos_c].add(xk)
        h = jax.nn.relu(jnp.einsum('ecm,emh->ech', disp, w1) + b1[:, None, :])
        y = jnp.einsum('ech,ehm->ecm', h, w2) + b2[:, None, :]
        out = jnp.sum(gate[..., None] * y[topi, pos_c], axis=1)
        return out.reshape(B, S, M)

    def _L1_attn_ref(hidden_states, qk_w, qk_b, v_w, v_b, hash_a):
        import jax, jax.numpy as jnp
        import numpy as np
        import math
        B, L, DIM = (2, 256, 128)
        HEADS = 16
        DH = DIM // HEADS
        M_IALSH = 2
        U_IALSH = 0.75
        NEG = -10000.0

        def _ialsh_mask(qkh, hash_a):
            norms = jnp.linalg.norm(qkh, axis=-1, keepdims=True)
            max_norm = jnp.max(norms, axis=2, keepdims=True)
            xk = qkh * (U_IALSH / jnp.maximum(max_norm, 1e-12))
            nk2 = jnp.sum(xk * xk, axis=-1, keepdims=True)
            P = jnp.concatenate([xk, 0.5 - nk2, 0.5 - nk2 * nk2], axis=-1)
            q_unit = qkh / jnp.maximum(norms, 1e-12)
            zeros = jnp.zeros_like(nk2)
            Q = jnp.concatenate([q_unit, zeros, zeros], axis=-1)
            hq = Q @ hash_a >= 0.0
            hk = P @ hash_a >= 0.0
            same = hq[..., :, None] == hk[..., None, :]
            return jnp.where(same, 0.0, NEG).astype(qkh.dtype)
        b, l, d = hidden_states.shape
        qk = hidden_states @ qk_w.T + qk_b
        v = hidden_states @ v_w.T + v_b

        def split(x):
            return x.reshape(b, l, HEADS, DH).transpose(0, 2, 1, 3)
        qkh, vh = (split(qk), split(v))
        scores = jnp.einsum('bhqd,bhkd->bhqk', qkh, qkh) / math.sqrt(DH)
        scores = scores + _ialsh_mask(qkh, hash_a)
        probs = jax.nn.softmax(scores, axis=-1)
        ctx = jnp.einsum('bhqk,bhkd->bhqd', probs, vh)
        return ctx.transpose(0, 2, 1, 3).reshape(b, l, d)

    def _L1_ffn_ref(hidden_states, Wg, Wu, Wd):
        import jax, jax.numpy as jnp
        import numpy as np
        NUM_EXPERTS = 8
        HIDDEN = 128
        FFN = 512
        BATCH = 2
        SEQ = 256
        B, S, H = hidden_states.shape
        x = hidden_states.reshape(-1, H)

        def expert_step(acc, w):
            wg, wu, wd = w
            h = jax.nn.silu(x @ wg) * (x @ wu)
            return (acc + h @ wd, None)
        acc, _ = jax.lax.scan(expert_step, jnp.zeros_like(x), (Wg, Wu, Wd))
        return acc.reshape(B, S, H)
    x = L0_attn_x
    x = _layernorm(x + _L0_attn_ref(x, L0_attn_ln1_w, L0_attn_ln2_w, L0_attn_time_decay, L0_attn_time_first, L0_attn_time_mix_k, L0_attn_time_mix_v, L0_attn_time_mix_r, L0_attn_W_key, L0_attn_W_value, L0_attn_W_recept, L0_attn_W_out, L0_attn_time_mix_k2, L0_attn_time_mix_r2, L0_attn_W_key2, L0_attn_W_value2, L0_attn_W_recept2), axis=-1)
    x = _layernorm(x + _L0_ffn_ref(x, L0_ffn_wg, L0_ffn_w1, L0_ffn_b1, L0_ffn_w2, L0_ffn_b2), axis=-1)
    x = _layernorm(x + _L1_attn_ref(x, L1_attn_qk_w, L1_attn_qk_b, L1_attn_v_w, L1_attn_v_b, L1_attn_hash_a), axis=-1)
    x = _layernorm(x + _L1_ffn_ref(x, L1_ffn_Wg, L1_ffn_Wu, L1_ffn_Wd), axis=-1)
    return x

_drawn_inputs = setup_inputs


def setup_inputs(seed=0):
    import zlib

    import numpy as np

    out = dict(_drawn_inputs(seed))
    spreads = {'L0_attn_ln1_w': (1.0, 0.6),
     'L0_attn_ln2_w': (1.0, 0.2),
     'L0_attn_time_mix_k': (0.5, 0.6),
     'L0_attn_time_mix_v': (0.5, 0.6),
     'L0_attn_time_mix_r': (0.5, 0.6),
     'L0_attn_time_mix_k2': (0.5, 0.2),
     'L0_attn_time_mix_r2': (0.5, 0.6),
     'L0_ffn_b1': (0.0, 0.1),
     'L0_ffn_b2': (0.0, 0.1),
     'L1_attn_qk_b': (0.0, 0.1),
     'L1_attn_v_b': (0.0, 0.1)}
    factors = {'L0_attn_time_decay': 8.0, 'L0_attn_time_first': 200.0, 'L0_attn_W_recept': 2.683}
    for name, (base, spread) in spreads.items():
        noise = np.random.default_rng([zlib.crc32(name.encode()), seed]).standard_normal(out[name].shape)
        drawn = base * np.exp(spread * noise) if base else spread * noise
        out[name] = jnp.asarray(drawn.astype(out[name].dtype))
    for name, factor in factors.items():
        out[name] = (out[name] * factor).astype(out[name].dtype)
    return out
```

```python
import math
from contextlib import ExitStack

import concourse.bass as bass
from concourse import mybir

ALU = mybir.AluOpType
ACT = mybir.ActivationFunctionType
AX = mybir.AxisListType
F32 = mybir.dt.float32
F16 = mybir.dt.float16
F32R = mybir.dt.float32r

P = 128
B, T, C = 2, 1024, 128
N = B * T
NT = N // P
CH = 512
NC = N // CH
TPC = CH // P
CPB = T // CH
E = 8
H = 512
HC = H // P
TOPK = 2
CAP = TOPK * N // E
HEADS = 16
DH = C // HEADS
HPG = 4
HG = HEADS // HPG
NG = B * HG
GT = T // P
AUG = P // HPG
HASH = DH + 2
U_HASH = 0.75
MASK = 10000.0
SAFE_SCORE = 60.0
RMS_EPS = 1e-6
LN_EPS = 1e-5
WKV_EPS = 1e-8
CLIP = 20.0
W_SCALE = 256.0

LN1, LN2, DECAY, FIRST, MIXK, MIXV, MIXR, MIXK2, MIXR2, B1 = range(10)
NCOLS = B1 + E * HC


class Shared:
    pass


def schedule(chunks, phases):
    return [(s - p, p) for s in range(chunks + phases - 1) for p in reversed(range(phases)) if 0 <= s - p < chunks]


def chain(eng, sem):
    count = [0]

    def link(ins):
        count[0] += 1
        ins.then_inc(sem, 1)
        eng.wait_ge(sem, count[0])

    return link


def shifted(buf, c):
    b, o = c // CPB, 1 + (c % CPB) * CH
    return buf[:, b, o:o + CH], buf[:, b, o - 1:o - 1 + CH]


def scale_raw(nc, pool, g, e):
    if e < E:
        pool.wait_ge(g.raw0_in[e], 32)
        nc.gpsimd.tensor_scalar(g.raw0[:, e, :], g.raw0[:, e, :], W_SCALE, 1.0, ALU.mult, ALU.mult).then_inc(g.raw0_scaled, 1)
    if e >= 1:
        pool.wait_ge(g.w0h_ready, e)
        nc.gpsimd.tensor_tensor(g.w0l[:, e - 1, :], g.raw0[:, e - 1, :], g.w0h[:, e - 1, :], ALU.subtract).then_inc(g.w0l_ready, 1)


def high_part(nc, act, g, e):
    act.wait_ge(g.raw0_scaled, e + 1)
    nc.scalar.activation(g.w0h[:, e, :], g.raw0[:, e, :], ACT.Copy).then_inc(g.w0h_ready, 1)


def time_mix(nc, g, a):
    with ExitStack() as ctx:
        def sb(name, shape, dt=F32):
            return ctx.enter_context(nc.sbuf_tensor(name, shape, dt))

        def sem(name):
            return ctx.enter_context(nc.semaphore(name))

        rows = sb("rows", [64, P])
        w_k, w_v, w_r, w_o = (sb(n, [P, P]) for n in ("w_k", "w_v", "w_r", "w_o"))
        junk = sb("junk", [P, P])
        ss = sb("ss", [P, NT])
        ms = sb("ms", [P, NT])
        rstd = sb("rstd", [P, NT])
        ew = sb("ew", [P, 4])
        hx = sb("hx", [P, 2, TPC, P])
        hT = sb("hT", [P, B, 1 + T])
        diff = sb("diff", [P, CH])
        xm = sb("xm", [P, 2, 3, CH])
        ex = sb("ex", [P, 2, 3, CH])
        ekv = sb("ekv", [P, CH])
        ektv = sb("ektv", [P, CH])
        aS = sb("aS", [P, B, 1 + T])
        bS = sb("bS", [P, B, 1 + T])
        den = sb("den", [P, CH])
        rden = sb("rden", [P, CH])
        yT = sb("yT", [P, 2, CH])
        pb = g.pb
        tr_bank = lambda c: pb[:, c % 2, :]
        k_ps, v_ps, r_ps = pb[:, 2, :], pb[:, 3, :], pb[:, 4, :]
        out_bank = lambda c: pb[:, 5 + c % 2, :]

        x_in = [sem(f"x_in{c}") for c in range(NC)]
        rows_in = sem("rows_in")
        w_in = sem("w_in")
        wo_in = sem("wo_in")
        ident_ready = sem("ident_ready")
        cols_turned = sem("cols_turned")
        zeros_ready = sem("zeros_ready")
        edecay_ready = sem("edecay_ready")
        wclip_ready = sem("wclip_ready")
        ew_ready = sem("ew_ready")
        ss_ready = sem("ss_ready")
        ms_ready = sem("ms_ready")
        rstd_ready = sem("rstd_ready")
        hx_ready = sem("hx_ready")
        turned = sem("turned")
        hT_ready = sem("hT_ready")
        xm_ready = sem("xm_ready")
        kvr_ready = sem("kvr_ready")
        ex_ready = sem("ex_ready")
        v_used = sem("v_used")
        y_ready = sem("y_ready")
        out_ready = sem("out_ready")
        x1_ready = sem("x1_ready")
        dve_step = sem("tm_dve_step")

        block = ctx.enter_context(nc.Block())
        plan = schedule(NC, 5)

        @block.sync
        def _(sp):
            for c in range(NC):
                sp.dma_start(g.x0[:, c * TPC:(c + 1) * TPC, :], a.x_tiles[:, c * TPC:(c + 1) * TPC, :]).then_inc(x_in[c], 16)
            for w, src in ((w_k, a.W_key), (w_v, a.W_value), (w_r, a.W_recept)):
                sp.dma_start(w[:, :], src).then_inc(w_in, 16)
            sp.dma_start(w_o[:, :], a.W_out).then_inc(wo_in, 16)
            for e in range(E):
                sp.dma_start(g.raw0[:, e, 0:H], a.w1[e]).then_inc(g.raw0_in[e], 16)
                sp.dma_start(g.raw0[:, e, H:2 * H].rearrange("p (k c) -> p k c", k=HC),
                             a.w2[e].rearrange("(k p) c -> p k c", p=P)).then_inc(g.raw0_in[e], 16)

        @block.gpsimd
        def _(pool):
            nc.gpsimd.memset(g.ident[:, :], 0.0).then_inc(ident_ready, 1)
            pool.wait_ge(ident_ready, 1)
            nc.gpsimd.affine_select(out=g.ident[:, :], in_=g.ident[:, :], compare_op=ALU.not_equal, fill=1.0,
                                    base=0, pattern=[[-1, P]], channel_multiplier=1).then_inc(ident_ready, 1)
            nc.gpsimd.memset(g.minus_half[:, :], -0.5).then_inc(ident_ready, 1)
            pool.wait_ge(ident_ready, 3)
            for c, phase in plan:
                if phase == 0:
                    t = slice(c * TPC, (c + 1) * TPC)
                    pool.wait_ge(ms_ready, c + 1)
                    nc.gpsimd.tensor_tensor(rstd[:, t], ms[:, t], g.minus_half[:, 0:TPC], ALU.pow).then_inc(rstd_ready, 1)
                    scale_raw(nc, pool, g, c)

        @block.scalar
        def _(act):
            for i, v in enumerate((a.ln1_w, a.ln2_w, a.decay, a.first, a.mix_k, a.mix_v, a.mix_r, a.mix_k2, a.mix_r2)):
                act.dma_start(rows[i:i + 1, :], v.rearrange("(a n) -> a n", a=1)).then_inc(rows_in, 16)
            act.dma_start(rows[B1:NCOLS, :], a.b1.rearrange("e (k p) -> (e k) p", p=P)).then_inc(rows_in, 16)
            for c, phase in plan:
                if phase == 0:
                    act.wait_ge(x_in[c], 16)
                    for t in range(c * TPC, (c + 1) * TPC):
                        last = nc.scalar.activation(junk[:, :], g.x0[:, t, :], ACT.Square, accum_out=ss[:, t:t + 1])
                        if t % TPC < TPC - 1:
                            last.then_inc(g.junk_done, 1)
                            act.wait_ge(g.junk_done, (TPC - 1) * c + t % TPC + 1)
                    last.then_inc(ss_ready, 1)
                    act.wait_ge(ss_ready, c + 1)
                    if c == 0:
                        act.wait_ge(g.cols_ready, 1)
                        nc.scalar.activation(ew[:, 0:1], g.cols[:, DECAY:DECAY + 1], ACT.Exp).then_inc(edecay_ready, 1)
                        act.wait_ge(wclip_ready, 1)
                        nc.scalar.activation(ew[:, 2:3], ew[:, 1:2], ACT.Exp).then_inc(ew_ready, 1)
                if phase == 1:
                    high_part(nc, act, g, c)
                if phase == 2:
                    act.wait_ge(turned, c + 1)
                    nc.scalar.activation(shifted(hT, c)[0], tr_bank(c), ACT.Copy,
                                         scale=g.cols[:, LN1:LN1 + 1]).then_inc(hT_ready, 1)
                if phase == 3:
                    act.wait_ge(kvr_ready, c + 1)
                    if c >= 2:
                        act.wait_ge(y_ready, c - 1)
                    nc.scalar.activation(ex[:, c % 2, 0, :], k_ps, ACT.Exp).then_inc(ex_ready, 1)
                    nc.scalar.activation(ex[:, c % 2, 1, :], k_ps, ACT.Exp,
                                         bias=g.cols[:, FIRST:FIRST + 1]).then_inc(ex_ready, 1)
                    nc.scalar.activation(ex[:, c % 2, 2, :], r_ps, ACT.Tanh, scale=0.5).then_inc(ex_ready, 1)

        @block.vector
        def _(dve):
            link = chain(dve, dve_step)
            for buf in (hT, aS, bS):
                nc.vector.memset(buf[:, :, 0:1], 0.0).then_inc(zeros_ready, 1)
            dve.wait_ge(zeros_ready, 3)
            dve.wait_ge(cols_turned, 1)
            nc.vector.tensor_copy(g.cols[:, :], pb[:, 7, 0:NCOLS]).then_inc(g.cols_ready, 1)
            dve.wait_ge(edecay_ready, 1)
            link(nc.vector.tensor_scalar(ew[:, 3:4], ew[:, 0:1], -1.0, -CLIP, ALU.mult, ALU.max))
            nc.vector.tensor_scalar(ew[:, 1:2], ew[:, 3:4], CLIP, None, ALU.min).then_inc(wclip_ready, 1)
            for c, phase in plan:
                h, sh = shifted(hT, c)
                if phase == 0:
                    t = slice(c * TPC, (c + 1) * TPC)
                    dve.wait_ge(ss_ready, c + 1)
                    nc.vector.tensor_scalar(ms[:, t], ss[:, t], 1.0 / C, RMS_EPS, ALU.mult, ALU.add).then_inc(ms_ready, 1)
                if phase == 1:
                    dve.wait_ge(rstd_ready, c + 1)
                    if c >= 2:
                        dve.wait_ge(turned, c - 1)
                    for i in range(TPC):
                        t = c * TPC + i
                        last = nc.vector.tensor_scalar(hx[:, c % 2, i, :], g.x0[:, t, :], rstd[:, t:t + 1], None, ALU.mult)
                    last.then_inc(hx_ready, 1)
                if phase == 2:
                    dve.wait_ge(hT_ready, c + 1)
                    if c >= 2:
                        dve.wait_ge(kvr_ready, c - 1)
                    link(nc.vector.tensor_tensor(diff[:, :], h, sh, ALU.subtract))
                    for i, m in enumerate((MIXK, MIXV, MIXR)):
                        last = nc.vector.scalar_tensor_tensor(out=xm[:, c % 2, i, :], in0=diff[:, :], scalar=g.cols[:, m:m + 1],
                                                              in1=sh, op0=ALU.mult, op1=ALU.add)
                    last.then_inc(xm_ready, 1)
                    dve.wait_ge(xm_ready, c + 1)
                if phase == 3:
                    b = c // CPB
                    ek, ekt, th = (ex[:, c % 2, i, :] for i in range(3))
                    a_now, a_before = shifted(aS, c)
                    b_now, b_before = shifted(bS, c)
                    dve.wait_ge(ex_ready, 3 * (c + 1))
                    if c == 0:
                        dve.wait_ge(ew_ready, 1)
                    link(nc.vector.tensor_scalar(ex[:, c % 2, 0:2, :], ex[:, c % 2, 0:2, :], math.exp(-CLIP), math.exp(CLIP),
                                                 ALU.max, ALU.min))
                    nc.vector.tensor_tensor(ektv[:, :], ekt, v_ps, ALU.mult)
                    nc.vector.tensor_tensor(ekv[:, :], ek, v_ps, ALU.mult).then_inc(v_used, 1)
                    dve.wait_ge(v_used, c + 1)
                    link(nc.vector.tensor_tensor_scan(a_now, ew[:, 2:3].broadcast_to([P, CH]), ekv[:, :],
                                                      a_before[:, 0:1], ALU.mult, ALU.add))
                    link(nc.vector.tensor_tensor_scan(b_now, ew[:, 2:3].broadcast_to([P, CH]), ek,
                                                      b_before[:, 0:1], ALU.mult, ALU.add))
                    link(nc.vector.scalar_tensor_tensor(out=den[:, :], in0=b_before, scalar=WKV_EPS, in1=ekt,
                                                        op0=ALU.add, op1=ALU.add))
                    link(nc.vector.tensor_tensor(ektv[:, :], ektv[:, :], a_before, ALU.add))
                    link(nc.vector.reciprocal(rden[:, :], den[:, :]))
                    link(nc.vector.tensor_tensor(ektv[:, :], ektv[:, :], rden[:, :], ALU.mult))
                    if c >= 2:
                        dve.wait_ge(out_ready, c - 1)
                    nc.vector.scalar_tensor_tensor(out=yT[:, c % 2, :], in0=th, scalar=1.0, in1=ektv[:, :],
                                                   op0=ALU.add, op1=ALU.mult).then_inc(y_ready, 1)
                    dve.wait_ge(y_ready, c + 1)
                if phase == 4:
                    dve.wait_ge(out_ready, c + 1)
                    nc.vector.scalar_tensor_tensor(
                        out=g.x1[:, c * TPC:(c + 1) * TPC, :].rearrange("p t c -> p (t c)"), in0=out_bank(c), scalar=0.5,
                        in1=g.x0[:, c * TPC:(c + 1) * TPC, :].rearrange("p t c -> p (t c)"),
                        op0=ALU.mult, op1=ALU.add).then_inc(x1_ready, 1)

        @block.tensor
        def _(pe):
            pe.wait_ge(ident_ready, 2)
            pe.wait_ge(rows_in, 16 * 10)
            nc.tensor.transpose(pb[:, 7, 0:NCOLS], rows[0:NCOLS, :], g.ident[0:NCOLS, 0:NCOLS]).then_inc(cols_turned, 1)
            for c, phase in plan:
                if phase == 1:
                    pe.wait_ge(hx_ready, c + 1)
                    if c >= 2:
                        pe.wait_ge(hT_ready, c - 1)
                    for i in range(TPC):
                        last = nc.tensor.transpose(tr_bank(c)[:, i * P:(i + 1) * P], hx[:, c % 2, i, :], g.ident[:, :])
                    last.then_inc(turned, 1)
                if phase == 2:
                    if c == 0:
                        pe.wait_ge(w_in, 48)
                    pe.wait_ge(xm_ready, c + 1)
                    if c >= 1:
                        pe.wait_ge(ex_ready, 3 * c)
                        pe.wait_ge(v_used, c)
                    for i, (w, ps) in enumerate(((w_k, k_ps), (w_v, v_ps), (w_r, r_ps))):
                        last = nc.tensor.matmul(ps, w[:, :], xm[:, c % 2, i, :], start=True, stop=True)
                    last.then_inc(kvr_ready, 1)
                if phase == 3:
                    if c == 0:
                        pe.wait_ge(wo_in, 16)
                    pe.wait_ge(y_ready, c + 1)
                    if c >= 2:
                        pe.wait_ge(x1_ready, c - 1)
                    for i in range(TPC):
                        last = nc.tensor.matmul(out_bank(c)[:, i * P:(i + 1) * P], yT[:, c % 2, i * P:(i + 1) * P], w_o[:, :],
                                                start=True, stop=True)
                    last.then_inc(out_ready, 1)


def channel_mix(nc, g, a):
    with ExitStack() as ctx:
        def sb(name, shape, dt=F32):
            return ctx.enter_context(nc.sbuf_tensor(name, shape, dt))

        def sem(name):
            return ctx.enter_context(nc.semaphore(name))

        w_k = sb("w_k2", [P, H])
        w_v = sb("w_v2", [P, HC, P])
        w_r = sb("w_r2", [P, P])
        junk = sb("junk2", [P, P])
        ss = sb("ss2", [P, NT])
        ms = sb("ms2", [P, NT])
        rstd = sb("rstd2", [P, NT])
        hx = sb("hx2", [P, 2, TPC, P])
        hT = sb("hT2", [P, B, 1 + T])
        diff = sb("diff2", [P, CH])
        xm = sb("xm2", [P, 2, 2, CH])
        relu = sb("relu2", [P, 2, CH])
        sq = sb("sq2", [P, 2, HC, CH])
        th = sb("th2", [P, 2, CH])
        z = sb("z2", [P, 2, CH])
        stats = sb("stats2", [P, TPC, 6])
        mv = sb("mv2", [P, 2, TPC, 2])
        vare = sb("vare2", [P, 2, TPC])
        rs = sb("rs2", [P, 2, TPC])
        pb = g.pb
        tr_bank = lambda c: pb[:, c % 2, :]
        key_bank = lambda n: pb[:, 2 + n % 2, :]
        r_ps = pb[:, 4, :]
        val_bank = lambda c: pb[:, 5 + c % 2, :]

        w_in = sem("cm_w_in")
        ss_ready = sem("cm_ss_ready")
        zero_ready = sem("cm_zero_ready")
        ms_ready = sem("cm_ms_ready")
        rstd_ready = sem("cm_rstd_ready")
        hx_ready = sem("cm_hx_ready")
        turned = sem("cm_turned")
        hT_ready = sem("cm_hT_ready")
        xm_ready = sem("cm_xm_ready")
        key_ready = sem("cm_key_ready")
        relu_ready = sem("cm_relu_ready")
        sq_ready = sem("cm_sq_ready")
        r_ready = sem("cm_r_ready")
        th_ready = sem("cm_th_ready")
        val_ready = sem("cm_val_ready")
        val_used = sem("cm_val_used")
        vare_ready = sem("cm_vare_ready")
        rs_ready = sem("cm_rs_ready")
        junk_done = sem("cm_junk_done")
        normed = sem("cm_normed")
        dve_step = sem("cm_dve_step")

        block = ctx.enter_context(nc.Block())
        plan = schedule(NC, 6)

        @block.sync
        def _(sp):
            sp.dma_start(w_k[:, :], a.W_key2).then_inc(w_in, 16)
            sp.dma_start(w_v[:, :, :], a.W_value2.rearrange("(k p) c -> p k c", p=P)).then_inc(w_in, 16)
            sp.dma_start(w_r[:, :], a.W_recept2).then_inc(w_in, 16)

        @block.gpsimd
        def _(pool):
            for c, phase in plan:
                if phase == 0:
                    t = slice(c * TPC, (c + 1) * TPC)
                    pool.wait_ge(ms_ready, c + 1)
                    nc.gpsimd.tensor_tensor(rstd[:, t], ms[:, t], g.minus_half[:, 0:TPC], ALU.pow).then_inc(rstd_ready, 1)
                    scale_raw(nc, pool, g, NC + c)
                if phase == 4:
                    pool.wait_ge(vare_ready, c + 1)
                    nc.gpsimd.tensor_tensor(rs[:, c % 2, :], vare[:, c % 2, :], g.minus_half[:, 0:TPC], ALU.pow).then_inc(rs_ready, 1)
            scale_raw(nc, pool, g, E)

        @block.scalar
        def _(act):
            for c, phase in plan:
                if phase == 0:
                    for i in range(TPC):
                        t = c * TPC + i
                        nc.scalar.activation(junk[:, :], g.x1[:, t, :], ACT.Square, accum_out=ss[:, t:t + 1]).then_inc(ss_ready, 1)
                        act.wait_ge(ss_ready, t + 1)
                if phase == 1:
                    high_part(nc, act, g, NC + c)
                if phase == 2:
                    act.wait_ge(turned, c + 1)
                    nc.scalar.activation(shifted(hT, c)[0], tr_bank(c), ACT.Copy,
                                         scale=g.cols[:, LN2:LN2 + 1]).then_inc(hT_ready, 1)
                if phase == 3:
                    for k in range(HC):
                        n = c * HC + k
                        act.wait_ge(key_ready, n + 1)
                        if n >= 2:
                            act.wait_ge(sq_ready, n - 1)
                        nc.scalar.activation(relu[:, n % 2, :], key_bank(n), ACT.Relu).then_inc(relu_ready, 1)
                    act.wait_ge(r_ready, c + 1)
                    if c >= 2:
                        act.wait_ge(val_used, c - 1)
                    nc.scalar.activation(th[:, c % 2, :], r_ps, ACT.Tanh, scale=0.5).then_inc(th_ready, 1)

        @block.vector
        def _(dve):
            link = chain(dve, dve_step)
            nc.vector.memset(hT[:, :, 0:1], 0.0).then_inc(zero_ready, 1)
            dve.wait_ge(zero_ready, 1)
            for c, phase in plan:
                h, sh = shifted(hT, c)
                rows = slice(c * TPC, (c + 1) * TPC)
                if phase == 0:
                    dve.wait_ge(ss_ready, TPC * (c + 1))
                    nc.vector.tensor_scalar(ms[:, rows], ss[:, rows], 1.0 / C, RMS_EPS, ALU.mult, ALU.add).then_inc(ms_ready, 1)
                if phase == 1:
                    dve.wait_ge(rstd_ready, c + 1)
                    if c >= 2:
                        dve.wait_ge(turned, c - 1)
                    for i in range(TPC):
                        t = c * TPC + i
                        last = nc.vector.tensor_scalar(hx[:, c % 2, i, :], g.x1[:, t, :], rstd[:, t:t + 1], None, ALU.mult)
                    last.then_inc(hx_ready, 1)
                if phase == 2:
                    dve.wait_ge(hT_ready, c + 1)
                    if c >= 2:
                        dve.wait_ge(r_ready, c - 1)
                    link(nc.vector.tensor_tensor(diff[:, :], h, sh, ALU.subtract))
                    for i, m in enumerate((MIXK2, MIXR2)):
                        last = nc.vector.scalar_tensor_tensor(out=xm[:, c % 2, i, :], in0=diff[:, :], scalar=g.cols[:, m:m + 1],
                                                              in1=sh, op0=ALU.mult, op1=ALU.add)
                    last.then_inc(xm_ready, 1)
                    dve.wait_ge(xm_ready, c + 1)
                if phase == 3:
                    if c >= 2:
                        dve.wait_ge(val_ready, c - 1)
                    for k in range(HC):
                        n = c * HC + k
                        dve.wait_ge(relu_ready, n + 1)
                        nc.vector.tensor_tensor(sq[:, c % 2, k, :], relu[:, n % 2, :], relu[:, n % 2, :], ALU.mult).then_inc(sq_ready, 1)
                if phase == 4:
                    zc = z[:, c % 2, :]
                    dve.wait_ge(th_ready, c + 1)
                    dve.wait_ge(val_ready, c + 1)
                    nc.vector.scalar_tensor_tensor(out=zc, in0=th[:, c % 2, :], scalar=1.0, in1=val_bank(c),
                                                   op0=ALU.add, op1=ALU.mult).then_inc(val_used, 1)
                    dve.wait_ge(val_used, c + 1)
                    link(nc.vector.scalar_tensor_tensor(out=zc, in0=zc, scalar=0.5, in1=g.x1[:, rows, :].rearrange("p t c -> p (t c)"),
                                                        op0=ALU.mult, op1=ALU.add))
                    link(nc.vector.tensor_tensor(zc, zc, g.x0[:, rows, :].rearrange("p t c -> p (t c)"), ALU.add))
                    for i in range(TPC):
                        last = nc.vector.bn_stats(stats[:, i, :], zc[:, i * C:(i + 1) * C])
                    link(last)
                    for i in range(TPC):
                        last = nc.vector.bn_aggr(mv[:, c % 2, i, :], stats[:, i, :])
                    link(last)
                    if c >= 2:
                        dve.wait_ge(rs_ready, c - 1)
                    nc.vector.tensor_scalar(vare[:, c % 2, :], mv[:, c % 2, :, 1], LN_EPS, None, ALU.add).then_inc(vare_ready, 1)
                if phase == 5:
                    dve.wait_ge(rs_ready, c + 1)
                    for i in range(TPC):
                        last = nc.vector.tensor_scalar(g.x0[:, c * TPC + i, :], z[:, c % 2, i * C:(i + 1) * C],
                                                       mv[:, c % 2, i, 0:1], rs[:, c % 2, i:i + 1], ALU.subtract, ALU.mult)
                    last.then_inc(normed, 1)
                    dve.wait_ge(normed, c + 1)

        @block.tensor
        def _(pe):
            for c, phase in plan:
                if phase == 1:
                    pe.wait_ge(hx_ready, c + 1)
                    if c >= 2:
                        pe.wait_ge(hT_ready, c - 1)
                    for i in range(TPC):
                        last = nc.tensor.transpose(tr_bank(c)[:, i * P:(i + 1) * P], hx[:, c % 2, i, :], g.ident[:, :])
                    last.then_inc(turned, 1)
                if phase == 2:
                    if c == 0:
                        pe.wait_ge(w_in, 48)
                    pe.wait_ge(xm_ready, c + 1)
                    for k in range(HC):
                        n = c * HC + k
                        if n >= 2:
                            pe.wait_ge(relu_ready, n - 1)
                        nc.tensor.matmul(key_bank(n), w_k[:, k * P:(k + 1) * P], xm[:, c % 2, 0, :],
                                         start=True, stop=True).then_inc(key_ready, 1)
                    if c >= 1:
                        pe.wait_ge(th_ready, c)
                    for i in range(TPC):
                        last = nc.tensor.matmul(r_ps[:, i * P:(i + 1) * P], xm[:, c % 2, 1, i * P:(i + 1) * P], w_r[:, :],
                                                start=True, stop=True)
                    last.then_inc(r_ready, 1)
                if phase == 3:
                    if c >= 2:
                        pe.wait_ge(val_used, c - 1)
                    pe.wait_ge(sq_ready, HC * (c + 1))
                    for i in range(TPC):
                        for k in range(HC):
                            last = nc.tensor.matmul(val_bank(c)[:, i * P:(i + 1) * P], sq[:, c % 2, k, i * P:(i + 1) * P],
                                                    w_v[:, k, :], start=(k == 0), stop=(k == HC - 1))
                    last.then_inc(val_ready, 1)


def route(nc, g, a):
    with ExitStack() as ctx:
        def sb(name, shape, dt=F32):
            return ctx.enter_context(nc.sbuf_tensor(name, shape, dt))

        def sem(name):
            return ctx.enter_context(nc.semaphore(name))

        xT = sb("xT", [P, N])
        w_g = sb("w_g", [P, E])
        b2 = sb("b2", [E, C])
        logit = sb("logit", [P, NT, E])
        rest = sb("rest", [P, NT, E])
        rank = sb("rank", [P, NT, E])
        tied = sb("tied", [P, NT, E])
        top = sb("top", [P, TOPK, NT])
        topr = sb("topr", [P, NT])
        onehot = sb("onehot", [P, E, TOPK, NT])
        keep = sb("keep", [P, E, TOPK, NT])
        upper = sb("upper", [P, P])
        ones = sb("ones", [P, P])
        resets = sb("resets", [P, E, TOPK * NT])
        upto = sb("upto", [P, E, TOPK, NT])
        gap = sb("gap", [P, NT])
        egap = sb("egap", [P, NT])
        esum = sb("esum", [P, NT])
        wk = sb("wk", [P, TOPK, NT])
        gT = sb("gT", [E, N])
        pb = g.pb
        tr_bank = lambda c: pb[:, c % 2, :]
        logit_ps = pb[:, 2, 0:NT * E].rearrange("p (t e) -> p t e", e=E)
        within_ps = pb[:, 3, 0:E * TOPK * NT]
        total_ps = pb[:, 3, 256:256 + E * TOPK * NT]
        bias_bank = lambda c: pb[:, 4 + c % 2, :]

        w_in = sem("ro_w_in")
        turned = sem("ro_turned")
        xT_ready = sem("ro_xT_ready")
        xh_ready = sem("ro_xh_ready")
        logit_ready = sem("ro_logit_ready")
        consts_ready = sem("ro_consts_ready")
        onehot_ready = sem("ro_onehot_ready")
        counts_ready = sem("ro_counts_ready")
        gap_ready = sem("ro_gap_ready")
        egap_ready = sem("ro_egap_ready")
        gate_ready = sem("ro_gate_ready")
        gate_turned = sem("ro_gate_turned")
        gT_ready = sem("ro_gT_ready")
        bias_ready = sem("ro_bias_ready")
        bias_used = sem("ro_bias_used")
        xl_ready = sem("ro_xl_ready")
        dve_step = sem("ro_dve_step")

        block = ctx.enter_context(nc.Block())

        @block.sync
        def _(sp):
            sp.dma_start(w_g[:, :], a.wg).then_inc(w_in, 16)
            sp.dma_start(b2[:, :], a.b2).then_inc(w_in, 16)

        @block.gpsimd
        def _(pool):
            nc.gpsimd.memset(upper[:, :], 1.0).then_inc(consts_ready, 1)
            nc.gpsimd.memset(ones[:, :], 1.0).then_inc(consts_ready, 1)
            nc.gpsimd.memset(resets[:, :, :], 1.0).then_inc(consts_ready, 1)
            nc.gpsimd.iota(rank[:, :, :], pattern=[[0, NT], [-1, E]], base=E, channel_multiplier=0,
                           allow_small_or_imprecise_dtypes=True).then_inc(consts_ready, 1)
            pool.wait_ge(consts_ready, 4)
            nc.gpsimd.affine_select(out=upper[:, :], in_=upper[:, :], compare_op=ALU.is_ge, fill=0.0,
                                    base=0, pattern=[[1, P]], channel_multiplier=-1).then_inc(consts_ready, 1)
            nc.gpsimd.memset(resets[:, :, 0:1], 0.0).then_inc(consts_ready, 1)

        @block.scalar
        def _(act):
            for c in range(NC):
                cols = slice(c * CH, (c + 1) * CH)
                act.wait_ge(turned, c + 1)
                nc.scalar.activation(xT[:, cols], tr_bank(c), ACT.Copy).then_inc(xT_ready, 1)
                nc.scalar.activation(g.xh[:, cols], tr_bank(c), ACT.Copy).then_inc(xh_ready, 1)
            act.wait_ge(gap_ready, 1)
            nc.scalar.activation(egap[:, :], gap[:, :], ACT.Exp).then_inc(egap_ready, 1)
            for c in range(NC):
                act.wait_ge(gate_turned, c + 1)
                nc.scalar.activation(gT[:, c * CH:(c + 1) * CH], tr_bank(c)[0:E, :], ACT.Copy).then_inc(gT_ready, 1)

        @block.vector
        def _(dve):
            link = chain(dve, dve_step)
            dve.wait_ge(consts_ready, 6)
            dve.wait_ge(logit_ready, 1)
            link(nc.vector.tensor_copy(logit[:, :, :], logit_ps))
            src = logit
            for k in range(TOPK):
                oh = onehot[:, :, k, :].rearrange("p e t -> p t e")
                link(nc.vector.tensor_reduce(top[:, k, :], src[:, :, :], AX.X, ALU.max))
                link(nc.vector.tensor_tensor(tied[:, :, :], src[:, :, :], top[:, k, :].rearrange("p (t o) -> p t o", o=1)
                                             .broadcast_to([P, NT, E]), ALU.is_equal))
                link(nc.vector.tensor_tensor(tied[:, :, :], tied[:, :, :], rank[:, :, :], ALU.mult))
                link(nc.vector.tensor_reduce(topr[:, :], tied[:, :, :], AX.X, ALU.max))
                link(nc.vector.tensor_tensor(oh, tied[:, :, :], topr[:, :].rearrange("p (t o) -> p t o", o=1)
                                             .broadcast_to([P, NT, E]), ALU.is_equal))
                if k == 0:
                    link(nc.vector.scalar_tensor_tensor(out=rest[:, :, :], in0=oh, scalar=-3e38, in1=logit[:, :, :],
                                                        op0=ALU.mult, op1=ALU.add))
                    src = rest
            nc.vector.tensor_tensor(gap[:, :], top[:, 1, :], top[:, 0, :], ALU.subtract).then_inc(gap_ready, 1)
            dve.sem_inc(onehot_ready, 1)
            dve.wait_ge(counts_ready, 1)
            flat = lambda buf: buf[:, :, :, :].rearrange("p e k t -> p (e k t)")
            link(nc.vector.tensor_tensor_scan(flat(upto), resets[:, :, :].rearrange("p e n -> p (e n)"), total_ps, 0.0,
                                              ALU.mult, ALU.add))
            link(nc.vector.tensor_tensor(flat(upto), flat(upto), total_ps, ALU.subtract))
            link(nc.vector.tensor_tensor(flat(upto), flat(upto), within_ps, ALU.add))
            link(nc.vector.scalar_tensor_tensor(out=flat(keep), in0=flat(upto), scalar=float(CAP), in1=flat(onehot),
                                                op0=ALU.is_le, op1=ALU.mult))
            dve.wait_ge(egap_ready, 1)
            link(nc.vector.tensor_scalar(esum[:, :], egap[:, :], 1.0, None, ALU.add))
            link(nc.vector.reciprocal(wk[:, 0, :], esum[:, :]))
            link(nc.vector.tensor_tensor(wk[:, 1, :], egap[:, :], wk[:, 0, :], ALU.mult))
            for k in range(TOPK):
                last = nc.vector.tensor_tensor(keep[:, :, k, :], keep[:, :, k, :],
                                               wk[:, k, :].rearrange("p (o t) -> p o t", o=1).broadcast_to([P, E, NT]), ALU.mult)
            link(last)
            nc.vector.tensor_tensor(g.gate[:, :, :], keep[:, :, 0, :], keep[:, :, 1, :], ALU.add).then_inc(gate_ready, 1)
            dve.wait_ge(gate_ready, 1)
            link(nc.vector.tensor_scalar(g.gate_down[:, :, :], g.gate[:, :, :], 1.0 / W_SCALE, None, ALU.mult))
            for c in range(NC):
                cols = slice(c * CH, (c + 1) * CH)
                dve.wait_ge(xh_ready, c + 1)
                nc.vector.tensor_tensor(g.xl[:, cols], xT[:, cols], g.xh[:, cols], ALU.subtract).then_inc(xl_ready, 1)
            for c in range(NC):
                rows = slice(c * TPC, (c + 1) * TPC)
                dve.wait_ge(bias_ready, c + 1)
                nc.vector.tensor_tensor(g.moe[:, rows, :].rearrange("p t c -> p (t c)"), bias_bank(c),
                                        g.x0[:, rows, :].rearrange("p t c -> p (t c)"), ALU.add).then_inc(bias_used, 1)

        @block.tensor
        def _(pe):
            for c in range(NC):
                if c >= 2:
                    pe.wait_ge(xh_ready, c - 1)
                for i in range(TPC):
                    last = nc.tensor.transpose(tr_bank(c)[:, i * P:(i + 1) * P], g.x0[:, c * TPC + i, :], g.ident[:, :])
                last.then_inc(turned, 1)
            pe.wait_ge(w_in, 32)
            for t in range(NT):
                pe.wait_ge(xT_ready, t // TPC + 1)
                last = nc.tensor.matmul(logit_ps[:, t, :], xT[:, t * P:(t + 1) * P], w_g[:, :], start=True, stop=True)
            last.then_inc(logit_ready, 1)
            pe.wait_ge(consts_ready, 6)
            pe.wait_ge(onehot_ready, 1)
            oh = onehot[:, :, :, :].rearrange("p e k t -> p (e k t)")
            nc.tensor.matmul(within_ps, upper[:, :], oh, start=True, stop=True)
            nc.tensor.matmul(total_ps, ones[:, :], oh, start=True, stop=True).then_inc(counts_ready, 1)
            pe.wait_ge(gate_ready, 1)
            pe.wait_ge(xh_ready, NC)
            for c in range(NC):
                if c >= 2:
                    pe.wait_ge(gT_ready, c - 1)
                for i in range(TPC):
                    last = nc.tensor.transpose(tr_bank(c)[0:E, i * P:(i + 1) * P], g.gate[:, :, c * TPC + i], g.ident[:, :])
                last.then_inc(gate_turned, 1)
            for c in range(NC):
                pe.wait_ge(gT_ready, c + 1)
                if c >= 2:
                    pe.wait_ge(bias_used, c - 1)
                for i in range(TPC):
                    t = c * TPC + i
                    last = nc.tensor.matmul(bias_bank(c)[:, i * P:(i + 1) * P], gT[:, t * P:(t + 1) * P], b2[:, :],
                                            start=True, stop=True)
                last.then_inc(bias_ready, 1)


def experts(nc, g, a):
    with ExitStack() as ctx:
        def sb(name, shape, dt=F32):
            return ctx.enter_context(nc.sbuf_tensor(name, shape, dt))

        def sem(name):
            return ctx.enter_context(nc.semaphore(name))

        RING = 4
        h32 = sb("h32", [P, RING, CH])
        hh = sb("hh", [P, 2, HC, CH], F16)
        b1_now = sb("b1_now", [P, HC])
        hl = sb("hl", [P, 2, HC, CH], F16)
        pb = g.pb
        hid_bank = lambda n: pb[:, n % RING, :]
        out_bank = lambda c: pb[:, 4 + c % 2, :]
        hid_ready = sem("ex_hid_ready")
        h32_ready = sem("ex_h32_ready")
        b1_ready = sem("ex_b1_ready")
        hh_ready = sem("ex_hh_ready")
        hl_ready = sem("ex_hl_ready")
        out_ready = sem("ex_out_ready")
        out_used = sem("ex_out_used")

        block = ctx.enter_context(nc.Block())

        def chunks(step, e, final):
            for c in range(NC):
                if c < NC - 1:
                    step(0, e, c + 1)
                elif not final:
                    step(0, e + 1, 0)
                step(1, e, c)

        def every_expert(eng, step):
            step(0, 0, 0)
            with eng.Fori(0, E - 1) as e:
                chunks(step, e, False)
            chunks(step, E - 1, True)

        @block.tensor
        def _(pe):
            def step(layer, e, c):
                q = e * NC + c
                if layer == 0:
                    x = slice(c * CH, (c + 1) * CH)
                    for k in range(HC):
                        pe.wait_ge(hh_ready, q * HC + k + 1)
                        w = slice(k * P, (k + 1) * P)
                        for i, (lhs, rhs) in enumerate(((g.w0h, g.xh), (g.w0h, g.xl), (g.w0l, g.xh))):
                            last = nc.tensor.matmul(hid_bank(k), lhs[:, bass.ds(e, 1), w], rhs[:, x], start=(i == 0), stop=(i == 2))
                        last.then_inc(hid_ready, 1)
                else:
                    pe.wait_ge(hl_ready, q * HC + (RING + HC))
                    pe.wait_ge(out_used, q + 1)
                    for i in range(TPC):
                        tok = slice(i * P, (i + 1) * P)
                        for k in range(HC):
                            w2 = slice(H + k * P, H + (k + 1) * P)
                            for j, (lhs, rhs) in enumerate(((hh, g.w0h), (hh, g.w0l), (hl, g.w0h))):
                                last = nc.tensor.matmul(out_bank(c)[:, tok], lhs[:, c % 2, k, tok], rhs[:, bass.ds(e, 1), w2],
                                                        start=(k == 0 and j == 0), stop=(k == HC - 1 and j == 2))
                    last.then_inc(out_ready, 1)

            pe.sem_inc(out_ready, 2)
            every_expert(pe, step)

        @block.scalar
        def _(act):
            def step(layer, e, c):
                if layer == 0:
                    q = e * NC + c
                    act.wait_ge(b1_ready, e + 1)
                    act.wait_ge(out_ready, q + 1)
                    for k in range(HC):
                        n = q * HC + k
                        b1 = b1_now[:, k:k + 1]
                        act.wait_ge(hid_ready, n + 1)
                        act.wait_ge(hl_ready, n + 1)
                        nc.scalar.activation(h32[:, k, :], hid_bank(k), ACT.Relu, scale=1.0 / W_SCALE, bias=b1).then_inc(h32_ready, 1)
                        nc.scalar.activation(hh[:, c % 2, k, :], hid_bank(k), ACT.Relu, scale=1.0 / W_SCALE,
                                             bias=b1).then_inc(hh_ready, 1)

            act.sem_inc(hh_ready, RING)
            every_expert(act, step)

        @block.vector
        def _(dve):
            def step(layer, e, c):
                q = e * NC + c
                if layer == 0:
                    if c == 0:
                        dve.wait_ge(hh_ready, q * HC + RING)
                        nc.vector.tensor_scalar(b1_now[:, :], g.cols[:, bass.ds(e * HC + B1, HC)], 1.0, None, ALU.mult).then_inc(b1_ready, 1)
                    for k in range(HC):
                        dve.wait_ge(hh_ready, q * HC + (k + 1 + RING))
                        nc.vector.tensor_tensor(hl[:, c % 2, k, :], h32[:, k, :], hh[:, c % 2, k, :], ALU.subtract).then_inc(hl_ready, 1)
                else:
                    dve.wait_ge(out_ready, q + 3)
                    for i in range(TPC):
                        t = c * TPC + i
                        last = nc.vector.scalar_tensor_tensor(
                            out=g.moe[:, t, :], in0=out_bank(c)[:, i * C:(i + 1) * C], scalar=g.gate_down_flat[:, bass.ds(e * NT + t, 1)],
                            in1=g.moe[:, t, :], op0=ALU.mult, op1=ALU.add)
                    last.then_inc(out_used, 1)

            dve.sem_inc(hl_ready, RING)
            dve.sem_inc(out_used, 2)
            every_expert(dve, step)


def project(nc, g, a):
    with ExitStack() as ctx:
        def sb(name, shape, dt=F32):
            return ctx.enter_context(nc.sbuf_tensor(name, shape, dt))

        def sem(name):
            return ctx.enter_context(nc.semaphore(name))

        NB = 2 * C + HASH
        w_raw = sb("pj_w_raw", [P, 2, C])
        w_T = sb("pj_w_T", [P, 2 * C])
        brow = sb("pj_brow", [1, NB])
        one_row = sb("pj_one_row", [1, P])
        ones = sb("pj_ones", [P, P])
        bcast = sb("pj_bcast", [P, NB])
        stats = sb("pj_stats", [P, TPC, 6])
        mv = sb("pj_mv", [P, 2, TPC, 2])
        vare = sb("pj_vare", [P, 2, TPC])
        rs = sb("pj_rs", [P, 2, TPC])
        xT = sb("pj_xT", [P, 2, CH])
        prod = sb("pj_prod", [P, NG, GT, HPG, DH])
        half = sb("pj_half", [P, NG * HPG])
        nsq = sb("pj_nsq", [P, NG, GT, HPG])
        qa = sb("pj_qa", [P, NG, GT, HPG])
        tmp = sb("pj_tmp", [P, NG, GT, HPG])
        nsq2 = sb("pj_nsq2", [P, NG, GT, HPG])
        pk = sb("pj_pk", [P, NG, GT, HPG])
        hq = sb("pj_hq", [P, NG, GT, HPG])
        hk = sb("pj_hk", [P, NG, GT, HPG])
        mx = sb("pj_mx", [P, NG, HPG])
        mxall = sb("pj_mxall", [P, NG, HPG])
        sc = sb("pj_sc", [P, 3, NG, HPG])
        longest = sb("pj_longest", [P, 1])
        n1 = sb("pj_n1", [P, NG, HPG])
        none = sb("pj_none", [P, 3, NG, HPG])
        pb = g.pb
        tr_bank = lambda c: pb[:, c % 2, :]
        qkv_ps = lambda c: pb[:, 2 + 2 * (c % 2):4 + 2 * (c % 2), :].rearrange("p a n -> p (a n)").rearrange("p (t m) -> p t m", m=2 * C)

        w_in = sem("pj_w_in")
        brow_in = sem("pj_brow_in")
        ones_ready = sem("pj_ones_ready")
        w_turned = sem("pj_w_turned")
        bcast_done = sem("pj_bcast_done")
        consts_ready = sem("pj_consts_ready")
        vare_ready = sem("pj_vare_ready")
        rs_ready = sem("pj_rs_ready")
        x_ready = sem("pj_x_ready")
        turned = sem("pj_turned")
        xT_ready = sem("pj_xT_ready")
        qkv_ready = sem("pj_qkv_ready")
        qkv_used = sem("pj_qkv_used")
        mx_ready = sem("pj_mx_ready")
        mxall_ready = sem("pj_mxall_ready")
        s2_ready = sem("pj_s2_ready")
        s_ready = sem("pj_s_ready")
        hk_ready = sem("pj_hk_ready")
        counts_ready = sem("pj_counts_ready")
        dve_step = sem("pj_dve_step")

        block = ctx.enter_context(nc.Block())
        plan = schedule(NC, 4)

        @block.sync
        def _(sp):
            sp.dma_start(w_raw[:, 0, :], a.qk_w).then_inc(w_in, 16)
            sp.dma_start(w_raw[:, 1, :], a.v_w).then_inc(w_in, 16)
            for lo, v in ((0, a.qk_b), (C, a.v_b), (2 * C, a.hash_a)):
                sp.dma_start(brow[:, lo:lo + v.shape[0]], v.rearrange("(a n) -> a n", a=1)).then_inc(brow_in, 16)

        @block.gpsimd
        def _(pool):
            nc.gpsimd.memset(one_row[:, :], 1.0).then_inc(ones_ready, 1)
            nc.gpsimd.memset(ones[:, :], 1.0).then_inc(ones_ready, 1)
            nc.gpsimd.memset(half[:, :], 0.5).then_inc(ones_ready, 1)
            pool.wait_ge(ones_ready, 3)
            for c, phase in plan:
                if phase == 0:
                    pool.wait_ge(vare_ready, c + 1)
                    nc.gpsimd.tensor_tensor(rs[:, c % 2, :], vare[:, c % 2, :], g.minus_half[:, 0:TPC], ALU.pow).then_inc(rs_ready, 1)
            heads = lambda buf: buf.rearrange("p g h -> p (g h)")
            pool.wait_ge(mx_ready, 1)
            nc.gpsimd.partition_all_reduce(heads(mxall[:, :, :]), heads(mx[:, :, :]), P,
                                           bass.bass_isa.ReduceOp.max).then_inc(mxall_ready, 1)
            pool.wait_ge(s2_ready, 1)
            nc.gpsimd.tensor_tensor(heads(sc[:, 0, :, :]), heads(sc[:, 1, :, :]), half[:, :], ALU.pow).then_inc(s_ready, 1)

        @block.scalar
        def _(act):
            for c, phase in plan:
                if phase == 2:
                    act.wait_ge(turned, c + 1)
                    if c >= 2:
                        act.wait_ge(qkv_ready, c - 1)
                    nc.scalar.activation(xT[:, c % 2, :], tr_bank(c), ACT.Copy).then_inc(xT_ready, 1)

        @block.vector
        def _(dve):
            link = chain(dve, dve_step)
            for c, phase in plan:
                rows = slice(c * TPC, (c + 1) * TPC)
                if phase == 0:
                    for i in range(TPC):
                        last = nc.vector.bn_stats(stats[:, i, :], g.moe[:, c * TPC + i, :])
                    link(last)
                    for i in range(TPC):
                        last = nc.vector.bn_aggr(mv[:, c % 2, i, :], stats[:, i, :])
                    link(last)
                    nc.vector.tensor_scalar(vare[:, c % 2, :], mv[:, c % 2, :, 1], LN_EPS, None, ALU.add).then_inc(vare_ready, 1)
                if phase == 1:
                    dve.wait_ge(rs_ready, c + 1)
                    for i in range(TPC):
                        t = c * TPC + i
                        last = nc.vector.tensor_scalar(g.x0[:, t, :], g.moe[:, t, :], mv[:, c % 2, i, 0:1], rs[:, c % 2, i:i + 1],
                                                       ALU.subtract, ALU.mult)
                    last.then_inc(x_ready, 1)
                    dve.wait_ge(x_ready, c + 1)
                    if c == 0:
                        dve.wait_ge(w_turned, 1)
                        nc.vector.tensor_copy(w_T[:, :], pb[:, 6, 0:2 * C]).then_inc(consts_ready, 1)
                        dve.wait_ge(bcast_done, 1)
                        nc.vector.tensor_copy(bcast[:, :], pb[:, 7, 0:NB]).then_inc(consts_ready, 1)
                        dve.wait_ge(consts_ready, 2)
                if phase == 3:
                    b, t0 = c // CPB, (c % CPB) * TPC
                    dve.wait_ge(qkv_ready, c + 1)
                    for i in range(TPC):
                        for j, dst in enumerate((g.q, g.v)):
                            last = nc.vector.tensor_tensor(
                                dst[:, b * HG:(b + 1) * HG, t0 + i, :, :].rearrange("p g h d -> p g (h d)"),
                                qkv_ps(c)[:, i, j * C:(j + 1) * C].rearrange("p (g n) -> p g n", g=HG),
                                bcast[:, j * C:(j + 1) * C].rearrange("p (g n) -> p g n", g=HG), ALU.add)
                    last.then_inc(qkv_used, 1)
            dve.wait_ge(qkv_used, NC)
            every = lambda buf: buf[:, :, :, :].rearrange("p g t h -> p (g t h)")
            rowsof = lambda buf: buf[:, :, :, :, :].rearrange("p g t h d -> p (g t h) d")
            per_head = lambda buf: buf.rearrange("p g (o h) -> p g o h", o=1).broadcast_to([P, NG, GT, HPG])
            link(nc.vector.tensor_tensor(rowsof(prod), rowsof(g.q), rowsof(g.q), ALU.mult))
            link(nc.vector.tensor_reduce(every(nsq), rowsof(prod), AX.X, ALU.add))
            nc.vector.tensor_reduce(mx[:, :, :], nsq[:, :, :, :].rearrange("p g t h -> p g h t"), AX.X, ALU.max).then_inc(mx_ready, 1)
            link(nc.vector.tensor_tensor(rowsof(prod), rowsof(g.q), bcast[:, 2 * C:2 * C + DH].rearrange("p (o d) -> p o d", o=1)
                                         .broadcast_to([P, NG * GT * HPG, DH]), ALU.mult))
            link(nc.vector.tensor_reduce(every(qa), rowsof(prod), AX.X, ALU.add))
            dve.wait_ge(mxall_ready, 1)
            link(nc.vector.tensor_scalar(sc[:, 0, :, :], mxall[:, :, :], 1e-24, None, ALU.max))
            link(nc.vector.reciprocal(sc[:, 2, :, :], sc[:, 0, :, :]))
            nc.vector.tensor_scalar(sc[:, 1, :, :], sc[:, 2, :, :], U_HASH ** 2, None, ALU.mult).then_inc(s2_ready, 1)
            link(nc.vector.tensor_reduce(longest[:, :], mxall[:, :, :].rearrange("p g h -> p (g h)"), AX.X, ALU.max))
            link(nc.vector.tensor_scalar(g.large[:, :], longest[:, :], SAFE_SCORE * DH ** 0.5, None, ALU.is_gt))
            link(nc.vector.tensor_scalar(every(hq), every(qa), 0.0, None, ALU.is_ge))
            link(nc.vector.tensor_scalar(every(g.qbit), every(hq), 2.0, -1.0, ALU.mult, ALU.add))
            dve.wait_ge(s2_ready, 1)
            link(nc.vector.tensor_tensor(nsq2[:, :, :, :], nsq[:, :, :, :], per_head(sc[:, 1, :, :]), ALU.mult))
            link(nc.vector.tensor_tensor(every(tmp), every(nsq2), every(nsq2), ALU.mult))
            for i, part in enumerate((nsq2, tmp)):
                link(nc.vector.tensor_scalar(every(part), every(part), -1.0, 0.5, ALU.mult, ALU.add))
                link(nc.vector.tensor_scalar(every(part), every(part), bcast[:, 2 * C + DH + i:2 * C + DH + i + 1], None, ALU.mult))
            link(nc.vector.tensor_tensor(every(tmp), every(tmp), every(nsq2), ALU.add))
            dve.wait_ge(s_ready, 1)
            link(nc.vector.tensor_tensor(pk[:, :, :, :], qa[:, :, :, :], per_head(sc[:, 0, :, :]), ALU.mult))
            link(nc.vector.tensor_tensor(every(pk), every(pk), every(tmp), ALU.add))
            nc.vector.tensor_scalar(every(hk), every(pk), 0.0, None, ALU.is_ge).then_inc(hk_ready, 1)
            dve.wait_ge(hk_ready, 1)
            link(nc.vector.tensor_scalar(every(g.kbit), every(hk), MASK, -MASK / 2, ALU.mult, ALU.add))
            dve.wait_ge(counts_ready, 1)
            link(nc.vector.tensor_reduce(n1[:, :, :], pb[:, 5, 0:NG * GT * HPG].rearrange("p (g t h) -> p g h t", g=NG, t=GT), AX.X, ALU.add))
            link(nc.vector.tensor_scalar(none[:, 0, :, :], n1[:, :, :], 0.0, MASK, ALU.is_equal, ALU.mult))
            link(nc.vector.tensor_scalar(none[:, 1, :, :], n1[:, :, :], float(T), MASK, ALU.is_equal, ALU.mult))
            link(nc.vector.tensor_tensor(none[:, 2, :, :], none[:, 0, :, :], none[:, 1, :, :], ALU.subtract))
            link(nc.vector.tensor_tensor(tmp[:, :, :, :], hq[:, :, :, :], per_head(none[:, 2, :, :]), ALU.mult))
            link(nc.vector.tensor_tensor(g.lift[:, :, :, :], tmp[:, :, :, :], per_head(none[:, 1, :, :]), ALU.add))

        @block.tensor
        def _(pe):
            pe.wait_ge(w_in, 32)
            nc.tensor.transpose(pb[:, 6, 0:C], w_raw[:, 0, :], g.ident[:, :])
            nc.tensor.transpose(pb[:, 6, C:2 * C], w_raw[:, 1, :], g.ident[:, :]).then_inc(w_turned, 1)
            pe.wait_ge(ones_ready, 3)
            pe.wait_ge(brow_in, 48)
            nc.tensor.matmul(pb[:, 7, 0:NB], one_row[:, :], brow[:, :], start=True, stop=True).then_inc(bcast_done, 1)
            for c, phase in plan:
                if phase == 1:
                    pe.wait_ge(x_ready, c + 1)
                    if c >= 2:
                        pe.wait_ge(xT_ready, c - 1)
                    for i in range(TPC):
                        last = nc.tensor.transpose(tr_bank(c)[:, i * P:(i + 1) * P], g.x0[:, c * TPC + i, :], g.ident[:, :])
                    last.then_inc(turned, 1)
                if phase == 2:
                    pe.wait_ge(consts_ready, 2)
                    pe.wait_ge(xT_ready, c + 1)
                    if c >= 2:
                        pe.wait_ge(qkv_used, c - 1)
                    for i in range(TPC):
                        last = nc.tensor.matmul(qkv_ps(c)[:, i, :], xT[:, c % 2, i * P:(i + 1) * P], w_T[:, :], start=True, stop=True)
                    last.then_inc(qkv_ready, 1)
            pe.wait_ge(hk_ready, 1)
            nc.tensor.matmul(pb[:, 5, 0:NG * GT * HPG], ones[:, :], hk[:, :, :, :].rearrange("p g t h -> p (g t h)"),
                             start=True, stop=True).then_inc(counts_ready, 1)


def one_group(buf, G):
    if len(buf.shape) == 5:
        return buf[:, bass.ds(G, 1), :, :, :].rearrange("p o t h d -> p (o t h) d")
    return buf[:, bass.ds(G, 1), :, :].rearrange("p o t (h d) -> p (o t h) d", d=1)


def side_rows(buf, lo, n):
    return buf[:, :, :, lo:lo + n].rearrange("p t h d -> p (t h) d")


def clear_sides(nc, pool, qs, ks, done):
    nc.gpsimd.memset(qs[:, :, :, :], 0.0).then_inc(done, 1)
    nc.gpsimd.memset(ks[:, :, :, :], 0.0).then_inc(done, 1)
    pool.wait_ge(done, 2)
    nc.gpsimd.memset(qs[:, :, :, 0:1], 1.0).then_inc(done, 1)
    nc.gpsimd.memset(ks[:, :, :, 0:1], -MASK / 2).then_inc(done, 1)
    nc.gpsimd.memset(ks[:, :, :, 2:4], 1.0).then_inc(done, 1)


def write_sides(nc, dve, g, G, qs, ks, scaled, step, ready, with_lift):
    flat = scaled[:, :, :, :].rearrange("p t h d -> p (t h) d")
    nc.vector.tensor_copy(side_rows(ks, 1, 1), one_group(g.kbit, G))
    nc.vector.tensor_copy(side_rows(qs, 1, 1), one_group(g.qbit, G))
    nc.vector.tensor_scalar(flat, one_group(g.q, G), DH ** -0.5, None, ALU.mult)
    if with_lift:
        nc.vector.tensor_copy(side_rows(qs, 2, 1).bitcast(F32R), one_group(g.lift, G))
    nc.vector.tensor_copy(side_rows(ks, 4, DH).bitcast(F32R), one_group(g.q, G)).then_inc(step, 1)
    dve.wait_ge(step, 2 * G + 1)
    nc.vector.tensor_copy(side_rows(ks, 4 + DH, DH), side_rows(ks, 4, DH))
    nc.vector.tensor_tensor(side_rows(ks, 4 + 2 * DH, DH), one_group(g.q, G), side_rows(ks, 4, DH), ALU.subtract)
    if with_lift:
        nc.vector.tensor_tensor(side_rows(qs, 3, 1), one_group(g.lift, G), side_rows(qs, 2, 1), ALU.subtract)
    nc.vector.tensor_copy(side_rows(qs, 4, DH).bitcast(F32R), flat).then_inc(step, 1)
    dve.wait_ge(step, 2 * G + 2)
    nc.vector.tensor_tensor(side_rows(qs, 4 + DH, DH), flat, side_rows(qs, 4, DH), ALU.subtract)
    nc.vector.tensor_copy(side_rows(qs, 4 + 2 * DH, DH), side_rows(qs, 4, DH)).then_inc(ready, 1)


def maxima(nc, g, a):
    with ExitStack() as ctx:
        def sb(name, shape, dt=F32):
            return ctx.enter_context(nc.sbuf_tensor(name, shape, dt))

        def sem(name):
            return ctx.enter_context(nc.semaphore(name))

        qs = sb("mx_qs", [P, GT, HPG, AUG])
        ks = sb("mx_ks", [P, GT, HPG, AUG])
        scaled = sb("mx_scaled", [P, GT, HPG, DH])
        qT = sb("mx_qT", [P, T], F32R)
        kT = sb("mx_kT", [P, T], F32R)
        peak = sb("mx_peak", [P, GT, HPG])
        pb = g.pb
        place = lambda i: pb[:, 2 * i:2 * i + 2, :].rearrange("p a n -> p (a n)")
        USES = GT * HPG

        cleared = sem("mx_cleared")
        step = sem("mx_step")
        sides_ready = sem("mx_sides_ready")
        turned = sem("mx_turned")
        taken = sem("mx_taken")
        s_ready = sem("mx_s_ready")
        peak_ready = sem("mx_peak_ready")
        lift_ready = sem("mx_lift_ready")

        block = ctx.enter_context(nc.Block())

        @block.gpsimd
        def _(pool):
            clear_sides(nc, pool, qs, ks, cleared)

        @block.vector
        def _(dve):
            large = dve.value_load(g.large[0:1, 0:1])
            with dve.If(large > 0):
                dve.wait_ge(cleared, 5)
                with dve.Fori(0, NG) as G:
                    write_sides(nc, dve, g, G, qs, ks, scaled, step, sides_ready, False)
                    dve.wait_ge(turned, 2 * G + 2)
                    nc.vector.tensor_copy(qT[:, :], place(2))
                    nc.vector.tensor_copy(kT[:, :], place(3)).then_inc(taken, 1)
                    for t in range(GT):
                        for h in range(HPG):
                            n = t * HPG + h
                            dve.wait_ge(s_ready, G * USES + (n + 1))
                            nc.vector.tensor_reduce(peak[:, t, h:h + 1], place(n % 2), AX.X, ALU.max).then_inc(peak_ready, 1)
                    dve.wait_ge(peak_ready, G * USES + USES)
                    nc.vector.tensor_scalar(one_group(g.lift, G), peak[:, :, :].rearrange("p t (h d) -> p (t h) d", d=1),
                                            -1.0, None, ALU.mult).then_inc(lift_ready, 1)
                    dve.wait_ge(lift_ready, G + 1)

        @block.tensor
        def _(pe):
            large = pe.value_load(g.large[0:1, 0:1])
            with pe.If(large > 0):
                with pe.Fori(0, NG) as G:
                    pe.wait_ge(sides_ready, G + 1)
                    for i, side in enumerate((qs, ks)):
                        for t in range(GT):
                            last = nc.tensor.transpose(place(2 + i)[:, t * P:(t + 1) * P],
                                                       side[:, t, :, :].rearrange("p h r -> p (h r)"), g.ident[:, :])
                        last.then_inc(turned, 1)
                    pe.wait_ge(taken, G + 1)
                    for t in range(GT):
                        for h in range(HPG):
                            n = t * HPG + h
                            if n >= 2:
                                pe.wait_ge(peak_ready, G * USES + (n - 1))
                            part = slice(h * AUG, (h + 1) * AUG)
                            for half in range(2):
                                cols = slice(half * CH, (half + 1) * CH)
                                last = nc.tensor.matmul(place(n % 2)[:, cols], qT[part, t * P:(t + 1) * P], kT[part, cols],
                                                        start=True, stop=True)
                            last.then_inc(s_ready, 1)


def attend(nc, g, a):
    with ExitStack() as ctx:
        def sb(name, shape, dt=F32):
            return ctx.enter_context(nc.sbuf_tensor(name, shape, dt))

        def sem(name):
            return ctx.enter_context(nc.semaphore(name))

        qs = sb("at_qs", [P, GT, HPG, AUG])
        ks = sb("at_ks", [P, GT, HPG, AUG])
        scaled = sb("at_scaled", [P, GT, HPG, DH])
        qT = sb("at_qT", [P, 2, T], F32R)
        kT = sb("at_kT", [P, 2, T], F32R)
        va = sb("at_va", [P, 2, GT, HPG, AUG])
        ex = sb("at_ex", [P, 2, HPG, T])
        oT = sb("at_oT", [P, T])
        rden = sb("at_rden", [P, GT, HPG])
        raw1 = sb("at_raw1", [P, 2, 3 * H])
        pb = g.pb
        ring = lambda pos: pb[:, 2 * (pos % 3):2 * (pos % 3) + 2, :].rearrange("p a n -> p (a n)")
        pv_ps = pb[:, 6:8, :].rearrange("p a n -> p (a n)")

        init_done = sem("at_init_done")
        prep_ready = sem("at_prep_ready")
        q_turned = sem("at_q_turned")
        k_turned = sem("at_k_turned")
        qT_ready = sem("at_qT_ready")
        kT_ready = sem("at_kT_ready")
        s_ready = sem("at_s_ready")
        exp_done = sem("at_exp_done")
        pv_done = sem("at_pv_done")
        oT_ready = sem("at_oT_ready")
        o_turned = sem("at_o_turned")
        o_ready = sem("at_o_ready")
        raw1_in = [sem(f"at_raw1_in{i}") for i in range(2)]
        raw1_used = sem("at_raw1_used")
        prep_step = sem("at_prep_step")
        rden_ready = sem("at_rden_ready")
        high_ready = sem("at_high_ready")

        uses = [("S", n) for n in range(GT * HPG)]
        uses.insert(8, ("O", 0))
        uses.insert(25, ("Q", 0))
        uses.insert(26, ("K", 0))
        assert len(uses) == 35
        POS = {kind: pos for pos, (kind, n) in enumerate(uses) if kind != "S"}
        LEN = 36

        def place_free(eng, G, pos, first, last):
            back = pos - 3
            if back < 0:
                if first:
                    return
                back += LEN
                G = G - 1
                if back == LEN - 1:
                    back -= 3
            kind, n = uses[back]
            if kind == "S":
                eng.wait_ge(exp_done, G * (GT * HPG) + (n + 1))
            if kind == "O" and not first:
                eng.wait_ge(o_ready, G)
            if kind == "Q" and not last:
                eng.wait_ge(qT_ready, G + 2)
            if kind == "K" and not last:
                eng.wait_ge(kT_ready, G + 2)

        def groups(eng, group):
            group(0, 0, True, False)
            with eng.Fori(0, (NG - 2) // 2) as i:
                group(2 * i + 1, 1, False, False)
                group(2 * i + 2, 0, False, False)
            group(NG - 1, 1, False, True)

        block = ctx.enter_context(nc.Block())

        @block.sync
        def _(sp):
            for e in range(E):
                if e >= 2:
                    sp.wait_ge(raw1_used, e - 1)
                for i, src in enumerate((a.Wg[e], a.Wu[e])):
                    sp.dma_start(raw1[:, e % 2, i * H:(i + 1) * H], src).then_inc(raw1_in[e % 2], 16)
                sp.dma_start(raw1[:, e % 2, 2 * H:3 * H].rearrange("p (k c) -> p k c", k=HC),
                             a.Wd[e].rearrange("(k p) c -> p k c", p=P)).then_inc(raw1_in[e % 2], 16)

        @block.gpsimd
        def _(pool):
            clear_sides(nc, pool, qs, ks, init_done)
            nc.gpsimd.memset(va[:, :, :, :, :], 0.0).then_inc(init_done, 1)
            pool.wait_ge(init_done, 6)
            nc.gpsimd.memset(va[:, :, :, :, DH:DH + 1], 1.0).then_inc(init_done, 1)

        @block.scalar
        def _(act):
            def group(G, par, first, last):
                for pos, (kind, n) in enumerate(uses):
                    if kind == "S":
                        kt = n // HPG
                        act.wait_ge(s_ready, G * (GT * HPG) + (n + 1))
                        if n % HPG == 0 and not (first and kt < 2):
                            act.wait_ge(pv_done, G * GT + (kt - 1))
                        nc.scalar.activation(ex[:, kt % 2, n % HPG, :], ring(pos), ACT.Exp).then_inc(exp_done, 1)

            groups(act, group)

        @block.vector
        def _(dve):
            def prepare(G, par, first):
                if not first:
                    dve.wait_ge(k_turned, G)
                nc.vector.tensor_copy(va[:, par, :, :, 0:DH].rearrange("p t h d -> p (t h) d"), one_group(g.v, G))
                write_sides(nc, dve, g, G, qs, ks, scaled, prep_step, prep_ready, True)

            def take_sides(G, par):
                dve.wait_ge(q_turned, G + 1)
                nc.vector.tensor_copy(qT[:, par, :], ring(POS["Q"])).then_inc(qT_ready, 1)
                dve.wait_ge(k_turned, G + 1)
                nc.vector.tensor_copy(kT[:, par, :], ring(POS["K"])).then_inc(kT_ready, 1)

            def take_pv(G):
                dve.wait_ge(pv_done, (G + 1) * GT)
                nc.vector.tensor_copy(oT[:, :], pv_ps).then_inc(oT_ready, 1)

            def take_out(G):
                out = ring(POS["O"]).rearrange("p (t h r) -> p t h r", t=GT, h=HPG)
                dve.wait_ge(o_turned, G + 1)
                nc.vector.reciprocal(rden[:, :, :].rearrange("p t (h o) -> p t h o", o=1), out[:, :, :, DH:DH + 1]).then_inc(rden_ready, 1)
                dve.wait_ge(rden_ready, G + 1)
                rows = lambda buf: buf.rearrange("p t h d -> p (t h) d")
                nc.vector.tensor_tensor(
                    g.ctx[:, bass.ds(G, 1), :, :, :].rearrange("p o t h d -> p (o t h) d"),
                    rows(out[:, :, :, 0:DH]),
                    rden[:, :, :].rearrange("p t (h o) -> p (t h) o", o=1).broadcast_to([P, GT * HPG, DH]), ALU.mult).then_inc(o_ready, 1)

            def split(G, par):
                raw = raw1[:, par, :]
                high, low = (buf[:, bass.ds(G, 1), :].rearrange("p o n -> p (o n)") for buf in (g.w1h, g.w1l))
                dve.wait_ge(raw1_in[par], (G - par) * 24 + 48)
                nc.vector.tensor_scalar(high, raw, W_SCALE, None, ALU.mult).then_inc(high_ready, 1)
                dve.wait_ge(high_ready, G + 1)
                nc.vector.scalar_tensor_tensor(out=low, in0=raw, scalar=W_SCALE, in1=high, op0=ALU.mult,
                                               op1=ALU.subtract).then_inc(raw1_used, 1)

            def group(G, par, first, last):
                if not first:
                    take_pv(G - 1)
                    take_out(G - 1)
                if not last:
                    prepare(G + 1, 1 - par, False)
                    take_sides(G + 1, 1 - par)
                split(G, par)

            dve.wait_ge(init_done, 7)
            prepare(0, 0, True)
            take_sides(0, 0)
            groups(dve, group)
            take_pv(NG - 1)
            take_out(NG - 1)

        @block.tensor
        def _(pe):
            def turn(src, kind, done):
                for t in range(GT):
                    last = nc.tensor.transpose(ring(POS[kind])[:, t * P:(t + 1) * P],
                                               src[:, t, :, :].rearrange("p h r -> p (h r)"), g.ident[:, :])
                last.then_inc(done, 1)

            def turn_out(G):
                pe.wait_ge(oT_ready, G + 1)
                for t in range(GT):
                    last = nc.tensor.transpose(ring(POS["O"])[:, t * P:(t + 1) * P], oT[:, t * P:(t + 1) * P], g.ident[:, :])
                last.then_inc(o_turned, 1)

            def values(G, par, kt, half, first):
                if half == 0:
                    pe.wait_ge(exp_done, G * (GT * HPG) + (kt + 1) * HPG)
                    if kt == 0 and not first:
                        pe.wait_ge(oT_ready, G)
                for h in range(HPG):
                    cols = slice(half * CH, (half + 1) * CH)
                    last = nc.tensor.matmul(pv_ps[h * AUG:(h + 1) * AUG, cols], va[:, par, kt, h, :], ex[:, kt % 2, h, cols],
                                            start=(kt == 0), stop=(kt == GT - 1))
                if half == 1:
                    last.then_inc(pv_done, 1)

            def group(G, par, first, last_group):
                pe.wait_ge(kT_ready, G + 1)
                pe.wait_ge(qT_ready, G + 1)
                for pos, (kind, n) in enumerate(uses):
                    if kind == "S":
                        kt, h = n // HPG, n % HPG
                        place_free(pe, G, pos, first, last_group)
                        part = slice(h * AUG, (h + 1) * AUG)
                        for half in range(2):
                            cols = slice(half * CH, (half + 1) * CH)
                            last = nc.tensor.matmul(ring(pos)[:, cols], kT[part, par, kt * P:(kt + 1) * P], qT[part, par, cols],
                                                    start=True, stop=True)
                        last.then_inc(s_ready, 1)
                        if h in (1, 3):
                            if kt >= 1:
                                values(G, par, kt - 1, h // 2, first)
                            elif not first:
                                values(G - 1, 1 - par, GT - 1, h // 2, False)
                    if kind == "O" and not first:
                        place_free(pe, G, pos, first, last_group)
                        turn_out(G - 1)
                    if kind in "QK" and not last_group:
                        place_free(pe, G, pos, first, last_group)
                        if kind == "Q":
                            pe.wait_ge(prep_ready, G + 2)
                        turn(qs if kind == "Q" else ks, kind, q_turned if kind == "Q" else k_turned)

            pe.wait_ge(prep_ready, 1)
            turn(qs, "Q", q_turned)
            turn(ks, "K", k_turned)
            groups(pe, group)
            values(NG - 1, 1, GT - 1, 0, False)
            values(NG - 1, 1, GT - 1, 1, False)
            turn_out(NG - 1)


def feed(nc, g, a):
    with ExitStack() as ctx:
        def sb(name, shape, dt=F32):
            return ctx.enter_context(nc.sbuf_tensor(name, shape, dt))

        def sem(name):
            return ctx.enter_context(nc.semaphore(name))

        LAG = 2
        STEPS = E * HC
        silu = sb("fd_silu", [P, 2, CH])
        h32 = sb("fd_h32", [P, 2, CH])
        hh = sb("fd_hh", [P, HC, CH], F16)
        hl = sb("fd_hl", [P, HC, CH], F16)
        eye = sb("fd_eye", [P, P], F16)
        xT = sb("fd_xT", [P, CH])
        z = sb("fd_z", [P, 2, CH])
        sums = sb("fd_sums", [P, CH])
        stats = sb("fd_stats", [P, TPC, 6])
        mv_in = sb("fd_mv_in", [P, TPC, 2])
        mv_out = sb("fd_mv_out", [P, TPC, 2])
        vare = sb("fd_vare", [P, 2, TPC])
        rs = sb("fd_rs", [P, 2, TPC])
        xn = sb("fd_xn", [P, TPC, C])
        y = sb("fd_y", [P, 2, TPC, C])
        pb = g.pb
        gate_ps = lambda k: pb[:, 2 * (k % 2), :]
        up_ps = lambda k: pb[:, 2 * (k % 2) + 1, :]
        sum_ps = lambda c: pb[:, 4 + c % 2, :]
        turn_ps = pb[:, 6, :]

        eye_ready = sem("fd_eye_ready")
        in_vare_ready = sem("fd_in_vare_ready")
        in_rs_ready = sem("fd_in_rs_ready")
        x_ready = sem("fd_x_ready")
        x_turned = sem("fd_x_turned")
        xT_ready = sem("fd_xT_ready")
        xh_ready = sem("fd_xh_ready")
        xl_ready = sem("fd_xl_ready")
        gate_ready = sem("fd_gate_ready")
        up_ready = sem("fd_up_ready")
        silu_ready = sem("fd_silu_ready")
        h_ready = sem("fd_h_ready")
        hh_ready = sem("fd_hh_ready")
        hl_ready = sem("fd_hl_ready")
        added = sem("fd_added")
        summed = sem("fd_summed")
        sums_ready = sem("fd_sums_ready")
        sums_turned = sem("fd_sums_turned")
        out_vare_ready = sem("fd_out_vare_ready")
        out_rs_ready = sem("fd_out_rs_ready")
        y_ready = sem("fd_y_ready")
        stored = [sem(f"fd_stored{i}") for i in range(2)]
        dve_step = sem("fd_dve_step")

        block = ctx.enter_context(nc.Block())

        def whole(eng, step, mid, late):
            for c in range(NC):
                for k in range(HC):
                    step(c, 0, k)
                mid(c)
                with eng.Fori(1, E // 2) as e:
                    for k in range(HC):
                        step(c, e, k)
                late(c)
                with eng.Fori(E // 2, E) as e:
                    for k in range(HC):
                        step(c, e, k)

        def wait(eng, sem, value):
            if not (isinstance(value, int) and value <= 0):
                eng.wait_ge(sem, value)

        @block.sync
        def _(sp):
            for c in range(NC):
                sp.wait_ge(y_ready, c + 1)
                sp.dma_start(a.out_tiles[:, c * TPC:(c + 1) * TPC, :], y[:, c % 2, :, :]).then_inc(stored[c % 2], 16)
            sp.wait_ge(stored[0], 16 * (NC // 2))
            sp.wait_ge(stored[1], 16 * (NC // 2))

        @block.gpsimd
        def _(pool):
            nc.gpsimd.memset(eye[:, :], 0.0).then_inc(eye_ready, 1)
            pool.wait_ge(eye_ready, 1)
            nc.gpsimd.affine_select(out=eye[:, :], in_=eye[:, :], compare_op=ALU.not_equal, fill=W_SCALE,
                                    base=0, pattern=[[-1, P]], channel_multiplier=1).then_inc(eye_ready, 1)

            def rsqrt_in(c):
                pool.wait_ge(in_vare_ready, c + 1)
                nc.gpsimd.tensor_tensor(rs[:, 0, :], vare[:, 0, :], g.minus_half[:, 0:TPC], ALU.pow).then_inc(in_rs_ready, 1)

            def rsqrt_out(c):
                pool.wait_ge(out_vare_ready, c + 1)
                nc.gpsimd.tensor_tensor(rs[:, 1, :], vare[:, 1, :], g.minus_half[:, 0:TPC], ALU.pow).then_inc(out_rs_ready, 1)

            rsqrt_in(0)
            for c in range(NC):
                if c < NC - 1:
                    rsqrt_in(c + 1)
                if c >= 1:
                    rsqrt_out(c - 1)
            rsqrt_out(NC - 1)

        @block.scalar
        def _(act):
            def take_x(c):
                cols = slice(c * CH, (c + 1) * CH)
                act.wait_ge(x_turned, c + 1)
                if c >= 1:
                    act.wait_ge(xl_ready, c)
                nc.scalar.activation(xT[:, :], turn_ps, ACT.Copy).then_inc(xT_ready, 1)
                nc.scalar.activation(g.xh[:, cols], turn_ps, ACT.Copy).then_inc(xh_ready, 1)

            def take_sums(c):
                act.wait_ge(summed, c + 1)
                if c >= 1:
                    act.wait_ge(sums_turned, c)
                nc.scalar.activation(sums[:, :], sum_ps(c), ACT.Copy, scale=1.0 / W_SCALE).then_inc(sums_ready, 1)

            def high(n, k):
                act.wait_ge(h_ready, n + 1)
                wait(act, added, n - 2)
                nc.scalar.activation(hh[:, k, :], h32[:, k % 2, :], ACT.Copy).then_inc(hh_ready, 1)

            def step(c, e, k):
                n = c * STEPS + e * HC + k
                act.wait_ge(gate_ready, n + 1)
                wait(act, h_ready, n - 1)
                nc.scalar.activation(silu[:, k % 2, :], gate_ps(k), ACT.Silu, scale=1.0 / W_SCALE).then_inc(silu_ready, 1)
                if not (isinstance(n, int) and n == 0):
                    high(n - 1, (k - 1) % HC)
                if c >= 1 and isinstance(e, int) and k == LAG:
                    take_sums(c - 1)

            take_x(0)
            whole(act, step, lambda c: None, lambda c: take_x(c + 1) if c < NC - 1 else None)
            high(NC * STEPS - 1, HC - 1)
            take_sums(NC - 1)

        @block.vector
        def _(dve):
            link = chain(dve, dve_step)

            def norm_stats(mv, of):
                for i in range(TPC):
                    last = nc.vector.bn_stats(stats[:, i, :], of[:, i * C:(i + 1) * C])
                link(last)
                for i in range(TPC):
                    last = nc.vector.bn_aggr(mv[:, i, :], stats[:, i, :])
                link(last)

            def norm_in_stats(c):
                b, t0, rows = c // CPB, (c % CPB) * TPC, slice(c * TPC, (c + 1) * TPC)
                zc = z[:, c % 2, :]
                link(nc.vector.tensor_tensor(
                    zc.rearrange("p (t g n) -> p t g n", t=TPC, g=HG),
                    g.x0[:, rows, :].rearrange("p t (g n) -> p t g n", g=HG),
                    g.ctx[:, b * HG:(b + 1) * HG, t0:t0 + TPC, :, :].rearrange("p g t h d -> p t g (h d)"), ALU.add))
                norm_stats(mv_in, zc)
                nc.vector.tensor_scalar(vare[:, 0, :], mv_in[:, :, 1], LN_EPS, None, ALU.add).then_inc(in_vare_ready, 1)

            def norm_in(c):
                dve.wait_ge(in_rs_ready, c + 1)
                for i in range(TPC):
                    last = nc.vector.tensor_scalar(xn[:, i, :], z[:, c % 2, i * C:(i + 1) * C], mv_in[:, i, 0:1], rs[:, 0, i:i + 1],
                                                   ALU.subtract, ALU.mult)
                last.then_inc(x_ready, 1)
                dve.wait_ge(xh_ready, c + 1)
                nc.vector.tensor_tensor(g.xl[:, c * CH:(c + 1) * CH], xT[:, :], g.xh[:, c * CH:(c + 1) * CH],
                                        ALU.subtract).then_inc(xl_ready, 1)

            def norm_out_stats(c):
                dve.wait_ge(sums_turned, c + 1)
                norm_stats(mv_out, sum_ps(c))
                nc.vector.tensor_scalar(vare[:, 1, :], mv_out[:, :, 1], LN_EPS, None, ALU.add).then_inc(out_vare_ready, 1)

            def norm_out(c):
                dve.wait_ge(out_rs_ready, c + 1)
                if c >= 2:
                    dve.wait_ge(stored[c % 2], 16)
                for i in range(TPC):
                    last = nc.vector.tensor_scalar(y[:, c % 2, i, :], sum_ps(c)[:, i * C:(i + 1) * C], mv_out[:, i, 0:1],
                                                   rs[:, 1, i:i + 1], ALU.subtract, ALU.mult)
                last.then_inc(y_ready, 1)

            def low(n, k):
                dve.wait_ge(hh_ready, n + 1)
                wait(dve, added, n - 2)
                nc.vector.tensor_tensor(hl[:, k, :], h32[:, k % 2, :], hh[:, k, :], ALU.subtract).then_inc(hl_ready, 1)

            def step(c, e, k):
                n = c * STEPS + e * HC + k
                dve.wait_ge(up_ready, n + 1)
                dve.wait_ge(silu_ready, n + 1)
                wait(dve, hl_ready, n - 1)
                nc.vector.scalar_tensor_tensor(out=h32[:, k % 2, :], in0=up_ps(k), scalar=1.0 / W_SCALE, in1=silu[:, k % 2, :],
                                               op0=ALU.mult, op1=ALU.mult).then_inc(h_ready, 1)
                if not (isinstance(n, int) and n == 0):
                    low(n - 1, (k - 1) % HC)

            def mid(c):
                if c < NC - 1:
                    norm_in_stats(c + 1)
                if c >= 1:
                    norm_out_stats(c - 1)

            def late(c):
                if c < NC - 1:
                    norm_in(c + 1)
                if c >= 1:
                    norm_out(c - 1)

            norm_in_stats(0)
            norm_in(0)
            whole(dve, step, mid, late)
            low(NC * STEPS - 1, HC - 1)
            norm_out_stats(NC - 1)
            norm_out(NC - 1)

        @block.tensor
        def _(pe):
            def turn_x(c):
                pe.wait_ge(x_ready, c + 1)
                for i in range(TPC):
                    last = nc.tensor.transpose(turn_ps[:, i * P:(i + 1) * P], xn[:, i, :], g.ident[:, :])
                last.then_inc(x_turned, 1)

            def begin(c):
                if c >= 2:
                    pe.wait_ge(y_ready, c - 1)
                nc.tensor.matmul(sum_ps(c), eye[:, :], g.xh[:, c * CH:(c + 1) * CH], start=True, stop=False, skip_group_check=True)

            def end(c):
                nc.tensor.matmul(sum_ps(c), eye[:, :], g.xl[:, c * CH:(c + 1) * CH], start=False, stop=True,
                                 skip_group_check=True).then_inc(summed, 1)

            def turn_sums(c):
                pe.wait_ge(sums_ready, c + 1)
                for i in range(TPC):
                    last = nc.tensor.transpose(sum_ps(c)[:, i * P:(i + 1) * P], sums[:, i * P:(i + 1) * P], g.ident[:, :])
                last.then_inc(sums_turned, 1)

            def add(c, e, k, n):
                pe.wait_ge(hl_ready, n + 1)
                wd = slice(2 * H + k * P, 2 * H + (k + 1) * P)
                for w, h in ((g.w1h, hh), (g.w1h, hl), (g.w1l, hh)):
                    last = nc.tensor.matmul(sum_ps(c), w[:, bass.ds(e, 1), wd], h[:, k, :], start=False, stop=False,
                                            skip_group_check=True)
                last.then_inc(added, 1)

            def step(c, e, k):
                n = c * STEPS + e * HC + k
                x = slice(c * CH, (c + 1) * CH)
                wait(pe, silu_ready, n - 1)
                wait(pe, h_ready, n - 1)
                for ps, lo, done in ((gate_ps(k), 0, gate_ready), (up_ps(k), H, up_ready)):
                    w = slice(lo + k * P, lo + (k + 1) * P)
                    for i, (lhs, rhs) in enumerate(((g.w1h, g.xh), (g.w1h, g.xl), (g.w1l, g.xh))):
                        last = nc.tensor.matmul(ps, lhs[:, bass.ds(e, 1), w], rhs[:, x], start=(i == 0), stop=(i == 2))
                    last.then_inc(done, 1)
                if k >= LAG:
                    add(c, e, k - LAG, n - LAG)
                elif isinstance(e, int) and e == 0:
                    if c >= 1:
                        add(c - 1, E - 1, k - LAG + HC, n - LAG)
                        if k == LAG - 1:
                            end(c - 1)
                            begin(c)
                else:
                    add(c, e - 1, k - LAG + HC, n - LAG)

            turn_x(0)
            pe.wait_ge(eye_ready, 2)
            pe.wait_ge(xl_ready, 1)
            begin(0)

            def mid(c):
                if c >= 1:
                    turn_sums(c - 1)

            def late(c):
                if c < NC - 1:
                    turn_x(c + 1)
                    pe.wait_ge(xl_ready, c + 2)

            whole(pe, step, mid, late)
            for k in range(HC - LAG, HC):
                add(NC - 1, E - 1, k, NC * STEPS - HC + k)
            end(NC - 1)
            turn_sums(NC - 1)


def mixture0(nc, ctx, g):
    g.w0h = ctx.enter_context(nc.sbuf_tensor("w0h", [P, E, 2 * H], F16))
    g.w0l = ctx.enter_context(nc.sbuf_tensor("w0l", [P, E, 2 * H], F16))
    g.raw0 = ctx.enter_context(nc.sbuf_tensor("raw0", [P, E, 2 * H], F32))


def mixture1(nc, ctx, g):
    g.w1h = ctx.enter_context(nc.sbuf_tensor("w1h", [P, E, 3 * H], F16))
    g.w1l = ctx.enter_context(nc.sbuf_tensor("w1l", [P, E, 3 * H], F16))


def globals_(nc, ctx, g):
    def sb(name, shape, dt=F32):
        return ctx.enter_context(nc.sbuf_tensor(name, shape, dt))

    def sem(name):
        return ctx.enter_context(nc.semaphore(name))

    g.pb = ctx.enter_context(nc.psum_tensor("pb", [P, 8, CH], F32))
    g.x0 = sb("x0", [P, NT, C])
    g.x1 = sb("x1", [P, NT, C])
    g.ident = sb("ident", [P, P])
    g.minus_half = sb("minus_half", [P, NT])
    g.cols = sb("cols", [P, NCOLS])
    g.gate = sb("gate", [P, E, NT])
    g.gate_down = sb("gate_down", [P, E, NT])
    g.gate_down_flat = g.gate_down[:, :, :].rearrange("p e t -> p (e t)")
    g.moe = sb("moe", [P, NT, C])
    g.xh = sb("xh", [P, N], F16)
    g.xl = sb("xl", [P, N], F16)
    g.raw0_scaled = sem("raw0_scaled")
    g.w0h_ready = sem("w0h_ready")
    g.w0l_ready = sem("w0l_ready")
    g.q = sb("q", [P, NG, GT, HPG, DH])
    g.v = sb("v", [P, NG, GT, HPG, DH])
    g.ctx = sb("ctx", [P, NG, GT, HPG, DH])
    g.qbit = sb("qbit", [P, NG, GT, HPG])
    g.kbit = sb("kbit", [P, NG, GT, HPG])
    g.lift = sb("lift", [P, NG, GT, HPG])
    g.large = sb("large", [P, 1], mybir.dt.int32)
    g.raw0_in = [sem(f"raw0_in{e}") for e in range(E)]
    g.cols_ready = sem("cols_ready")
    g.junk_done = sem("junk_done")


_INS = ['L0_attn_x', 'L0_attn_ln1_w', 'L0_attn_ln2_w', 'L0_attn_time_decay', 'L0_attn_time_first', 'L0_attn_time_mix_k',
        'L0_attn_time_mix_v', 'L0_attn_time_mix_r', 'L0_attn_W_key', 'L0_attn_W_value', 'L0_attn_W_recept',
        'L0_attn_W_out', 'L0_attn_time_mix_k2', 'L0_attn_time_mix_r2', 'L0_attn_W_key2', 'L0_attn_W_value2',
        'L0_attn_W_recept2', 'L0_ffn_wg', 'L0_ffn_w1', 'L0_ffn_b1', 'L0_ffn_w2', 'L0_ffn_b2', 'L1_attn_qk_w',
        'L1_attn_qk_b', 'L1_attn_v_w', 'L1_attn_v_b', 'L1_attn_hash_a', 'L1_ffn_Wg', 'L1_ffn_Wu', 'L1_ffn_Wd']


def inputs(a, aps):
    (a.x, a.ln1_w, a.ln2_w, a.decay, a.first, a.mix_k, a.mix_v, a.mix_r, a.W_key, a.W_value, a.W_recept, a.W_out,
     a.mix_k2, a.mix_r2, a.W_key2, a.W_value2, a.W_recept2, a.wg, a.w1, a.b1, a.w2, a.b2, a.qk_w, a.qk_b, a.v_w, a.v_b,
     a.hash_a, a.Wg, a.Wu, a.Wd) = aps
    a.x_tiles = a.x.rearrange("b (t p) c -> p (b t) c", p=P)


def program(nc, *aps):
    with ExitStack() as ctx:
        g, a = Shared(), Shared()
        inputs(a, aps[:-1])
        a.out_tiles = aps[-1].rearrange("b (t p) c -> p (b t) c", p=P)
        globals_(nc, ctx, g)
        with ExitStack() as weights:
            mixture0(nc, weights, g)
            time_mix(nc, g, a)
            channel_mix(nc, g, a)
            route(nc, g, a)
            experts(nc, g, a)
            project(nc, g, a)
            maxima(nc, g, a)
        with ExitStack() as weights:
            mixture1(nc, weights, g)
            attend(nc, g, a)
            feed(nc, g, a)


_OUTS = [((B, T, C), 'float32')]


def kernel(**inputs):
    import numpy as _np
    import concourse.bacc as _bacc
    from concourse import mybir as _mybir
    from concourse.bass_utils import run_bass_kernel_spmd as _run

    nc = _bacc.Bacc("TRN2", target_bir_lowering=False, num_devices=1)
    arrays, args = {}, []
    for name in _INS:
        a = _np.ascontiguousarray(inputs[name])
        arrays[f"in_{name}_dram"] = a
        args.append(nc.dram_tensor(f"in_{name}_dram", a.shape, _mybir.dt.from_np(a.dtype), kind="ExternalInput").ap())
    for i, (shape, dtype) in enumerate(_OUTS):
        dt = _mybir.dt.from_np(_np.dtype(dtype))
        args.append(nc.dram_tensor(f"out_{i}_dram", shape, dt, kind="ExternalOutput").ap())
    program(nc, *args)
    r = _run(nc, [arrays], core_ids=[0])
    return r.results[0]["out_0_dram"]
```

```python
import math
from contextlib import ExitStack

import concourse.bass as bass
from concourse import mybir

ALU = mybir.AluOpType
ACT = mybir.ActivationFunctionType
AX = mybir.AxisListType
F32 = mybir.dt.float32
F16 = mybir.dt.float16
F32R = mybir.dt.float32r

P = 128
B, T, C = 2, 1024, 128
N = B * T
NT = N // P
CH = 512
NC = N // CH
TPC = CH // P
CPB = T // CH
E = 8
H = 512
HC = H // P
TOPK = 2
CAP = TOPK * N // E
HEADS = 16
DH = C // HEADS
HPG = 4
HG = HEADS // HPG
NG = B * HG
GT = T // P
AUG = P // HPG
HASH = DH + 2
U_HASH = 0.75
MASK = 10000.0
SAFE_SCORE = 60.0
RMS_EPS = 1e-6
LN_EPS = 1e-5
WKV_EPS = 1e-8
CLIP = 20.0
W_SCALE = 256.0

LN1, LN2, DECAY, FIRST, MIXK, MIXV, MIXR, MIXK2, MIXR2, B1 = range(10)
NCOLS = B1 + E * HC


class Shared:
    pass


def schedule(chunks, order):
    return [(s - p, p) for s in range(chunks + len(order) - 1) for p in order if 0 <= s - p < chunks]


def chain(eng, sem, count=None):
    count = [0] if count is None else count

    def link(ins):
        count[0] += 1
        ins.then_inc(sem, 1)
        eng.wait_ge(sem, count[0])

    return link


def shifted(buf, c):
    b, o = c // CPB, 1 + (c % CPB) * CH
    return buf[:, b, o:o + CH], buf[:, b, o - 1:o - 1 + CH]


def scale_raw(nc, pool, g, e):
    if e < E:
        pool.wait_ge(g.raw0_in[e], 32)
        nc.gpsimd.tensor_scalar(g.raw0[:, e, :], g.raw0[:, e, :], W_SCALE, 1.0, ALU.mult, ALU.mult).then_inc(g.raw0_scaled, 1)
    if e >= 1:
        pool.wait_ge(g.w0h_ready, e)
        nc.gpsimd.tensor_tensor(g.w0l[:, e - 1, :], g.raw0[:, e - 1, :], g.w0h[:, e - 1, :], ALU.subtract).then_inc(g.w0l_ready, 1)


def high_part(nc, act, g, e):
    act.wait_ge(g.raw0_scaled, e + 1)
    nc.scalar.activation(g.w0h[:, e, :], g.raw0[:, e, :], ACT.Copy).then_inc(g.w0h_ready, 1)


def time_mix(nc, g, a):
    with ExitStack() as ctx:
        def sb(name, shape, dt=F32):
            return ctx.enter_context(nc.sbuf_tensor(name, shape, dt))

        def sem(name):
            return ctx.enter_context(nc.semaphore(name))

        rows = sb("rows", [64, P])
        w_k, w_v, w_r, w_o = (sb(n, [P, P]) for n in ("w_k", "w_v", "w_r", "w_o"))
        junk = sb("junk", [P, P])
        ss = sb("ss", [P, NT])
        ms = sb("ms", [P, NT])
        rstd = sb("rstd", [P, NT])
        ew = sb("ew", [P, 4])
        hx = sb("hx", [P, 2, TPC, P])
        hT = sb("hT", [P, B, 1 + T])
        diff = sb("diff", [P, CH])
        xm = sb("xm", [P, 2, 3, CH])
        ex = sb("ex", [P, 2, 3, CH])
        ekv = sb("ekv", [P, CH])
        ektv = sb("ektv", [P, CH])
        aS = sb("aS", [P, B, 1 + T])
        bS = sb("bS", [P, B, 1 + T])
        den = sb("den", [P, CH])
        rden = sb("rden", [P, CH])
        yT = sb("yT", [P, 2, CH])
        pb = g.pb
        tr_bank = lambda c: pb[:, c % 2, :]
        k_ps, v_ps, r_ps = pb[:, 2, :], pb[:, 3, :], pb[:, 4, :]
        out_bank = lambda c: pb[:, 5 + c % 2, :]

        x_in = [sem(f"x_in{c}") for c in range(NC)]
        rows_in = sem("rows_in")
        w_in = sem("w_in")
        wo_in = sem("wo_in")
        ident_ready = sem("ident_ready")
        cols_turned = sem("cols_turned")
        zeros_ready = sem("zeros_ready")
        edecay_ready = sem("edecay_ready")
        wclip_ready = sem("wclip_ready")
        ew_ready = sem("ew_ready")
        ss_ready = sem("ss_ready")
        ms_ready = sem("ms_ready")
        rstd_ready = sem("rstd_ready")
        hx_ready = sem("hx_ready")
        turned = sem("turned")
        hT_ready = sem("hT_ready")
        xm_ready = sem("xm_ready")
        kvr_ready = sem("kvr_ready")
        ex_ready = sem("ex_ready")
        v_used = sem("v_used")
        y_ready = sem("y_ready")
        out_ready = sem("out_ready")
        x1_ready = sem("x1_ready")
        dve_step = sem("tm_dve_step")

        block = ctx.enter_context(nc.Block())
        plan = schedule(NC, (2, 1, 0, 3, 4))

        @block.sync
        def _(sp):
            def load_x(c):
                sp.dma_start(g.x0[:, c * TPC:(c + 1) * TPC, :], a.x_tiles[:, c * TPC:(c + 1) * TPC, :]).then_inc(x_in[c], 16)

            load_x(0)
            for i, v in enumerate((a.ln1_w, a.ln2_w, a.decay, a.first, a.mix_k, a.mix_v, a.mix_r, a.mix_k2, a.mix_r2)):
                sp.dma_start(rows[i:i + 1, :], v.rearrange("(a n) -> a n", a=1)).then_inc(rows_in, 16)
            sp.dma_start(rows[B1:NCOLS, :], a.b1.rearrange("e (k p) -> (e k) p", p=P)).then_inc(rows_in, 16)
            load_x(1)
            for w, src in ((w_k, a.W_key), (w_v, a.W_value), (w_r, a.W_recept)):
                sp.dma_start(w[:, :], src).then_inc(w_in, 16)
            for c in range(2, NC):
                load_x(c)
            sp.dma_start(w_o[:, :], a.W_out).then_inc(wo_in, 16)
            for e in range(E):
                sp.dma_start(g.raw0[:, e, 0:H], a.w1[e]).then_inc(g.raw0_in[e], 16)
                sp.dma_start(g.raw0[:, e, H:2 * H].rearrange("p (k c) -> p k c", k=HC),
                             a.w2[e].rearrange("(k p) c -> p k c", p=P)).then_inc(g.raw0_in[e], 16)

        @block.gpsimd
        def _(pool):
            nc.gpsimd.memset(g.ident[:, :], 0.0).then_inc(ident_ready, 1)
            pool.wait_ge(ident_ready, 1)
            nc.gpsimd.affine_select(out=g.ident[:, :], in_=g.ident[:, :], compare_op=ALU.not_equal, fill=1.0,
                                    base=0, pattern=[[-1, P]], channel_multiplier=1).then_inc(ident_ready, 1)
            nc.gpsimd.memset(g.minus_half[:, :], -0.5).then_inc(ident_ready, 1)
            pool.wait_ge(ident_ready, 3)
            for c, phase in plan:
                if phase == 0:
                    t = slice(c * TPC, (c + 1) * TPC)
                    pool.wait_ge(ms_ready, c + 1)
                    nc.gpsimd.tensor_tensor(rstd[:, t], ms[:, t], g.minus_half[:, 0:TPC], ALU.pow).then_inc(rstd_ready, 1)
                if phase == 3:
                    scale_raw(nc, pool, g, c)

        @block.scalar
        def _(act):
            for c, phase in plan:
                if phase == 0:
                    act.wait_ge(x_in[c], 16)
                    for t in range(c * TPC, (c + 1) * TPC):
                        last = nc.scalar.activation(junk[:, :], g.x0[:, t, :], ACT.Square, accum_out=ss[:, t:t + 1])
                        if t % TPC < TPC - 1:
                            last.then_inc(g.junk_done, 1)
                            act.wait_ge(g.junk_done, (TPC - 1) * c + t % TPC + 1)
                    last.then_inc(ss_ready, 1)
                    act.wait_ge(ss_ready, c + 1)
                if phase == 1:
                    for i in range(TPC):
                        t = c * TPC + i
                        if i == 0:
                            act.wait_ge(rstd_ready, c + 1)
                            if c >= 2:
                                act.wait_ge(turned, c - 1)
                        last = nc.scalar.activation(hx[:, c % 2, i, :], g.x0[:, t, :], ACT.Copy, scale=rstd[:, t:t + 1])
                    last.then_inc(hx_ready, 1)
                    if c == 0:
                        act.wait_ge(g.cols_ready, 1)
                        nc.scalar.activation(ew[:, 0:1], g.cols[:, DECAY:DECAY + 1], ACT.Exp).then_inc(edecay_ready, 1)
                        act.wait_ge(wclip_ready, 1)
                        nc.scalar.activation(ew[:, 2:3], ew[:, 1:2], ACT.Exp).then_inc(ew_ready, 1)
                if phase == 2:
                    act.wait_ge(turned, c + 1)
                    nc.scalar.activation(shifted(hT, c)[0], tr_bank(c), ACT.Copy,
                                         scale=g.cols[:, LN1:LN1 + 1]).then_inc(hT_ready, 1)
                if phase == 3:
                    act.wait_ge(kvr_ready, c + 1)
                    if c >= 2:
                        act.wait_ge(y_ready, c - 1)
                    nc.scalar.activation(ex[:, c % 2, 0, :], k_ps, ACT.Exp).then_inc(ex_ready, 1)
                    nc.scalar.activation(ex[:, c % 2, 1, :], k_ps, ACT.Exp,
                                         bias=g.cols[:, FIRST:FIRST + 1]).then_inc(ex_ready, 1)
                    nc.scalar.activation(ex[:, c % 2, 2, :], r_ps, ACT.Tanh, scale=0.5).then_inc(ex_ready, 1)
                    high_part(nc, act, g, c)

        @block.vector
        def _(dve):
            link = chain(dve, dve_step)
            for buf in (hT, aS, bS):
                nc.vector.memset(buf[:, :, 0:1], 0.0).then_inc(zeros_ready, 1)
            dve.wait_ge(zeros_ready, 3)
            for c, phase in plan:
                h, sh = shifted(hT, c)
                if phase == 0:
                    t = slice(c * TPC, (c + 1) * TPC)
                    dve.wait_ge(ss_ready, c + 1)
                    nc.vector.tensor_scalar(ms[:, t], ss[:, t], 1.0 / C, RMS_EPS, ALU.mult, ALU.add).then_inc(ms_ready, 1)
                    if c == 0:
                        dve.wait_ge(cols_turned, 1)
                        nc.vector.tensor_copy(g.cols[:, :], pb[:, 7, 0:NCOLS]).then_inc(g.cols_ready, 1)
                        dve.wait_ge(edecay_ready, 1)
                        link(nc.vector.tensor_scalar(ew[:, 3:4], ew[:, 0:1], -1.0, -CLIP, ALU.mult, ALU.max))
                        nc.vector.tensor_scalar(ew[:, 1:2], ew[:, 3:4], CLIP, None, ALU.min).then_inc(wclip_ready, 1)
                if phase == 2:
                    dve.wait_ge(hT_ready, c + 1)
                    if c >= 2:
                        dve.wait_ge(kvr_ready, c - 1)
                    link(nc.vector.tensor_tensor(diff[:, :], h, sh, ALU.subtract))
                    for i, m in enumerate((MIXK, MIXV, MIXR)):
                        last = nc.vector.scalar_tensor_tensor(out=xm[:, c % 2, i, :], in0=diff[:, :], scalar=g.cols[:, m:m + 1],
                                                              in1=sh, op0=ALU.mult, op1=ALU.add)
                    last.then_inc(xm_ready, 1)
                    dve.wait_ge(xm_ready, c + 1)
                if phase == 3:
                    b = c // CPB
                    ek, ekt, th = (ex[:, c % 2, i, :] for i in range(3))
                    a_now, a_before = shifted(aS, c)
                    b_now, b_before = shifted(bS, c)
                    dve.wait_ge(ex_ready, 3 * (c + 1))
                    if c == 0:
                        dve.wait_ge(ew_ready, 1)
                    link(nc.vector.tensor_scalar(ex[:, c % 2, 0:2, :], ex[:, c % 2, 0:2, :], math.exp(-CLIP), math.exp(CLIP),
                                                 ALU.max, ALU.min))
                    nc.vector.tensor_tensor(ektv[:, :], ekt, v_ps, ALU.mult)
                    nc.vector.tensor_tensor(ekv[:, :], ek, v_ps, ALU.mult).then_inc(v_used, 1)
                    dve.wait_ge(v_used, c + 1)
                    link(nc.vector.tensor_tensor_scan(a_now, ew[:, 2:3].broadcast_to([P, CH]), ekv[:, :],
                                                      a_before[:, 0:1], ALU.mult, ALU.add))
                    link(nc.vector.tensor_tensor_scan(b_now, ew[:, 2:3].broadcast_to([P, CH]), ek,
                                                      b_before[:, 0:1], ALU.mult, ALU.add))
                    link(nc.vector.scalar_tensor_tensor(out=den[:, :], in0=b_before, scalar=WKV_EPS, in1=ekt,
                                                        op0=ALU.add, op1=ALU.add))
                    link(nc.vector.tensor_tensor(ektv[:, :], ektv[:, :], a_before, ALU.add))
                    link(nc.vector.reciprocal(rden[:, :], den[:, :]))
                    link(nc.vector.tensor_tensor(ektv[:, :], ektv[:, :], rden[:, :], ALU.mult))
                    if c >= 2:
                        dve.wait_ge(out_ready, c - 1)
                    nc.vector.scalar_tensor_tensor(out=yT[:, c % 2, :], in0=th, scalar=1.0, in1=ektv[:, :],
                                                   op0=ALU.add, op1=ALU.mult).then_inc(y_ready, 1)
                    dve.wait_ge(y_ready, c + 1)
                if phase == 4:
                    dve.wait_ge(out_ready, c + 1)
                    nc.vector.scalar_tensor_tensor(
                        out=g.x1[:, c * TPC:(c + 1) * TPC, :].rearrange("p t c -> p (t c)"), in0=out_bank(c), scalar=0.5,
                        in1=g.x0[:, c * TPC:(c + 1) * TPC, :].rearrange("p t c -> p (t c)"),
                        op0=ALU.mult, op1=ALU.add).then_inc(x1_ready, 1)

        @block.tensor
        def _(pe):
            pe.wait_ge(ident_ready, 2)
            pe.wait_ge(rows_in, 16 * 10)
            nc.tensor.transpose(pb[:, 7, 0:NCOLS], rows[0:NCOLS, :], g.ident[0:NCOLS, 0:NCOLS]).then_inc(cols_turned, 1)
            for c, phase in plan:
                if phase == 1:
                    pe.wait_ge(hx_ready, c + 1)
                    if c >= 2:
                        pe.wait_ge(hT_ready, c - 1)
                    for i in range(TPC):
                        last = nc.tensor.transpose(tr_bank(c)[:, i * P:(i + 1) * P], hx[:, c % 2, i, :], g.ident[:, :])
                    last.then_inc(turned, 1)
                if phase == 2:
                    if c == 0:
                        pe.wait_ge(w_in, 48)
                    pe.wait_ge(xm_ready, c + 1)
                    if c >= 1:
                        pe.wait_ge(ex_ready, 3 * c)
                        pe.wait_ge(v_used, c)
                    for i, (w, ps) in enumerate(((w_k, k_ps), (w_v, v_ps), (w_r, r_ps))):
                        last = nc.tensor.matmul(ps, w[:, :], xm[:, c % 2, i, :], start=True, stop=True)
                    last.then_inc(kvr_ready, 1)
                if phase == 3:
                    if c == 0:
                        pe.wait_ge(wo_in, 16)
                    pe.wait_ge(y_ready, c + 1)
                    if c >= 2:
                        pe.wait_ge(x1_ready, c - 1)
                    for i in range(TPC):
                        last = nc.tensor.matmul(out_bank(c)[:, i * P:(i + 1) * P], yT[:, c % 2, i * P:(i + 1) * P], w_o[:, :],
                                                start=True, stop=True)
                    last.then_inc(out_ready, 1)


def channel_mix(nc, g, a):
    with ExitStack() as ctx:
        def sb(name, shape, dt=F32):
            return ctx.enter_context(nc.sbuf_tensor(name, shape, dt))

        def sem(name):
            return ctx.enter_context(nc.semaphore(name))

        w_k = sb("w_k2", [P, H])
        w_v = sb("w_v2", [P, HC, P])
        w_r = sb("w_r2", [P, P])
        junk = sb("junk2", [P, P])
        ss = sb("ss2", [P, NT])
        ms = sb("ms2", [P, NT])
        rstd = sb("rstd2", [P, NT])
        hx = sb("hx2", [P, 2, TPC, P])
        hT = sb("hT2", [P, B, 1 + T])
        diff = sb("diff2", [P, CH])
        xm = sb("xm2", [P, 2, 2, CH])
        relu = sb("relu2", [P, 2, CH])
        sq = sb("sq2", [P, 2, HC, CH])
        th = sb("th2", [P, 2, CH])
        z = sb("z2", [P, 2, CH])
        stats = sb("stats2", [P, TPC, 6])
        mv = sb("mv2", [P, 2, TPC, 2])
        vare = sb("vare2", [P, 2, TPC])
        rs = sb("rs2", [P, 2, TPC])
        pb = g.pb
        tr_bank = lambda c: pb[:, c % 2, :]
        key_bank = lambda n: pb[:, 2 + n % 2, :]
        r_ps = pb[:, 4, :]
        val_bank = lambda c: pb[:, 5 + c % 2, :]

        w_in = sem("cm_w_in")
        ss_ready = sem("cm_ss_ready")
        zero_ready = sem("cm_zero_ready")
        ms_ready = sem("cm_ms_ready")
        rstd_ready = sem("cm_rstd_ready")
        hx_ready = sem("cm_hx_ready")
        turned = sem("cm_turned")
        hT_ready = sem("cm_hT_ready")
        xm_ready = sem("cm_xm_ready")
        key_ready = sem("cm_key_ready")
        relu_ready = sem("cm_relu_ready")
        sq_ready = sem("cm_sq_ready")
        r_ready = sem("cm_r_ready")
        th_ready = sem("cm_th_ready")
        val_ready = sem("cm_val_ready")
        val_used = sem("cm_val_used")
        vare_ready = sem("cm_vare_ready")
        rs_ready = sem("cm_rs_ready")
        junk_done = sem("cm_junk_done")
        normed = sem("cm_normed")
        dve_step = sem("cm_dve_step")

        block = ctx.enter_context(nc.Block())
        plan = schedule(NC, (5, 4, 3, 2, 1, 0))

        @block.sync
        def _(sp):
            sp.dma_start(w_k[:, :], a.W_key2).then_inc(w_in, 16)
            sp.dma_start(w_v[:, :, :], a.W_value2.rearrange("(k p) c -> p k c", p=P)).then_inc(w_in, 16)
            sp.dma_start(w_r[:, :], a.W_recept2).then_inc(w_in, 16)

        @block.gpsimd
        def _(pool):
            for c, phase in plan:
                if phase == 0:
                    t = slice(c * TPC, (c + 1) * TPC)
                    pool.wait_ge(ms_ready, c + 1)
                    nc.gpsimd.tensor_tensor(rstd[:, t], ms[:, t], g.minus_half[:, 0:TPC], ALU.pow).then_inc(rstd_ready, 1)
                    scale_raw(nc, pool, g, NC + c)
                if phase == 4:
                    pool.wait_ge(vare_ready, c + 1)
                    nc.gpsimd.tensor_tensor(rs[:, c % 2, :], vare[:, c % 2, :], g.minus_half[:, 0:TPC], ALU.pow).then_inc(rs_ready, 1)
            scale_raw(nc, pool, g, E)

        @block.scalar
        def _(act):
            for c, phase in plan:
                if phase == 0:
                    for i in range(TPC):
                        t = c * TPC + i
                        nc.scalar.activation(junk[:, :], g.x1[:, t, :], ACT.Square, accum_out=ss[:, t:t + 1]).then_inc(ss_ready, 1)
                        act.wait_ge(ss_ready, t + 1)
                if phase == 1:
                    high_part(nc, act, g, NC + c)
                if phase == 2:
                    act.wait_ge(turned, c + 1)
                    nc.scalar.activation(shifted(hT, c)[0], tr_bank(c), ACT.Copy,
                                         scale=g.cols[:, LN2:LN2 + 1]).then_inc(hT_ready, 1)
                if phase == 3:
                    for k in range(HC):
                        n = c * HC + k
                        act.wait_ge(key_ready, n + 1)
                        if n >= 2:
                            act.wait_ge(sq_ready, n - 1)
                        nc.scalar.activation(relu[:, n % 2, :], key_bank(n), ACT.Relu).then_inc(relu_ready, 1)
                    act.wait_ge(r_ready, c + 1)
                    if c >= 2:
                        act.wait_ge(val_used, c - 1)
                    nc.scalar.activation(th[:, c % 2, :], r_ps, ACT.Tanh, scale=0.5).then_inc(th_ready, 1)

        @block.vector
        def _(dve):
            link = chain(dve, dve_step)
            nc.vector.memset(hT[:, :, 0:1], 0.0).then_inc(zero_ready, 1)
            dve.wait_ge(zero_ready, 1)
            for c, phase in plan:
                h, sh = shifted(hT, c)
                rows = slice(c * TPC, (c + 1) * TPC)
                if phase == 0:
                    dve.wait_ge(ss_ready, TPC * (c + 1))
                    nc.vector.tensor_scalar(ms[:, rows], ss[:, rows], 1.0 / C, RMS_EPS, ALU.mult, ALU.add).then_inc(ms_ready, 1)
                if phase == 1:
                    dve.wait_ge(rstd_ready, c + 1)
                    if c >= 2:
                        dve.wait_ge(turned, c - 1)
                    for i in range(TPC):
                        t = c * TPC + i
                        last = nc.vector.tensor_scalar(hx[:, c % 2, i, :], g.x1[:, t, :], rstd[:, t:t + 1], None, ALU.mult)
                    last.then_inc(hx_ready, 1)
                if phase == 2:
                    dve.wait_ge(hT_ready, c + 1)
                    if c >= 2:
                        dve.wait_ge(r_ready, c - 1)
                    link(nc.vector.tensor_tensor(diff[:, :], h, sh, ALU.subtract))
                    for i, m in enumerate((MIXK2, MIXR2)):
                        last = nc.vector.scalar_tensor_tensor(out=xm[:, c % 2, i, :], in0=diff[:, :], scalar=g.cols[:, m:m + 1],
                                                              in1=sh, op0=ALU.mult, op1=ALU.add)
                    last.then_inc(xm_ready, 1)
                    dve.wait_ge(xm_ready, c + 1)
                if phase == 3:
                    if c >= 2:
                        dve.wait_ge(val_ready, c - 1)
                    for k in range(HC):
                        n = c * HC + k
                        dve.wait_ge(relu_ready, n + 1)
                        nc.vector.tensor_tensor(sq[:, c % 2, k, :], relu[:, n % 2, :], relu[:, n % 2, :], ALU.mult).then_inc(sq_ready, 1)
                if phase == 4:
                    zc = z[:, c % 2, :]
                    dve.wait_ge(th_ready, c + 1)
                    dve.wait_ge(val_ready, c + 1)
                    nc.vector.scalar_tensor_tensor(out=zc, in0=th[:, c % 2, :], scalar=1.0, in1=val_bank(c),
                                                   op0=ALU.add, op1=ALU.mult).then_inc(val_used, 1)
                    dve.wait_ge(val_used, c + 1)
                    link(nc.vector.scalar_tensor_tensor(out=zc, in0=zc, scalar=0.5, in1=g.x1[:, rows, :].rearrange("p t c -> p (t c)"),
                                                        op0=ALU.mult, op1=ALU.add))
                    link(nc.vector.tensor_tensor(zc, zc, g.x0[:, rows, :].rearrange("p t c -> p (t c)"), ALU.add))
                    for i in range(TPC):
                        last = nc.vector.bn_stats(stats[:, i, :], zc[:, i * C:(i + 1) * C])
                    link(last)
                    for i in range(TPC):
                        last = nc.vector.bn_aggr(mv[:, c % 2, i, :], stats[:, i, :])
                    link(last)
                    if c >= 2:
                        dve.wait_ge(rs_ready, c - 1)
                    nc.vector.tensor_scalar(vare[:, c % 2, :], mv[:, c % 2, :, 1], LN_EPS, None, ALU.add).then_inc(vare_ready, 1)
                if phase == 5:
                    dve.wait_ge(rs_ready, c + 1)
                    for i in range(TPC):
                        last = nc.vector.tensor_scalar(g.x0[:, c * TPC + i, :], z[:, c % 2, i * C:(i + 1) * C],
                                                       mv[:, c % 2, i, 0:1], rs[:, c % 2, i:i + 1], ALU.subtract, ALU.mult)
                    last.then_inc(normed, 1)
                    dve.wait_ge(normed, c + 1)

        @block.tensor
        def _(pe):
            for c, phase in plan:
                if phase == 1:
                    pe.wait_ge(hx_ready, c + 1)
                    if c >= 2:
                        pe.wait_ge(hT_ready, c - 1)
                    for i in range(TPC):
                        last = nc.tensor.transpose(tr_bank(c)[:, i * P:(i + 1) * P], hx[:, c % 2, i, :], g.ident[:, :])
                    last.then_inc(turned, 1)
                if phase == 2:
                    if c == 0:
                        pe.wait_ge(w_in, 48)
                    pe.wait_ge(xm_ready, c + 1)
                    for k in range(HC):
                        n = c * HC + k
                        if n >= 2:
                            pe.wait_ge(relu_ready, n - 1)
                        nc.tensor.matmul(key_bank(n), w_k[:, k * P:(k + 1) * P], xm[:, c % 2, 0, :],
                                         start=True, stop=True).then_inc(key_ready, 1)
                    if c >= 1:
                        pe.wait_ge(th_ready, c)
                    for i in range(TPC):
                        last = nc.tensor.matmul(r_ps[:, i * P:(i + 1) * P], xm[:, c % 2, 1, i * P:(i + 1) * P], w_r[:, :],
                                                start=True, stop=True)
                    last.then_inc(r_ready, 1)
                if phase == 3:
                    if c >= 2:
                        pe.wait_ge(val_used, c - 1)
                    pe.wait_ge(sq_ready, HC * (c + 1))
                    for i in range(TPC):
                        for k in range(HC):
                            last = nc.tensor.matmul(val_bank(c)[:, i * P:(i + 1) * P], sq[:, c % 2, k, i * P:(i + 1) * P],
                                                    w_v[:, k, :], start=(k == 0), stop=(k == HC - 1))
                    last.then_inc(val_ready, 1)


def route(nc, g, a):
    with ExitStack() as ctx:
        def sb(name, shape, dt=F32):
            return ctx.enter_context(nc.sbuf_tensor(name, shape, dt))

        def sem(name):
            return ctx.enter_context(nc.semaphore(name))

        xT = sb("xT", [P, N])
        w_g = sb("w_g", [P, E])
        b2 = sb("b2", [E, C])
        logit = sb("logit", [P, NT, E])
        rest = sb("rest", [P, NT, E])
        rank = sb("rank", [P, NT, E])
        tied = sb("tied", [P, NT, E])
        top = sb("top", [P, TOPK, NT])
        topr = sb("topr", [P, NT])
        onehot = sb("onehot", [P, E, TOPK, NT])
        keep = sb("keep", [P, E, TOPK, NT])
        upper = sb("upper", [P, P])
        ones = sb("ones", [P, P])
        resets = sb("resets", [P, E, TOPK * NT])
        upto = sb("upto", [P, E, TOPK, NT])
        gap = sb("gap", [P, NT])
        egap = sb("egap", [P, NT])
        esum = sb("esum", [P, NT])
        wk = sb("wk", [P, TOPK, NT])
        gT = sb("gT", [E, N])
        pb = g.pb
        tr_bank = lambda c: pb[:, c % 2, :]
        logit_ps = pb[:, 2, 0:NT * E].rearrange("p (t e) -> p t e", e=E)
        within_ps = pb[:, 3, 0:E * TOPK * NT]
        total_ps = pb[:, 3, 256:256 + E * TOPK * NT]
        bias_bank = lambda c: pb[:, 4 + c % 2, :]

        w_in = sem("ro_w_in")
        turned = sem("ro_turned")
        xT_ready = sem("ro_xT_ready")
        xh_ready = sem("ro_xh_ready")
        logit_ready = sem("ro_logit_ready")
        consts_ready = sem("ro_consts_ready")
        onehot_ready = sem("ro_onehot_ready")
        counts_ready = sem("ro_counts_ready")
        gap_ready = sem("ro_gap_ready")
        egap_ready = sem("ro_egap_ready")
        gate_ready = sem("ro_gate_ready")
        gate_turned = sem("ro_gate_turned")
        gT_ready = sem("ro_gT_ready")
        bias_ready = sem("ro_bias_ready")
        bias_used = sem("ro_bias_used")
        xl_ready = sem("ro_xl_ready")
        dve_step = sem("ro_dve_step")

        block = ctx.enter_context(nc.Block())

        @block.sync
        def _(sp):
            sp.dma_start(w_g[:, :], a.wg).then_inc(w_in, 16)
            sp.dma_start(b2[:, :], a.b2).then_inc(w_in, 16)

        @block.gpsimd
        def _(pool):
            nc.gpsimd.memset(upper[:, :], 1.0).then_inc(consts_ready, 1)
            nc.gpsimd.memset(ones[:, :], 1.0).then_inc(consts_ready, 1)
            nc.gpsimd.memset(resets[:, :, :], 1.0).then_inc(consts_ready, 1)
            nc.gpsimd.iota(rank[:, :, :], pattern=[[0, NT], [-1, E]], base=E, channel_multiplier=0,
                           allow_small_or_imprecise_dtypes=True).then_inc(consts_ready, 1)
            pool.wait_ge(consts_ready, 4)
            nc.gpsimd.affine_select(out=upper[:, :], in_=upper[:, :], compare_op=ALU.is_ge, fill=0.0,
                                    base=0, pattern=[[1, P]], channel_multiplier=-1).then_inc(consts_ready, 1)
            nc.gpsimd.memset(resets[:, :, 0:1], 0.0).then_inc(consts_ready, 1)

        @block.scalar
        def _(act):
            for c in range(NC):
                cols = slice(c * CH, (c + 1) * CH)
                act.wait_ge(turned, c + 1)
                nc.scalar.activation(xT[:, cols], tr_bank(c), ACT.Copy).then_inc(xT_ready, 1)
                nc.scalar.activation(g.xh[:, cols], tr_bank(c), ACT.Copy).then_inc(xh_ready, 1)
            act.wait_ge(gap_ready, 1)
            nc.scalar.activation(egap[:, :], gap[:, :], ACT.Exp).then_inc(egap_ready, 1)
            for c in range(NC):
                act.wait_ge(gate_turned, c + 1)
                nc.scalar.activation(gT[:, c * CH:(c + 1) * CH], tr_bank(c)[0:E, :], ACT.Copy).then_inc(gT_ready, 1)

        @block.vector
        def _(dve):
            link = chain(dve, dve_step)
            dve.wait_ge(consts_ready, 6)
            dve.wait_ge(logit_ready, 1)
            link(nc.vector.tensor_copy(logit[:, :, :], logit_ps))
            src = logit
            for k in range(TOPK):
                oh = onehot[:, :, k, :].rearrange("p e t -> p t e")
                link(nc.vector.tensor_reduce(top[:, k, :], src[:, :, :], AX.X, ALU.max))
                link(nc.vector.tensor_tensor(tied[:, :, :], src[:, :, :], top[:, k, :].rearrange("p (t o) -> p t o", o=1)
                                             .broadcast_to([P, NT, E]), ALU.is_equal))
                link(nc.vector.tensor_tensor(tied[:, :, :], tied[:, :, :], rank[:, :, :], ALU.mult))
                link(nc.vector.tensor_reduce(topr[:, :], tied[:, :, :], AX.X, ALU.max))
                link(nc.vector.tensor_tensor(oh, tied[:, :, :], topr[:, :].rearrange("p (t o) -> p t o", o=1)
                                             .broadcast_to([P, NT, E]), ALU.is_equal))
                if k == 0:
                    link(nc.vector.scalar_tensor_tensor(out=rest[:, :, :], in0=oh, scalar=-3e38, in1=logit[:, :, :],
                                                        op0=ALU.mult, op1=ALU.add))
                    src = rest
            nc.vector.tensor_tensor(gap[:, :], top[:, 1, :], top[:, 0, :], ALU.subtract).then_inc(gap_ready, 1)
            dve.sem_inc(onehot_ready, 1)
            dve.wait_ge(counts_ready, 1)
            flat = lambda buf: buf[:, :, :, :].rearrange("p e k t -> p (e k t)")
            link(nc.vector.tensor_tensor_scan(flat(upto), resets[:, :, :].rearrange("p e n -> p (e n)"), total_ps, 0.0,
                                              ALU.mult, ALU.add))
            link(nc.vector.tensor_tensor(flat(upto), flat(upto), total_ps, ALU.subtract))
            link(nc.vector.tensor_tensor(flat(upto), flat(upto), within_ps, ALU.add))
            link(nc.vector.scalar_tensor_tensor(out=flat(keep), in0=flat(upto), scalar=float(CAP), in1=flat(onehot),
                                                op0=ALU.is_le, op1=ALU.mult))
            dve.wait_ge(egap_ready, 1)
            link(nc.vector.tensor_scalar(esum[:, :], egap[:, :], 1.0, None, ALU.add))
            link(nc.vector.reciprocal(wk[:, 0, :], esum[:, :]))
            link(nc.vector.tensor_tensor(wk[:, 1, :], egap[:, :], wk[:, 0, :], ALU.mult))
            for k in range(TOPK):
                last = nc.vector.tensor_tensor(keep[:, :, k, :], keep[:, :, k, :],
                                               wk[:, k, :].rearrange("p (o t) -> p o t", o=1).broadcast_to([P, E, NT]), ALU.mult)
            link(last)
            nc.vector.tensor_tensor(g.gate[:, :, :], keep[:, :, 0, :], keep[:, :, 1, :], ALU.add).then_inc(gate_ready, 1)
            dve.wait_ge(gate_ready, 1)
            link(nc.vector.tensor_scalar(g.gate_down[:, :, :], g.gate[:, :, :], 1.0 / W_SCALE, None, ALU.mult))
            for c in range(NC):
                cols = slice(c * CH, (c + 1) * CH)
                dve.wait_ge(xh_ready, c + 1)
                nc.vector.tensor_tensor(g.xl[:, cols], xT[:, cols], g.xh[:, cols], ALU.subtract).then_inc(xl_ready, 1)
            for c in range(NC):
                rows = slice(c * TPC, (c + 1) * TPC)
                dve.wait_ge(bias_ready, c + 1)
                nc.vector.tensor_tensor(g.moe[:, rows, :].rearrange("p t c -> p (t c)"), bias_bank(c),
                                        g.x0[:, rows, :].rearrange("p t c -> p (t c)"), ALU.add).then_inc(bias_used, 1)

        @block.tensor
        def _(pe):
            for c in range(NC):
                if c >= 2:
                    pe.wait_ge(xh_ready, c - 1)
                for i in range(TPC):
                    last = nc.tensor.transpose(tr_bank(c)[:, i * P:(i + 1) * P], g.x0[:, c * TPC + i, :], g.ident[:, :])
                last.then_inc(turned, 1)
            pe.wait_ge(w_in, 32)
            for t in range(NT):
                pe.wait_ge(xT_ready, t // TPC + 1)
                last = nc.tensor.matmul(logit_ps[:, t, :], xT[:, t * P:(t + 1) * P], w_g[:, :], start=True, stop=True)
            last.then_inc(logit_ready, 1)
            pe.wait_ge(consts_ready, 6)
            pe.wait_ge(onehot_ready, 1)
            oh = onehot[:, :, :, :].rearrange("p e k t -> p (e k t)")
            nc.tensor.matmul(within_ps, upper[:, :], oh, start=True, stop=True)
            nc.tensor.matmul(total_ps, ones[:, :], oh, start=True, stop=True).then_inc(counts_ready, 1)
            pe.wait_ge(gate_ready, 1)
            pe.wait_ge(xh_ready, NC)
            for c in range(NC):
                if c >= 2:
                    pe.wait_ge(gT_ready, c - 1)
                for i in range(TPC):
                    last = nc.tensor.transpose(tr_bank(c)[0:E, i * P:(i + 1) * P], g.gate[:, :, c * TPC + i], g.ident[:, :])
                last.then_inc(gate_turned, 1)
            for c in range(NC):
                pe.wait_ge(gT_ready, c + 1)
                if c >= 2:
                    pe.wait_ge(bias_used, c - 1)
                for i in range(TPC):
                    t = c * TPC + i
                    last = nc.tensor.matmul(bias_bank(c)[:, i * P:(i + 1) * P], gT[:, t * P:(t + 1) * P], b2[:, :],
                                            start=True, stop=True)
                last.then_inc(bias_ready, 1)


def experts(nc, g, a):
    with ExitStack() as ctx:
        def sb(name, shape, dt=F32):
            return ctx.enter_context(nc.sbuf_tensor(name, shape, dt))

        def sem(name):
            return ctx.enter_context(nc.semaphore(name))

        RING = 4
        h32 = sb("h32", [P, RING, CH])
        hh = sb("hh", [P, 2, HC, CH], F16)
        b1_now = sb("b1_now", [P, HC])
        hl = sb("hl", [P, 2, HC, CH], F16)
        pb = g.pb
        hid_bank = lambda n: pb[:, n % RING, :]
        out_bank = lambda c: pb[:, 4 + c % 2, :]
        hid_ready = sem("ex_hid_ready")
        h32_ready = sem("ex_h32_ready")
        b1_ready = sem("ex_b1_ready")
        hh_ready = sem("ex_hh_ready")
        hl_ready = sem("ex_hl_ready")
        out_ready = sem("ex_out_ready")
        out_used = sem("ex_out_used")

        block = ctx.enter_context(nc.Block())

        def chunks(step, e, final):
            for c in range(NC):
                if c < NC - 1:
                    step(0, e, c + 1)
                elif not final:
                    step(0, e + 1, 0)
                step(1, e, c)

        def every_expert(eng, step):
            step(0, 0, 0)
            with eng.Fori(0, E - 1) as e:
                chunks(step, e, False)
            chunks(step, E - 1, True)

        @block.tensor
        def _(pe):
            def step(layer, e, c):
                q = e * NC + c
                if layer == 0:
                    x = slice(c * CH, (c + 1) * CH)
                    for k in range(HC):
                        pe.wait_ge(hh_ready, q * HC + k + 1)
                        w = slice(k * P, (k + 1) * P)
                        for i, (lhs, rhs) in enumerate(((g.w0h, g.xh), (g.w0h, g.xl), (g.w0l, g.xh))):
                            last = nc.tensor.matmul(hid_bank(k), lhs[:, bass.ds(e, 1), w], rhs[:, x], start=(i == 0), stop=(i == 2))
                        last.then_inc(hid_ready, 1)
                else:
                    pe.wait_ge(hl_ready, q * HC + (RING + HC))
                    pe.wait_ge(out_used, q + 1)
                    for i in range(TPC):
                        tok = slice(i * P, (i + 1) * P)
                        for k in range(HC):
                            w2 = slice(H + k * P, H + (k + 1) * P)
                            for j, (lhs, rhs) in enumerate(((hh, g.w0h), (hh, g.w0l), (hl, g.w0h))):
                                last = nc.tensor.matmul(out_bank(c)[:, tok], lhs[:, c % 2, k, tok], rhs[:, bass.ds(e, 1), w2],
                                                        start=(k == 0 and j == 0), stop=(k == HC - 1 and j == 2))
                    last.then_inc(out_ready, 1)

            pe.sem_inc(out_ready, 2)
            every_expert(pe, step)

        @block.scalar
        def _(act):
            def step(layer, e, c):
                if layer == 0:
                    q = e * NC + c
                    act.wait_ge(b1_ready, e + 1)
                    act.wait_ge(out_ready, q + 1)
                    for k in range(HC):
                        n = q * HC + k
                        b1 = b1_now[:, k:k + 1]
                        act.wait_ge(hid_ready, n + 1)
                        act.wait_ge(hl_ready, n + 1)
                        nc.scalar.activation(h32[:, k, :], hid_bank(k), ACT.Relu, scale=1.0 / W_SCALE, bias=b1).then_inc(h32_ready, 1)
                        nc.scalar.activation(hh[:, c % 2, k, :], hid_bank(k), ACT.Relu, scale=1.0 / W_SCALE,
                                             bias=b1).then_inc(hh_ready, 1)

            act.sem_inc(hh_ready, RING)
            every_expert(act, step)

        @block.vector
        def _(dve):
            def step(layer, e, c):
                q = e * NC + c
                if layer == 0:
                    if c == 0:
                        dve.wait_ge(hh_ready, q * HC + RING)
                        nc.vector.tensor_scalar(b1_now[:, :], g.cols[:, bass.ds(e * HC + B1, HC)], 1.0, None, ALU.mult).then_inc(b1_ready, 1)
                    for k in range(HC):
                        dve.wait_ge(hh_ready, q * HC + (k + 1 + RING))
                        nc.vector.tensor_tensor(hl[:, c % 2, k, :], h32[:, k, :], hh[:, c % 2, k, :], ALU.subtract).then_inc(hl_ready, 1)
                else:
                    dve.wait_ge(out_ready, q + 3)
                    for i in range(TPC):
                        t = c * TPC + i
                        last = nc.vector.scalar_tensor_tensor(
                            out=g.moe[:, t, :], in0=out_bank(c)[:, i * C:(i + 1) * C], scalar=g.gate_down_flat[:, bass.ds(e * NT + t, 1)],
                            in1=g.moe[:, t, :], op0=ALU.mult, op1=ALU.add)
                    last.then_inc(out_used, 1)

            dve.sem_inc(hl_ready, RING)
            dve.sem_inc(out_used, 2)
            every_expert(dve, step)


def project(nc, g, a, m, ctx):
    stage = Shared()

    def sb(name, shape, dt=F32):
        return ctx.enter_context(nc.sbuf_tensor(name, shape, dt))

    def sem(name):
        return ctx.enter_context(nc.semaphore(name))

    NB = 2 * C + HASH
    w_raw, w_T = m.w_raw, m.w_T
    brow = sb("pj_brow", [1, NB])
    one_row = sb("pj_one_row", [1, P])
    ones = sb("pj_ones", [P, P])
    bcast = sb("pj_bcast", [P, NB])
    stats = sb("pj_stats", [P, TPC, 6])
    mv = sb("pj_mv", [P, 2, TPC, 2])
    vare = sb("pj_vare", [P, 2, TPC])
    rs = sb("pj_rs", [P, 2, TPC])
    xT = m.xT_project
    prod = g.x1[:, :, :].rearrange("p t c -> p (t c)")
    half = sb("pj_half", [P, NG * HPG])
    nsq = sb("pj_nsq", [P, NG, GT, HPG])
    qa = sb("pj_qa", [P, NG, GT, HPG])
    tmp = sb("pj_tmp", [P, NG, GT, HPG])
    nsq2 = sb("pj_nsq2", [P, NG, GT, HPG])
    pk = sb("pj_pk", [P, NG, GT, HPG])
    hq = sb("pj_hq", [P, NG, GT, HPG])
    hk = sb("pj_hk", [P, NG, GT, HPG])
    mx = sb("pj_mx", [P, NG, HPG])
    mxall = sb("pj_mxall", [P, NG, HPG])
    sc = sb("pj_sc", [P, 3, NG, HPG])
    longest = sb("pj_longest", [P, 1])
    n1 = sb("pj_n1", [P, NG, HPG])
    none = sb("pj_none", [P, 3, NG, HPG])
    pb = g.pb
    tr_bank = lambda c: pb[:, c % 2, :]
    qkv_ps = lambda c: pb[:, 2 + 2 * (c % 2):4 + 2 * (c % 2), :].rearrange("p a n -> p (a n)").rearrange("p (t m) -> p t m", m=2 * C)

    w_in = sem("pj_w_in")
    brow_in = sem("pj_brow_in")
    ones_ready = sem("pj_ones_ready")
    w_turned = sem("pj_w_turned")
    bcast_done = sem("pj_bcast_done")
    consts_ready = sem("pj_consts_ready")
    vare_ready = sem("pj_vare_ready")
    rs_ready = sem("pj_rs_ready")
    x_ready = sem("pj_x_ready")
    turned = sem("pj_turned")
    xT_ready = sem("pj_xT_ready")
    qkv_ready = sem("pj_qkv_ready")
    qkv_used = sem("pj_qkv_used")
    mx_ready = sem("pj_mx_ready")
    mxall_ready = sem("pj_mxall_ready")
    s2_ready = sem("pj_s2_ready")
    s_ready = sem("pj_s_ready")
    hk_ready = sem("pj_hk_ready")
    counts_ready = sem("pj_counts_ready")
    dve_step = sem("pj_dve_step")

    plan = schedule(NC, (3, 2, 1, 0))

    def sync(sp):
        sp.dma_start(w_raw[:, 0, :], a.qk_w).then_inc(w_in, 16)
        sp.dma_start(w_raw[:, 1, :], a.v_w).then_inc(w_in, 16)
        for lo, v in ((0, a.qk_b), (C, a.v_b), (2 * C, a.hash_a)):
            sp.dma_start(brow[:, lo:lo + v.shape[0]], v.rearrange("(a n) -> a n", a=1)).then_inc(brow_in, 16)

    def gpsimd(pool):
        nc.gpsimd.memset(one_row[:, :], 1.0).then_inc(ones_ready, 1)
        nc.gpsimd.memset(ones[:, :], 1.0).then_inc(ones_ready, 1)
        nc.gpsimd.memset(half[:, :], 0.5).then_inc(ones_ready, 1)
        pool.wait_ge(ones_ready, 3)
        for c, phase in plan:
            if phase == 0:
                pool.wait_ge(vare_ready, c + 1)
                nc.gpsimd.tensor_tensor(rs[:, c % 2, :], vare[:, c % 2, :], g.minus_half[:, 0:TPC], ALU.pow).then_inc(rs_ready, 1)
        heads = lambda buf: buf.rearrange("p g h -> p (g h)")
        clear_sides(nc, pool, m)
        pool.wait_ge(mx_ready, 1)
        nc.gpsimd.partition_all_reduce(heads(mxall[:, :, :]), heads(mx[:, :, :]), P,
                                       bass.bass_isa.ReduceOp.max).then_inc(mxall_ready, 1)
        pool.wait_ge(s2_ready, 1)
        nc.gpsimd.tensor_tensor(heads(sc[:, 0, :, :]), heads(sc[:, 1, :, :]), half[:, :], ALU.pow).then_inc(s_ready, 1)

    def scalar(act):
        for c, phase in plan:
            if phase == 2:
                act.wait_ge(turned, c + 1)
                if c >= 2:
                    act.wait_ge(qkv_ready, c - 1)
                nc.scalar.activation(xT[:, c % 2, :], tr_bank(c), ACT.Copy).then_inc(xT_ready, 1)

    def vector(dve):
        link = chain(dve, dve_step)
        for c, phase in plan:
            rows = slice(c * TPC, (c + 1) * TPC)
            if phase == 0:
                for i in range(TPC):
                    last = nc.vector.bn_stats(stats[:, i, :], g.moe[:, c * TPC + i, :])
                link(last)
                for i in range(TPC):
                    last = nc.vector.bn_aggr(mv[:, c % 2, i, :], stats[:, i, :])
                link(last)
                nc.vector.tensor_scalar(vare[:, c % 2, :], mv[:, c % 2, :, 1], LN_EPS, None, ALU.add).then_inc(vare_ready, 1)
            if phase == 1:
                dve.wait_ge(rs_ready, c + 1)
                for i in range(TPC):
                    t = c * TPC + i
                    last = nc.vector.tensor_scalar(g.x0[:, t, :], g.moe[:, t, :], mv[:, c % 2, i, 0:1], rs[:, c % 2, i:i + 1],
                                                   ALU.subtract, ALU.mult)
                last.then_inc(x_ready, 1)
                dve.wait_ge(x_ready, c + 1)
                if c == 0:
                    dve.wait_ge(w_turned, 1)
                    nc.vector.tensor_copy(w_T[:, :], pb[:, 6, 0:2 * C]).then_inc(consts_ready, 1)
                    dve.wait_ge(bcast_done, 1)
                    nc.vector.tensor_copy(bcast[:, :], pb[:, 7, 0:NB]).then_inc(consts_ready, 1)
                    dve.wait_ge(consts_ready, 2)
            if phase == 3:
                b, t0 = c // CPB, (c % CPB) * TPC
                dve.wait_ge(qkv_ready, c + 1)
                for i in range(TPC):
                    for j, dst in enumerate((g.q, g.v)):
                        last = nc.vector.tensor_tensor(
                            dst[:, b * HG:(b + 1) * HG, t0 + i, :, :].rearrange("p g h d -> p g (h d)"),
                            qkv_ps(c)[:, i, j * C:(j + 1) * C].rearrange("p (g n) -> p g n", g=HG),
                            bcast[:, j * C:(j + 1) * C].rearrange("p (g n) -> p g n", g=HG), ALU.add)
                last.then_inc(qkv_used, 1)
        dve.wait_ge(qkv_used, NC)
        every = lambda buf: buf[:, :, :, :].rearrange("p g t h -> p (g t h)")
        rowsof = lambda buf: buf[:, :, :, :, :].rearrange("p g t h d -> p (g t h) d")
        per_head = lambda buf: buf.rearrange("p g (o h) -> p g o h", o=1).broadcast_to([P, NG, GT, HPG])
        link(nc.vector.tensor_tensor(prod.rearrange("p (n d) -> p n d", d=DH), rowsof(g.q), rowsof(g.q), ALU.mult))
        link(nc.vector.tensor_reduce(every(nsq), prod.rearrange("p (n d) -> p n d", d=DH), AX.X, ALU.add))
        nc.vector.tensor_reduce(mx[:, :, :], nsq[:, :, :, :].rearrange("p g t h -> p g h t"), AX.X, ALU.max).then_inc(mx_ready, 1)
        link(nc.vector.tensor_tensor(prod.rearrange("p (n d) -> p n d", d=DH), rowsof(g.q), bcast[:, 2 * C:2 * C + DH].rearrange("p (o d) -> p o d", o=1)
                                     .broadcast_to([P, NG * GT * HPG, DH]), ALU.mult))
        link(nc.vector.tensor_reduce(every(qa), prod.rearrange("p (n d) -> p n d", d=DH), AX.X, ALU.add))
        dve.wait_ge(mxall_ready, 1)
        link(nc.vector.tensor_scalar(sc[:, 0, :, :], mxall[:, :, :], 1e-24, None, ALU.max))
        link(nc.vector.reciprocal(sc[:, 2, :, :], sc[:, 0, :, :]))
        nc.vector.tensor_scalar(sc[:, 1, :, :], sc[:, 2, :, :], U_HASH ** 2, None, ALU.mult).then_inc(s2_ready, 1)
        link(nc.vector.tensor_reduce(longest[:, :], mxall[:, :, :].rearrange("p g h -> p (g h)"), AX.X, ALU.max))
        nc.vector.tensor_scalar(g.large[:, :], longest[:, :], SAFE_SCORE * DH ** 0.5, None, ALU.is_gt).then_inc(m.large_ready, 1)
        link(nc.vector.tensor_scalar(every(hq), every(qa), 0.0, None, ALU.is_ge))
        link(nc.vector.tensor_scalar(every(g.qbit), every(hq), 2.0, -1.0, ALU.mult, ALU.add))
        dve.wait_ge(s2_ready, 1)
        link(nc.vector.tensor_tensor(nsq2[:, :, :, :], nsq[:, :, :, :], per_head(sc[:, 1, :, :]), ALU.mult))
        link(nc.vector.tensor_tensor(every(tmp), every(nsq2), every(nsq2), ALU.mult))
        for i, part in enumerate((nsq2, tmp)):
            link(nc.vector.tensor_scalar(every(part), every(part), -1.0, 0.5, ALU.mult, ALU.add))
            link(nc.vector.tensor_scalar(every(part), every(part), bcast[:, 2 * C + DH + i:2 * C + DH + i + 1], None, ALU.mult))
        link(nc.vector.tensor_tensor(every(tmp), every(tmp), every(nsq2), ALU.add))
        dve.wait_ge(s_ready, 1)
        link(nc.vector.tensor_tensor(pk[:, :, :, :], qa[:, :, :, :], per_head(sc[:, 0, :, :]), ALU.mult))
        link(nc.vector.tensor_tensor(every(pk), every(pk), every(tmp), ALU.add))
        nc.vector.tensor_scalar(every(hk), every(pk), 0.0, None, ALU.is_ge).then_inc(hk_ready, 1)
        dve.wait_ge(hk_ready, 1)
        link(nc.vector.tensor_scalar(every(g.kbit), every(hk), MASK, -MASK / 2, ALU.mult, ALU.add))
        dve.wait_ge(counts_ready, 1)
        link(nc.vector.tensor_reduce(n1[:, :, :], pb[:, 5, 0:NG * GT * HPG].rearrange("p (g t h) -> p g h t", g=NG, t=GT), AX.X, ALU.add))
        link(nc.vector.tensor_scalar(none[:, 0, :, :], n1[:, :, :], 0.0, MASK, ALU.is_equal, ALU.mult))
        link(nc.vector.tensor_scalar(none[:, 1, :, :], n1[:, :, :], float(T), MASK, ALU.is_equal, ALU.mult))
        link(nc.vector.tensor_tensor(none[:, 2, :, :], none[:, 0, :, :], none[:, 1, :, :], ALU.subtract))
        link(nc.vector.tensor_tensor(tmp[:, :, :, :], hq[:, :, :, :], per_head(none[:, 2, :, :]), ALU.mult))
        link(nc.vector.tensor_tensor(g.lift[:, :, :, :], tmp[:, :, :, :], per_head(none[:, 1, :, :]), ALU.add))

    def tensor(pe):
        pe.wait_ge(w_in, 32)
        nc.tensor.transpose(pb[:, 6, 0:C], w_raw[:, 0, :], g.ident[:, :])
        nc.tensor.transpose(pb[:, 6, C:2 * C], w_raw[:, 1, :], g.ident[:, :]).then_inc(w_turned, 1)
        pe.wait_ge(ones_ready, 3)
        pe.wait_ge(brow_in, 48)
        nc.tensor.matmul(pb[:, 7, 0:NB], one_row[:, :], brow[:, :], start=True, stop=True).then_inc(bcast_done, 1)
        for c, phase in plan:
            if phase == 1:
                pe.wait_ge(x_ready, c + 1)
                if c >= 2:
                    pe.wait_ge(xT_ready, c - 1)
                for i in range(TPC):
                    last = nc.tensor.transpose(tr_bank(c)[:, i * P:(i + 1) * P], g.x0[:, c * TPC + i, :], g.ident[:, :])
                last.then_inc(turned, 1)
            if phase == 2:
                pe.wait_ge(consts_ready, 2)
                pe.wait_ge(xT_ready, c + 1)
                if c >= 2:
                    pe.wait_ge(qkv_used, c - 1)
                for i in range(TPC):
                    last = nc.tensor.matmul(qkv_ps(c)[:, i, :], xT[:, c % 2, i * P:(i + 1) * P], w_T[:, :], start=True, stop=True)
                last.then_inc(qkv_ready, 1)
        pe.wait_ge(hk_ready, 1)
        nc.tensor.matmul(pb[:, 5, 0:NG * GT * HPG], ones[:, :], hk[:, :, :, :].rearrange("p g t h -> p (g t h)"),
                         start=True, stop=True).then_inc(counts_ready, 1)
    stage.sync = sync
    stage.gpsimd = gpsimd
    stage.scalar = scalar
    stage.vector = vector
    stage.tensor = tensor
    return stage



def one_group(buf, G):
    if len(buf.shape) == 5:
        return buf[:, bass.ds(G, 1), :, :, :].rearrange("p o t h d -> p (o t h) d")
    return buf[:, bass.ds(G, 1), :, :].rearrange("p o t (h d) -> p (o t h) d", d=1)


def side_rows(buf, lo, n):
    return buf[:, :, :, lo:lo + n].rearrange("p t h d -> p (t h) d")


def clear_sides(nc, pool, m):
    nc.gpsimd.memset(m.qs[:, :, :, :], 0.0).then_inc(m.cleared, 1)
    nc.gpsimd.memset(m.ks[:, :, :, :], 0.0).then_inc(m.cleared, 1)
    nc.gpsimd.memset(m.va[:, :, :, :, :], 0.0).then_inc(m.cleared, 1)
    pool.wait_ge(m.cleared, 3)
    nc.gpsimd.memset(m.qs[:, :, :, 0:1], 1.0).then_inc(m.cleared, 1)
    nc.gpsimd.memset(m.ks[:, :, :, 0:1], -MASK / 2).then_inc(m.cleared, 1)
    nc.gpsimd.memset(m.ks[:, :, :, 2:4], 1.0).then_inc(m.cleared, 1)
    nc.gpsimd.memset(m.va[:, :, :, :, DH:DH + 1], 1.0).then_inc(m.cleared, 1)


def write_sides(nc, dve, g, G, qs, ks, scaled, step, ready, with_lift):
    flat = scaled[:, :, :, :].rearrange("p t h d -> p (t h) d")
    nc.vector.tensor_copy(side_rows(ks, 1, 1), one_group(g.kbit, G))
    nc.vector.tensor_copy(side_rows(qs, 1, 1), one_group(g.qbit, G))
    nc.vector.tensor_scalar(flat, one_group(g.q, G), DH ** -0.5, None, ALU.mult)
    if with_lift:
        nc.vector.tensor_copy(side_rows(qs, 2, 1).bitcast(F32R), one_group(g.lift, G))
    nc.vector.tensor_copy(side_rows(ks, 4, DH).bitcast(F32R), one_group(g.q, G)).then_inc(step, 1)
    dve.wait_ge(step, 2 * G + 1)
    nc.vector.tensor_copy(side_rows(ks, 4 + DH, DH), side_rows(ks, 4, DH))
    nc.vector.tensor_tensor(side_rows(ks, 4 + 2 * DH, DH), one_group(g.q, G), side_rows(ks, 4, DH), ALU.subtract)
    if with_lift:
        nc.vector.tensor_tensor(side_rows(qs, 3, 1), one_group(g.lift, G), side_rows(qs, 2, 1), ALU.subtract)
    nc.vector.tensor_copy(side_rows(qs, 4, DH).bitcast(F32R), flat).then_inc(step, 1)
    dve.wait_ge(step, 2 * G + 2)
    nc.vector.tensor_tensor(side_rows(qs, 4 + DH, DH), flat, side_rows(qs, 4, DH), ALU.subtract)
    nc.vector.tensor_copy(side_rows(qs, 4 + 2 * DH, DH), side_rows(qs, 4, DH)).then_inc(ready, 1)


def maxima(nc, g, a, m, ctx):
    stage = Shared()

    def sb(name, shape, dt=F32):
        return ctx.enter_context(nc.sbuf_tensor(name, shape, dt))

    def sem(name):
        return ctx.enter_context(nc.semaphore(name))

    qs, ks, scaled = m.qs, m.ks, m.scaled
    qT, kT = m.qT[:, 0, :], m.kT[:, 0, :]
    peak = sb("mx_peak", [P, GT, HPG])
    pb = g.pb
    place = lambda i: pb[:, 2 * i:2 * i + 2, :].rearrange("p a n -> p (a n)")
    USES = GT * HPG

    step = sem("mx_step")
    sides_ready = sem("mx_sides_ready")
    turned = sem("mx_turned")
    taken = sem("mx_taken")
    s_ready = sem("mx_s_ready")
    peak_ready = sem("mx_peak_ready")
    lift_ready = sem("mx_lift_ready")

    def vector(dve):
        dve.wait_ge(m.cleared, 7)
        dve.wait_ge(m.large_ready, 1)
        large = dve.value_load(g.large[0:1, 0:1])
        with dve.If(large > 0):
            with dve.Fori(0, NG) as G:
                write_sides(nc, dve, g, G, qs, ks, scaled, step, sides_ready, False)
                dve.wait_ge(turned, 2 * G + 2)
                nc.vector.tensor_copy(qT, place(2))
                nc.vector.tensor_copy(kT, place(3)).then_inc(taken, 1)
                for t in range(GT):
                    for h in range(HPG):
                        n = t * HPG + h
                        dve.wait_ge(s_ready, G * USES + (n + 1))
                        nc.vector.tensor_reduce(peak[:, t, h:h + 1], place(n % 2), AX.X, ALU.max).then_inc(peak_ready, 1)
                dve.wait_ge(peak_ready, G * USES + USES)
                nc.vector.tensor_scalar(one_group(g.lift, G), peak[:, :, :].rearrange("p t (h d) -> p (t h) d", d=1),
                                        -1.0, None, ALU.mult).then_inc(lift_ready, 1)
                dve.wait_ge(lift_ready, G + 1)

    def tensor(pe):
        pe.wait_ge(m.large_ready, 1)
        large = pe.value_load(g.large[0:1, 0:1])
        with pe.If(large > 0):
            with pe.Fori(0, NG) as G:
                pe.wait_ge(sides_ready, G + 1)
                for i, side in enumerate((qs, ks)):
                    for t in range(GT):
                        last = nc.tensor.transpose(place(2 + i)[:, t * P:(t + 1) * P],
                                                   side[:, t, :, :].rearrange("p h r -> p (h r)"), g.ident[:, :])
                    last.then_inc(turned, 1)
                pe.wait_ge(taken, G + 1)
                for t in range(GT):
                    for h in range(HPG):
                        n = t * HPG + h
                        if n >= 2:
                            pe.wait_ge(peak_ready, G * USES + (n - 1))
                        part = slice(h * AUG, (h + 1) * AUG)
                        for half in range(2):
                            cols = slice(half * CH, (half + 1) * CH)
                            last = nc.tensor.matmul(place(n % 2)[:, cols], qT[part, t * P:(t + 1) * P], kT[part, cols],
                                                    start=True, stop=True)
                        last.then_inc(s_ready, 1)
    stage.vector = vector
    stage.tensor = tensor
    return stage



def attend(nc, g, a, m, ctx, following):
    stage = Shared()

    def sb(name, shape, dt=F32):
        return ctx.enter_context(nc.sbuf_tensor(name, shape, dt))

    def sem(name):
        return ctx.enter_context(nc.semaphore(name))

    qs, ks, scaled, qT, kT, va, ex = m.qs, m.ks, m.scaled, m.qT, m.kT, m.va, m.ex
    oT = m.oT
    rden = sb("at_rden", [P, GT, HPG])
    raw1 = sb("at_raw1", [P, 2, 3 * H])
    pb = g.pb
    ring = lambda pos: pb[:, 2 * (pos % 3):2 * (pos % 3) + 2, :].rearrange("p a n -> p (a n)")
    pv_ps = pb[:, 6:8, :].rearrange("p a n -> p (a n)")

    prep_ready = sem("at_prep_ready")
    q_turned = sem("at_q_turned")
    k_turned = sem("at_k_turned")
    qT_ready = sem("at_qT_ready")
    kT_ready = sem("at_kT_ready")
    s_ready = sem("at_s_ready")
    exp_done = sem("at_exp_done")
    pv_done = sem("at_pv_done")
    oT_ready = sem("at_oT_ready")
    o_turned = sem("at_o_turned")
    o_ready = sem("at_o_ready")
    raw1_in = [sem(f"at_raw1_in{i}") for i in range(2)]
    raw1_used = sem("at_raw1_used")
    prep_step = sem("at_prep_step")
    rden_ready = sem("at_rden_ready")
    high_ready = sem("at_high_ready")

    uses = [("S", n) for n in range(GT * HPG)]
    uses.insert(8, ("O", 0))
    uses.insert(25, ("Q", 0))
    uses.insert(26, ("K", 0))
    assert len(uses) == 35
    POS = {kind: pos for pos, (kind, n) in enumerate(uses) if kind != "S"}
    LEN = 36

    def place_free(eng, G, pos, first, last):
        back = pos - 3
        if back < 0:
            if first:
                return
            back += LEN
            G = G - 1
            if back == LEN - 1:
                back -= 3
        kind, n = uses[back]
        if kind == "S":
            eng.wait_ge(exp_done, G * (GT * HPG) + (n + 1))
        if kind == "O" and not first:
            eng.wait_ge(o_ready, G)
        if kind == "Q" and not last:
            eng.wait_ge(qT_ready, G + 2)
        if kind == "Q" and last:
            eng.wait_ge(following.xh_ready, 1)
        if kind == "K" and not last:
            eng.wait_ge(kT_ready, G + 2)

    def take_out(dve, G, turned_ps):
        out = turned_ps.rearrange("p (t h r) -> p t h r", t=GT, h=HPG)
        dve.wait_ge(o_turned, G + 1)
        nc.vector.reciprocal(rden[:, :, :].rearrange("p t (h o) -> p t h o", o=1), out[:, :, :, DH:DH + 1]).then_inc(rden_ready, 1)
        dve.wait_ge(rden_ready, G + 1)
        rows = lambda buf: buf.rearrange("p t h d -> p (t h) d")
        nc.vector.tensor_tensor(
            g.ctx[:, bass.ds(G, 1), :, :, :].rearrange("p o t h d -> p (o t h) d"),
            rows(out[:, :, :, 0:DH]),
            rden[:, :, :].rearrange("p t (h o) -> p (t h) o", o=1).broadcast_to([P, GT * HPG, DH]), ALU.mult).then_inc(o_ready, 1)

    def turn_out(pe, G, to):
        pe.wait_ge(oT_ready, G + 1)
        for t in range(GT):
            last = nc.tensor.transpose(to[:, t * P:(t + 1) * P], oT[:, t * P:(t + 1) * P], g.ident[:, :])
        last.then_inc(o_turned, 1)

    def groups(eng, group):
        group(0, 0, True, False)
        with eng.Fori(0, (NG - 2) // 2) as i:
            group(2 * i + 1, 1, False, False)
            group(2 * i + 2, 0, False, False)
        group(NG - 1, 1, False, True)

    def sync(sp):
        for e in range(E):
            if e >= 2:
                sp.wait_ge(raw1_used, e - 1)
            for i, src in enumerate((a.Wg[e], a.Wu[e])):
                sp.dma_start(raw1[:, e % 2, i * H:(i + 1) * H], src).then_inc(raw1_in[e % 2], 16)
            sp.dma_start(raw1[:, e % 2, 2 * H:3 * H].rearrange("p (k c) -> p k c", k=HC),
                         a.Wd[e].rearrange("(k p) c -> p k c", p=P)).then_inc(raw1_in[e % 2], 16)

    def scalar(act):
        def group(G, par, first, last):
            for pos, (kind, n) in enumerate(uses):
                if kind == "S":
                    kt = n // HPG
                    act.wait_ge(s_ready, G * (GT * HPG) + (n + 1))
                    if n % HPG == 0 and not (first and kt < 2):
                        act.wait_ge(pv_done, G * GT + (kt - 1))
                    nc.scalar.activation(ex[:, kt % 2, n % HPG, :], ring(pos), ACT.Exp).then_inc(exp_done, 1)
                if kind == "Q" and last:
                    following.take_x(act, 0, ring(pos)[:, 0:CH])

        groups(act, group)

    def vector(dve):
        def prepare(G, par, first):
            if not first:
                dve.wait_ge(k_turned, G)
            nc.vector.tensor_copy(va[:, par, :, :, 0:DH].rearrange("p t h d -> p (t h) d"), one_group(g.v, G))
            write_sides(nc, dve, g, G, qs, ks, scaled, prep_step, prep_ready, True)

        def take_sides(G, par):
            dve.wait_ge(q_turned, G + 1)
            nc.vector.tensor_copy(qT[:, par, :], ring(POS["Q"])).then_inc(qT_ready, 1)
            dve.wait_ge(k_turned, G + 1)
            nc.vector.tensor_copy(kT[:, par, :], ring(POS["K"])).then_inc(kT_ready, 1)

        def take_pv(G):
            dve.wait_ge(pv_done, (G + 1) * GT)
            nc.vector.tensor_copy(oT[:, :], pv_ps).then_inc(oT_ready, 1)

        def split(G, par):
            raw = raw1[:, par, :]
            high, low = (buf[:, bass.ds(G, 1), :].rearrange("p o n -> p (o n)") for buf in (g.w1h, g.w1l))
            dve.wait_ge(raw1_in[par], (G - par) * 24 + 48)
            nc.vector.tensor_scalar(high, raw, W_SCALE, None, ALU.mult).then_inc(high_ready, 1)
            dve.wait_ge(high_ready, G + 1)
            nc.vector.scalar_tensor_tensor(out=low, in0=raw, scalar=W_SCALE, in1=high, op0=ALU.mult,
                                           op1=ALU.subtract).then_inc(raw1_used, 1)

        def group(G, par, first, last):
            if not first:
                take_pv(G - 1)
                take_out(dve, G - 1, ring(POS["O"]))
            if not last:
                prepare(G + 1, 1 - par, False)
                take_sides(G + 1, 1 - par)
            split(G, par)
            if last:
                following.norm_in_stats(dve, 0)
                following.norm_in(dve, 0)

        prepare(0, 0, True)
        take_sides(0, 0)
        groups(dve, group)
        take_pv(NG - 1)

    def last_out(dve):
        take_out(dve, NG - 1, pv_ps)

    def tensor(pe):
        def turn(src, kind, done):
            for t in range(GT):
                last = nc.tensor.transpose(ring(POS[kind])[:, t * P:(t + 1) * P],
                                           src[:, t, :, :].rearrange("p h r -> p (h r)"), g.ident[:, :])
            last.then_inc(done, 1)

        def values(G, par, kt, half, first):
            if half == 0:
                pe.wait_ge(exp_done, G * (GT * HPG) + (kt + 1) * HPG)
                if kt == 0 and not first:
                    pe.wait_ge(oT_ready, G)
            for h in range(HPG):
                cols = slice(half * CH, (half + 1) * CH)
                last = nc.tensor.matmul(pv_ps[h * AUG:(h + 1) * AUG, cols], va[:, par, kt, h, :], ex[:, kt % 2, h, cols],
                                        start=(kt == 0), stop=(kt == GT - 1))
            if half == 1:
                last.then_inc(pv_done, 1)

        def group(G, par, first, last_group):
            pe.wait_ge(kT_ready, G + 1)
            pe.wait_ge(qT_ready, G + 1)
            for pos, (kind, n) in enumerate(uses):
                if kind == "S":
                    kt, h = n // HPG, n % HPG
                    place_free(pe, G, pos, first, last_group)
                    part = slice(h * AUG, (h + 1) * AUG)
                    for half in range(2):
                        cols = slice(half * CH, (half + 1) * CH)
                        last = nc.tensor.matmul(ring(pos)[:, cols], kT[part, par, kt * P:(kt + 1) * P], qT[part, par, cols],
                                                start=True, stop=True)
                    last.then_inc(s_ready, 1)
                    if h in (1, 3):
                        if kt >= 1:
                            values(G, par, kt - 1, h // 2, first)
                        elif not first:
                            values(G - 1, 1 - par, GT - 1, h // 2, False)
                if kind == "O" and not first:
                    place_free(pe, G, pos, first, last_group)
                    turn_out(pe, G - 1, ring(POS["O"]))
                if kind in "QK" and not last_group:
                    place_free(pe, G, pos, first, last_group)
                    if kind == "Q":
                        pe.wait_ge(prep_ready, G + 2)
                    turn(qs if kind == "Q" else ks, kind, q_turned if kind == "Q" else k_turned)
                if kind == "Q" and last_group:
                    place_free(pe, G, pos, first, last_group)
                    following.turn_x(pe, 0, ring(pos)[:, 0:CH])

        pe.wait_ge(prep_ready, 1)
        turn(qs, "Q", q_turned)
        turn(ks, "K", k_turned)
        groups(pe, group)
        values(NG - 1, 1, GT - 1, 0, False)
        values(NG - 1, 1, GT - 1, 1, False)

    def turn_last(pe):
        turn_out(pe, NG - 1, pv_ps)
    stage.sync = sync
    stage.scalar = scalar
    stage.last_out = last_out
    stage.turn_last = turn_last
    stage.vector = vector
    stage.tensor = tensor
    return stage


def feed(nc, g, a, m, ctx):
    stage = Shared()

    def sb(name, shape, dt=F32):
        return ctx.enter_context(nc.sbuf_tensor(name, shape, dt))

    def sem(name):
        return ctx.enter_context(nc.semaphore(name))

    LAG = 2
    STEPS = E * HC
    silu, h32, hh, hl, sums = m.silu, m.h32, m.hh, m.hl, m.sums
    eye = sb("fd_eye", [P, P], F16)
    xT, xn, z, y = m.xT, m.xn, m.z, m.y
    stats = sb("fd_stats", [P, TPC, 6])
    mv_in = sb("fd_mv_in", [P, TPC, 2])
    mv_out = sb("fd_mv_out", [P, TPC, 2])
    vare = sb("fd_vare", [P, 2, TPC])
    rs = sb("fd_rs", [P, 2, TPC])
    steps = [0]
    pb = g.pb
    gate_ps = lambda k: pb[:, 2 * (k % 2), :]
    up_ps = lambda k: pb[:, 2 * (k % 2) + 1, :]
    sum_ps = lambda c: pb[:, 4 + c % 2, :]
    turn_ps = pb[:, 6, :]

    eye_ready = sem("fd_eye_ready")
    in_vare_ready = sem("fd_in_vare_ready")
    in_rs_ready = sem("fd_in_rs_ready")
    x_ready = sem("fd_x_ready")
    x_turned = sem("fd_x_turned")
    xT_ready = sem("fd_xT_ready")
    xh_ready = sem("fd_xh_ready")
    xl_ready = sem("fd_xl_ready")
    gate_ready = sem("fd_gate_ready")
    up_ready = sem("fd_up_ready")
    silu_ready = sem("fd_silu_ready")
    h_ready = sem("fd_h_ready")
    hh_ready = sem("fd_hh_ready")
    hl_ready = sem("fd_hl_ready")
    added = sem("fd_added")
    summed = sem("fd_summed")
    sums_ready = sem("fd_sums_ready")
    sums_turned = sem("fd_sums_turned")
    out_vare_ready = sem("fd_out_vare_ready")
    out_rs_ready = sem("fd_out_rs_ready")
    y_ready = sem("fd_y_ready")
    stored = [sem(f"fd_stored{i}") for i in range(2)]
    dve_step = sem("fd_dve_step")

    def whole(eng, step, mid, late):
        for c in range(NC):
            for k in range(HC):
                step(c, 0, k)
            mid(c)
            with eng.Fori(1, E // 2) as e:
                for k in range(HC):
                    step(c, e, k)
            late(c)
            with eng.Fori(E // 2, E) as e:
                for k in range(HC):
                    step(c, e, k)

    def wait(eng, sem, value):
        if not (isinstance(value, int) and value <= 0):
            eng.wait_ge(sem, value)

    def take_x(act, c, ps):
        cols = slice(c * CH, (c + 1) * CH)
        act.wait_ge(x_turned, c + 1)
        if c >= 1:
            act.wait_ge(xl_ready, c)
        nc.scalar.activation(xT[:, :], ps, ACT.Copy).then_inc(xT_ready, 1)
        nc.scalar.activation(g.xh[:, cols], ps, ACT.Copy).then_inc(xh_ready, 1)

    def norm_stats(link, mv, of):
        for i in range(TPC):
            last = nc.vector.bn_stats(stats[:, i, :], of[:, i * C:(i + 1) * C])
        link(last)
        for i in range(TPC):
            last = nc.vector.bn_aggr(mv[:, i, :], stats[:, i, :])
        link(last)

    def norm_in_stats(dve, c):
        link = chain(dve, dve_step, steps)
        b, t0, rows = c // CPB, (c % CPB) * TPC, slice(c * TPC, (c + 1) * TPC)
        zc = z[:, c % 2, :]
        link(nc.vector.tensor_tensor(
            zc.rearrange("p (t g n) -> p t g n", t=TPC, g=HG),
            g.x0[:, rows, :].rearrange("p t (g n) -> p t g n", g=HG),
            g.ctx[:, b * HG:(b + 1) * HG, t0:t0 + TPC, :, :].rearrange("p g t h d -> p t g (h d)"), ALU.add))
        norm_stats(link, mv_in, zc)
        nc.vector.tensor_scalar(vare[:, 0, :], mv_in[:, :, 1], LN_EPS, None, ALU.add).then_inc(in_vare_ready, 1)

    def norm_in(dve, c):
        dve.wait_ge(in_rs_ready, c + 1)
        for i in range(TPC):
            last = nc.vector.tensor_scalar(xn[:, i, :], z[:, c % 2, i * C:(i + 1) * C], mv_in[:, i, 0:1], rs[:, 0, i:i + 1],
                                           ALU.subtract, ALU.mult)
        last.then_inc(x_ready, 1)
        dve.wait_ge(xh_ready, c + 1)
        nc.vector.tensor_tensor(g.xl[:, c * CH:(c + 1) * CH], xT[:, :], g.xh[:, c * CH:(c + 1) * CH],
                                ALU.subtract).then_inc(xl_ready, 1)

    def turn_x(pe, c, ps):
        pe.wait_ge(x_ready, c + 1)
        for i in range(TPC):
            last = nc.tensor.transpose(ps[:, i * P:(i + 1) * P], xn[:, i, :], g.ident[:, :])
        last.then_inc(x_turned, 1)

    def sync(sp):
        for c in range(NC):
            sp.wait_ge(y_ready, c + 1)
            sp.dma_start(a.out_tiles[:, c * TPC:(c + 1) * TPC, :], y[:, c % 2, :, :]).then_inc(stored[c % 2], 16)
        sp.wait_ge(stored[0], 16 * (NC // 2))
        sp.wait_ge(stored[1], 16 * (NC // 2))

    def gpsimd(pool):
        nc.gpsimd.memset(eye[:, :], 0.0).then_inc(eye_ready, 1)
        pool.wait_ge(eye_ready, 1)
        nc.gpsimd.affine_select(out=eye[:, :], in_=eye[:, :], compare_op=ALU.not_equal, fill=W_SCALE,
                                base=0, pattern=[[-1, P]], channel_multiplier=1).then_inc(eye_ready, 1)

        def rsqrt_in(c):
            pool.wait_ge(in_vare_ready, c + 1)
            nc.gpsimd.tensor_tensor(rs[:, 0, :], vare[:, 0, :], g.minus_half[:, 0:TPC], ALU.pow).then_inc(in_rs_ready, 1)

        def rsqrt_out(c):
            pool.wait_ge(out_vare_ready, c + 1)
            nc.gpsimd.tensor_tensor(rs[:, 1, :], vare[:, 1, :], g.minus_half[:, 0:TPC], ALU.pow).then_inc(out_rs_ready, 1)

        rsqrt_in(0)
        for c in range(NC):
            if c < NC - 1:
                rsqrt_in(c + 1)
            if c >= 1:
                rsqrt_out(c - 1)
        rsqrt_out(NC - 1)

    def scalar(act):
        def take_sums(c):
            act.wait_ge(summed, c + 1)
            if c >= 1:
                act.wait_ge(sums_turned, c)
            nc.scalar.activation(sums[:, :], sum_ps(c), ACT.Copy, scale=1.0 / W_SCALE).then_inc(sums_ready, 1)

        def high(n, k):
            act.wait_ge(h_ready, n + 1)
            wait(act, added, n - 2)
            nc.scalar.activation(hh[:, k, :], h32[:, k % 2, :], ACT.Copy).then_inc(hh_ready, 1)

        def step(c, e, k):
            n = c * STEPS + e * HC + k
            act.wait_ge(gate_ready, n + 1)
            wait(act, h_ready, n - 1)
            nc.scalar.activation(silu[:, k % 2, :], gate_ps(k), ACT.Silu, scale=1.0 / W_SCALE).then_inc(silu_ready, 1)
            if not (isinstance(n, int) and n == 0):
                high(n - 1, (k - 1) % HC)
            if c >= 1 and isinstance(e, int) and k == LAG:
                take_sums(c - 1)

        whole(act, step, lambda c: None, lambda c: take_x(act, c + 1, turn_ps) if c < NC - 1 else None)
        high(NC * STEPS - 1, HC - 1)
        take_sums(NC - 1)

    def vector(dve, before):
        link = chain(dve, dve_step, steps)

        def norm_out_stats(c):
            dve.wait_ge(sums_turned, c + 1)
            norm_stats(link, mv_out, sum_ps(c))
            nc.vector.tensor_scalar(vare[:, 1, :], mv_out[:, :, 1], LN_EPS, None, ALU.add).then_inc(out_vare_ready, 1)

        def norm_out(c):
            dve.wait_ge(out_rs_ready, c + 1)
            if c >= 2:
                dve.wait_ge(stored[c % 2], 16)
            for i in range(TPC):
                last = nc.vector.tensor_scalar(y[:, c % 2, i, :], sum_ps(c)[:, i * C:(i + 1) * C], mv_out[:, i, 0:1],
                                               rs[:, 1, i:i + 1], ALU.subtract, ALU.mult)
            last.then_inc(y_ready, 1)

        def low(n, k):
            dve.wait_ge(hh_ready, n + 1)
            wait(dve, added, n - 2)
            nc.vector.tensor_tensor(hl[:, k, :], h32[:, k % 2, :], hh[:, k, :], ALU.subtract).then_inc(hl_ready, 1)

        def step(c, e, k):
            n = c * STEPS + e * HC + k
            dve.wait_ge(up_ready, n + 1)
            dve.wait_ge(silu_ready, n + 1)
            wait(dve, hl_ready, n - 1)
            nc.vector.scalar_tensor_tensor(out=h32[:, k % 2, :], in0=up_ps(k), scalar=1.0 / W_SCALE, in1=silu[:, k % 2, :],
                                           op0=ALU.mult, op1=ALU.mult).then_inc(h_ready, 1)
            if not (isinstance(n, int) and n == 0):
                low(n - 1, (k - 1) % HC)

        def mid(c):
            if c == 0:
                before.last_out(dve)
            if c < NC - 1:
                norm_in_stats(dve, c + 1)
            if c >= 1:
                norm_out_stats(c - 1)

        def late(c):
            if c < NC - 1:
                norm_in(dve, c + 1)
            if c >= 1:
                norm_out(c - 1)

        whole(dve, step, mid, late)
        low(NC * STEPS - 1, HC - 1)
        norm_out_stats(NC - 1)
        norm_out(NC - 1)

    def tensor(pe, before):
        def begin(c):
            if c >= 2:
                pe.wait_ge(y_ready, c - 1)
            nc.tensor.matmul(sum_ps(c), eye[:, :], g.xh[:, c * CH:(c + 1) * CH], start=True, stop=False, skip_group_check=True)

        def end(c):
            nc.tensor.matmul(sum_ps(c), eye[:, :], g.xl[:, c * CH:(c + 1) * CH], start=False, stop=True,
                             skip_group_check=True).then_inc(summed, 1)

        def turn_sums(c):
            pe.wait_ge(sums_ready, c + 1)
            for i in range(TPC):
                last = nc.tensor.transpose(sum_ps(c)[:, i * P:(i + 1) * P], sums[:, i * P:(i + 1) * P], g.ident[:, :])
            last.then_inc(sums_turned, 1)

        def add(c, e, k, n):
            pe.wait_ge(hl_ready, n + 1)
            wd = slice(2 * H + k * P, 2 * H + (k + 1) * P)
            for w, h in ((g.w1h, hh), (g.w1h, hl), (g.w1l, hh)):
                last = nc.tensor.matmul(sum_ps(c), w[:, bass.ds(e, 1), wd], h[:, k, :], start=False, stop=False,
                                        skip_group_check=True)
            last.then_inc(added, 1)

        def step(c, e, k):
            n = c * STEPS + e * HC + k
            x = slice(c * CH, (c + 1) * CH)
            wait(pe, silu_ready, n - 1)
            wait(pe, h_ready, n - 1)
            for ps, lo, done in ((gate_ps(k), 0, gate_ready), (up_ps(k), H, up_ready)):
                w = slice(lo + k * P, lo + (k + 1) * P)
                for i, (lhs, rhs) in enumerate(((g.w1h, g.xh), (g.w1h, g.xl), (g.w1l, g.xh))):
                    last = nc.tensor.matmul(ps, lhs[:, bass.ds(e, 1), w], rhs[:, x], start=(i == 0), stop=(i == 2))
                last.then_inc(done, 1)
            if k >= LAG:
                add(c, e, k - LAG, n - LAG)
            elif isinstance(e, int) and e == 0:
                if c >= 1:
                    add(c - 1, E - 1, k - LAG + HC, n - LAG)
                    if k == LAG - 1:
                        end(c - 1)
                        begin(c)
            else:
                add(c, e - 1, k - LAG + HC, n - LAG)

        pe.wait_ge(eye_ready, 2)
        pe.wait_ge(xl_ready, 1)
        begin(0)

        def mid(c):
            if c == 0:
                before.turn_last(pe)
            if c >= 1:
                turn_sums(c - 1)

        def late(c):
            if c < NC - 1:
                turn_x(pe, c + 1, turn_ps)
                pe.wait_ge(xl_ready, c + 2)

        whole(pe, step, mid, late)
        for k in range(HC - LAG, HC):
            add(NC - 1, E - 1, k, NC * STEPS - HC + k)
        end(NC - 1)
        turn_sums(NC - 1)
    stage.sync = sync
    stage.gpsimd = gpsimd
    stage.scalar = scalar
    stage.vector = vector
    stage.tensor = tensor
    stage.take_x = take_x
    stage.norm_in_stats = norm_in_stats
    stage.norm_in = norm_in
    stage.turn_x = turn_x
    stage.xh_ready = xh_ready
    return stage


def layer1(nc, g, a):
    with ExitStack() as ctx:
        def sb(name, shape, dt=F32):
            return ctx.enter_context(nc.sbuf_tensor(name, shape, dt))

        m = Shared()
        m.qs = sb("qs", [P, GT, HPG, AUG])
        m.ks = sb("ks", [P, GT, HPG, AUG])
        m.scaled = sb("scaled", [P, GT, HPG, DH])
        m.qT = sb("qT", [P, 2, T], F32R)
        m.kT = sb("kT", [P, 2, T], F32R)
        m.va = sb("va", [P, 2, GT, HPG, AUG])
        m.ex = sb("ex_scores", [P, 2, HPG, T])
        m.cleared = ctx.enter_context(nc.semaphore("cleared"))
        m.large_ready = ctx.enter_context(nc.semaphore("large_ready"))
        m.hh = sb("fd_hh", [P, HC, CH], F16)
        m.hl = sb("fd_hl", [P, HC, CH], F16)
        idle = m.ex[:, :, :, :].rearrange("p a h t -> p (a h t)")
        m.xT_project, m.silu, m.h32 = (idle[:, i * 2 * CH:(i + 1) * 2 * CH].rearrange("p (a n) -> p a n", a=2) for i in range(3))
        m.sums = idle[:, 6 * CH:7 * CH]
        m.w_raw = idle[:, 7 * CH:7 * CH + 2 * C].rearrange("p (a n) -> p a n", a=2)
        m.w_T = idle[:, 8 * CH:8 * CH + 2 * C]
        m.oT = g.x1[:, 0:GT, :].rearrange("p t c -> p (t c)")
        m.xn = g.x1[:, GT:GT + TPC, :]
        m.xT = g.x1[:, GT + TPC:GT + 2 * TPC, :].rearrange("p t c -> p (t c)")
        m.z = g.moe[:, 0:2 * TPC, :].rearrange("p (a t) c -> p a (t c)", a=2)
        m.y = g.moe[:, 2 * TPC:4 * TPC, :].rearrange("p (a t) c -> p a t c", a=2)

        pj = project(nc, g, a, m, ctx)
        mx = maxima(nc, g, a, m, ctx)
        fd = feed(nc, g, a, m, ctx)
        at = attend(nc, g, a, m, ctx, fd)
        block = ctx.enter_context(nc.Block())

        @block.sync
        def _(sp):
            pj.sync(sp)
            at.sync(sp)
            fd.sync(sp)

        @block.gpsimd
        def _(pool):
            pj.gpsimd(pool)
            fd.gpsimd(pool)

        @block.scalar
        def _(act):
            pj.scalar(act)
            at.scalar(act)
            fd.scalar(act)

        @block.vector
        def _(dve):
            pj.vector(dve)
            mx.vector(dve)
            at.vector(dve)
            fd.vector(dve, at)

        @block.tensor
        def _(pe):
            pj.tensor(pe)
            mx.tensor(pe)
            at.tensor(pe)
            fd.tensor(pe, at)


def mixture0(nc, ctx, g):
    g.w0h = ctx.enter_context(nc.sbuf_tensor("w0h", [P, E, 2 * H], F16))
    g.w0l = ctx.enter_context(nc.sbuf_tensor("w0l", [P, E, 2 * H], F16))
    g.raw0 = ctx.enter_context(nc.sbuf_tensor("raw0", [P, E, 2 * H], F32))


def mixture1(nc, ctx, g):
    g.w1h = ctx.enter_context(nc.sbuf_tensor("w1h", [P, E, 3 * H], F16))
    g.w1l = ctx.enter_context(nc.sbuf_tensor("w1l", [P, E, 3 * H], F16))


def globals_(nc, ctx, g):
    def sb(name, shape, dt=F32):
        return ctx.enter_context(nc.sbuf_tensor(name, shape, dt))

    def sem(name):
        return ctx.enter_context(nc.semaphore(name))

    g.pb = ctx.enter_context(nc.psum_tensor("pb", [P, 8, CH], F32))
    g.x0 = sb("x0", [P, NT, C])
    g.x1 = sb("x1", [P, NT, C])
    g.ident = sb("ident", [P, P])
    g.minus_half = sb("minus_half", [P, NT])
    g.cols = sb("cols", [P, NCOLS])
    g.gate = sb("gate", [P, E, NT])
    g.gate_down = sb("gate_down", [P, E, NT])
    g.gate_down_flat = g.gate_down[:, :, :].rearrange("p e t -> p (e t)")
    g.moe = sb("moe", [P, NT, C])
    g.xh = sb("xh", [P, N], F16)
    g.xl = sb("xl", [P, N], F16)
    g.raw0_scaled = sem("raw0_scaled")
    g.w0h_ready = sem("w0h_ready")
    g.w0l_ready = sem("w0l_ready")
    g.q = sb("q", [P, NG, GT, HPG, DH])
    g.v = sb("v", [P, NG, GT, HPG, DH])
    g.ctx = sb("ctx", [P, NG, GT, HPG, DH])
    g.qbit = sb("qbit", [P, NG, GT, HPG])
    g.kbit = sb("kbit", [P, NG, GT, HPG])
    g.lift = sb("lift", [P, NG, GT, HPG])
    g.large = sb("large", [P, 1], mybir.dt.int32)
    g.raw0_in = [sem(f"raw0_in{e}") for e in range(E)]
    g.cols_ready = sem("cols_ready")
    g.junk_done = sem("junk_done")


_INS = ['L0_attn_x', 'L0_attn_ln1_w', 'L0_attn_ln2_w', 'L0_attn_time_decay', 'L0_attn_time_first', 'L0_attn_time_mix_k',
        'L0_attn_time_mix_v', 'L0_attn_time_mix_r', 'L0_attn_W_key', 'L0_attn_W_value', 'L0_attn_W_recept',
        'L0_attn_W_out', 'L0_attn_time_mix_k2', 'L0_attn_time_mix_r2', 'L0_attn_W_key2', 'L0_attn_W_value2',
        'L0_attn_W_recept2', 'L0_ffn_wg', 'L0_ffn_w1', 'L0_ffn_b1', 'L0_ffn_w2', 'L0_ffn_b2', 'L1_attn_qk_w',
        'L1_attn_qk_b', 'L1_attn_v_w', 'L1_attn_v_b', 'L1_attn_hash_a', 'L1_ffn_Wg', 'L1_ffn_Wu', 'L1_ffn_Wd']


def inputs(a, aps):
    (a.x, a.ln1_w, a.ln2_w, a.decay, a.first, a.mix_k, a.mix_v, a.mix_r, a.W_key, a.W_value, a.W_recept, a.W_out,
     a.mix_k2, a.mix_r2, a.W_key2, a.W_value2, a.W_recept2, a.wg, a.w1, a.b1, a.w2, a.b2, a.qk_w, a.qk_b, a.v_w, a.v_b,
     a.hash_a, a.Wg, a.Wu, a.Wd) = aps
    a.x_tiles = a.x.rearrange("b (t p) c -> p (b t) c", p=P)


def program(nc, *aps):
    with ExitStack() as ctx:
        g, a = Shared(), Shared()
        inputs(a, aps[:-1])
        a.out_tiles = aps[-1].rearrange("b (t p) c -> p (b t) c", p=P)
        globals_(nc, ctx, g)
        with ExitStack() as weights:
            mixture0(nc, weights, g)
            time_mix(nc, g, a)
            channel_mix(nc, g, a)
            route(nc, g, a)
            experts(nc, g, a)
        with ExitStack() as weights:
            mixture1(nc, weights, g)
            layer1(nc, g, a)


_OUTS = [((B, T, C), 'float32')]


def kernel(**inputs):
    import numpy as _np
    import concourse.bacc as _bacc
    from concourse import mybir as _mybir
    from concourse.bass_utils import run_bass_kernel_spmd as _run

    nc = _bacc.Bacc("TRN2", target_bir_lowering=False, num_devices=1)
    arrays, args = {}, []
    for name in _INS:
        a = _np.ascontiguousarray(inputs[name])
        arrays[f"in_{name}_dram"] = a
        args.append(nc.dram_tensor(f"in_{name}_dram", a.shape, _mybir.dt.from_np(a.dtype), kind="ExternalInput").ap())
    for i, (shape, dtype) in enumerate(_OUTS):
        dt = _mybir.dt.from_np(_np.dtype(dtype))
        args.append(nc.dram_tensor(f"out_{i}_dram", shape, dt, kind="ExternalOutput").ap())
    program(nc, *args)
    r = _run(nc, [arrays], core_ids=[0])
    return r.results[0]["out_0_dram"]
```

```python
import math
from contextlib import ExitStack

import concourse.bass as bass
from concourse import mybir

ALU = mybir.AluOpType
ACT = mybir.ActivationFunctionType
AX = mybir.AxisListType
F32 = mybir.dt.float32
F16 = mybir.dt.float16
F32R = mybir.dt.float32r

P = 128
B, T, C = 2, 1024, 128
N = B * T
NT = N // P
CH = 512
NC = N // CH
TPC = CH // P
CPB = T // CH
E = 8
H = 512
HC = H // P
TOPK = 2
CAP = TOPK * N // E
HEADS = 16
DH = C // HEADS
HPG = 4
HG = HEADS // HPG
NG = B * HG
GT = T // P
AUG = P // HPG
HASH = DH + 2
U_HASH = 0.75
MASK = 10000.0
SAFE_SCORE = 60.0
RMS_EPS = 1e-6
LN_EPS = 1e-5
WKV_EPS = 1e-8
CLIP = 20.0
W_SCALE = 256.0

LN1, LN2, DECAY, FIRST, MIXK, MIXV, MIXR, MIXK2, MIXR2, B1 = range(10)
NCOLS = B1 + E * HC


class Shared:
    pass


def schedule(chunks, order):
    return [(s - p, p) for s in range(chunks + len(order) - 1) for p in order if 0 <= s - p < chunks]


def chain(eng, sem, count=None):
    count = [0] if count is None else count

    def link(ins):
        count[0] += 1
        ins.then_inc(sem, 1)
        eng.wait_ge(sem, count[0])

    return link


def shifted(buf, c):
    b, o = c // CPB, 1 + (c % CPB) * CH
    return buf[:, b, o:o + CH], buf[:, b, o - 1:o - 1 + CH]


def scale_raw(nc, pool, g, e):
    if e < E:
        pool.wait_ge(g.raw0_in[e // 2], 64)
        nc.gpsimd.tensor_scalar(g.raw0[:, e, :], g.raw0[:, e, :], W_SCALE, 1.0, ALU.mult, ALU.mult).then_inc(g.raw0_scaled, 1)
    if e >= 1:
        pool.wait_ge(g.w0h_ready, e)
        nc.gpsimd.tensor_tensor(g.w0l[:, e - 1, :], g.raw0[:, e - 1, :], g.w0h[:, e - 1, :], ALU.subtract)


def high_part(nc, act, g, e):
    act.wait_ge(g.raw0_scaled, e + 1)
    nc.scalar.activation(g.w0h[:, e, :], g.raw0[:, e, :], ACT.Copy).then_inc(g.w0h_ready, 1)


def time_mix(nc, g, a):
    with ExitStack() as ctx:
        def sb(name, shape, dt=F32):
            return ctx.enter_context(nc.sbuf_tensor(name, shape, dt))

        def sem(name):
            return ctx.enter_context(nc.semaphore(name))

        rows = sb("rows", [64, P])
        w_k, w_v, w_r, w_o = (sb(n, [P, P]) for n in ("w_k", "w_v", "w_r", "w_o"))
        junk = sb("junk", [P, P])
        ss = sb("ss", [P, NT])
        ms = sb("ms", [P, NT])
        ss2 = sb("tm_ss2", [P, NT])
        ms2 = sb("tm_ms2", [P, NT])
        rstd = sb("rstd", [P, NT])
        ew = sb("ew", [P, 4])
        hx = sb("hx", [P, 2, TPC, P])
        hT = sb("hT", [P, B, 1 + T])
        diff = sb("diff", [P, CH])
        xm = sb("xm", [P, 2, 3, CH])
        ex = sb("ex", [P, 2, 3, CH])
        ekv = sb("ekv", [P, CH])
        ektv = sb("ektv", [P, CH])
        aS = sb("aS", [P, B, 1 + T])
        bS = sb("bS", [P, B, 1 + T])
        den = sb("den", [P, CH])
        rden = sb("rden", [P, CH])
        yT = sb("yT", [P, 2, CH])
        pb = g.pb
        tr_bank = lambda c: pb[:, c % 2, :]
        k_ps, v_ps, r_ps = pb[:, 2, :], pb[:, 3, :], pb[:, 4, :]
        out_bank = lambda c: pb[:, 5 + c % 2, :]

        x_in = [sem(f"x_in{c}") for c in range(NC)]
        rows_in = sem("rows_in")
        w_in = sem("w_in")
        wo_in = sem("wo_in")
        ident_ready = sem("ident_ready")
        cols_turned = sem("cols_turned")
        zeros_ready = sem("zeros_ready")
        edecay_ready = sem("edecay_ready")
        wclip_ready = sem("wclip_ready")
        ew_ready = sem("ew_ready")
        ss_ready = sem("ss_ready")
        ms_ready = sem("ms_ready")
        ss2_ready = sem("tm_ss2_ready")
        ms2_ready = sem("tm_ms2_ready")
        rstd_ready = sem("rstd_ready")
        hx_ready = sem("hx_ready")
        turned = sem("turned")
        hT_ready = sem("hT_ready")
        diff_ready = sem("diff_ready")
        xm_ready = sem("xm_ready")
        kvr_ready = sem("kvr_ready")
        ex_ready = sem("ex_ready")
        v_used = sem("v_used")
        y_ready = sem("y_ready")
        out_ready = sem("out_ready")
        x1_ready = sem("x1_ready")
        dve_step = sem("tm_dve_step")

        block = ctx.enter_context(nc.Block())
        plan = schedule(NC, (1, 2, 0, 3, 4, 5))

        @block.sync
        def _(sp):
            def load_x(c):
                sp.dma_start(g.x0[:, c * TPC:(c + 1) * TPC, :], a.x_tiles[:, c * TPC:(c + 1) * TPC, :]).then_inc(x_in[c], 16)

            load_x(0)
            for i, v in enumerate((a.ln1_w, a.ln2_w, a.decay, a.first, a.mix_k, a.mix_v, a.mix_r, a.mix_k2, a.mix_r2)):
                sp.dma_start(rows[i:i + 1, :], v.rearrange("(a n) -> a n", a=1)).then_inc(rows_in, 16)
            sp.dma_start(rows[B1:NCOLS, :], a.b1.rearrange("e (k p) -> (e k) p", p=P)).then_inc(rows_in, 16)
            load_x(1)
            for w, src in ((w_k, a.W_key), (w_v, a.W_value), (w_r, a.W_recept)):
                sp.dma_start(w[:, :], src).then_inc(w_in, 16)
            for c in range(2, NC):
                load_x(c)
            sp.dma_start(w_o[:, :], a.W_out).then_inc(wo_in, 16)
            for e in range(E):
                sp.dma_start(g.raw0[:, e, 0:H], a.w1[e]).then_inc(g.raw0_in[e // 2], 16)
                sp.dma_start(g.raw0[:, e, H:2 * H].rearrange("p (k c) -> p k c", k=HC),
                             a.w2[e].rearrange("(k p) c -> p k c", p=P)).then_inc(g.raw0_in[e // 2], 16)

        @block.gpsimd
        def _(pool):
            nc.gpsimd.memset(g.ident[:, :], 0.0).then_inc(ident_ready, 1)
            pool.wait_ge(ident_ready, 1)
            nc.gpsimd.affine_select(out=g.ident[:, :], in_=g.ident[:, :], compare_op=ALU.not_equal, fill=1.0,
                                    base=0, pattern=[[-1, P]], channel_multiplier=1).then_inc(ident_ready, 1)
            nc.gpsimd.memset(g.minus_half[:, :], -0.5).then_inc(ident_ready, 1)
            pool.wait_ge(ident_ready, 3)
            for c, phase in plan:
                if phase == 0:
                    t = slice(c * TPC, (c + 1) * TPC)
                    pool.wait_ge(ms_ready, c + 1)
                    nc.gpsimd.tensor_tensor(rstd[:, t], ms[:, t], g.minus_half[:, 0:TPC], ALU.pow).then_inc(rstd_ready, 1)
                if phase == 2:
                    h, sh = shifted(hT, c)
                    pool.wait_ge(zeros_ready, 3)
                    pool.wait_ge(hT_ready, c + 1)
                    if c >= 1:
                        pool.wait_ge(xm_ready, c)
                    nc.gpsimd.tensor_tensor(diff[:, :], h, sh, ALU.subtract).then_inc(diff_ready, 1)
                if phase == 3:
                    scale_raw(nc, pool, g, c)
                if phase == 5 and c < NC - 1:
                    t = slice(c * TPC, (c + 1) * TPC)
                    pool.wait_ge(ms2_ready, c + 1)
                    nc.gpsimd.tensor_tensor(g.rstd2[:, t], ms2[:, t], g.minus_half[:, 0:TPC], ALU.pow)

        @block.scalar
        def _(act):
            for c, phase in plan:
                if phase == 0:
                    act.wait_ge(x_in[c], 16)
                    for t in range(c * TPC, (c + 1) * TPC):
                        last = nc.scalar.activation(junk[:, :], g.x0[:, t, :], ACT.Square, accum_out=ss[:, t:t + 1])
                        if t % TPC < TPC - 1:
                            last.then_inc(g.junk_done, 1)
                            act.wait_ge(g.junk_done, (TPC - 1) * c + t % TPC + 1)
                    last.then_inc(ss_ready, 1)
                    act.wait_ge(ss_ready, c + 1)
                if phase == 1:
                    for i in range(TPC):
                        t = c * TPC + i
                        if i == 0:
                            act.wait_ge(rstd_ready, c + 1)
                            if c >= 2:
                                act.wait_ge(turned, c - 1)
                        last = nc.scalar.activation(hx[:, c % 2, i, :], g.x0[:, t, :], ACT.Copy, scale=rstd[:, t:t + 1])
                    last.then_inc(hx_ready, 1)
                    if c == 0:
                        act.wait_ge(g.cols_ready, 1)
                        nc.scalar.activation(ew[:, 0:1], g.cols[:, DECAY:DECAY + 1], ACT.Exp).then_inc(edecay_ready, 1)
                        act.wait_ge(wclip_ready, 1)
                        nc.scalar.activation(ew[:, 2:3], ew[:, 1:2], ACT.Exp).then_inc(ew_ready, 1)
                if phase == 5 and c < NC - 1:
                    act.wait_ge(x1_ready, c + 1)
                    for t in range(c * TPC, (c + 1) * TPC):
                        nc.scalar.activation(junk[:, :], g.x1[:, t, :], ACT.Square, accum_out=ss2[:, t:t + 1]).then_inc(ss2_ready, 1)
                        act.wait_ge(ss2_ready, t + 1)
                if phase == 2:
                    act.wait_ge(turned, c + 1)
                    nc.scalar.activation(shifted(hT, c)[0], tr_bank(c), ACT.Copy,
                                         scale=g.cols[:, LN1:LN1 + 1]).then_inc(hT_ready, 1)
                if phase == 3:
                    act.wait_ge(kvr_ready, c + 1)
                    if c >= 2:
                        act.wait_ge(y_ready, c - 1)
                    nc.scalar.activation(ex[:, c % 2, 0, :], k_ps, ACT.Exp).then_inc(ex_ready, 1)
                    nc.scalar.activation(ex[:, c % 2, 1, :], k_ps, ACT.Exp,
                                         bias=g.cols[:, FIRST:FIRST + 1]).then_inc(ex_ready, 1)
                    nc.scalar.activation(ex[:, c % 2, 2, :], r_ps, ACT.Tanh, scale=0.5).then_inc(ex_ready, 1)
                    high_part(nc, act, g, c)

        @block.vector
        def _(dve):
            link = chain(dve, dve_step)
            for buf in (hT, aS, bS):
                nc.vector.memset(buf[:, :, 0:1], 0.0).then_inc(zeros_ready, 1)
            dve.wait_ge(zeros_ready, 3)
            for c, phase in plan:
                h, sh = shifted(hT, c)
                if phase == 0:
                    t = slice(c * TPC, (c + 1) * TPC)
                    dve.wait_ge(ss_ready, c + 1)
                    nc.vector.tensor_scalar(ms[:, t], ss[:, t], 1.0 / C, RMS_EPS, ALU.mult, ALU.add).then_inc(ms_ready, 1)
                    if c == 0:
                        dve.wait_ge(cols_turned, 1)
                        nc.vector.tensor_copy(g.cols[:, :], pb[:, 7, 0:NCOLS]).then_inc(g.cols_ready, 1)
                        dve.wait_ge(edecay_ready, 1)
                        link(nc.vector.tensor_scalar(ew[:, 3:4], ew[:, 0:1], -1.0, -CLIP, ALU.mult, ALU.max))
                        nc.vector.tensor_scalar(ew[:, 1:2], ew[:, 3:4], CLIP, None, ALU.min).then_inc(wclip_ready, 1)
                if phase == 2:
                    dve.wait_ge(hT_ready, c + 1)
                    if c >= 2:
                        dve.wait_ge(kvr_ready, c - 1)
                    dve.wait_ge(diff_ready, c + 1)
                    for i, m in enumerate((MIXK, MIXV, MIXR)):
                        last = nc.vector.scalar_tensor_tensor(out=xm[:, c % 2, i, :], in0=diff[:, :], scalar=g.cols[:, m:m + 1],
                                                              in1=sh, op0=ALU.mult, op1=ALU.add)
                    last.then_inc(xm_ready, 1)
                if phase == 3:
                    ek, ekt, th = (ex[:, c % 2, i, :] for i in range(3))
                    a_now, a_before = shifted(aS, c)
                    b_now, b_before = shifted(bS, c)
                    dve.wait_ge(ex_ready, 3 * (c + 1))
                    if c == 0:
                        dve.wait_ge(ew_ready, 1)
                    link(nc.vector.tensor_scalar(ex[:, c % 2, 0:2, :], ex[:, c % 2, 0:2, :], math.exp(-CLIP), math.exp(CLIP),
                                                 ALU.max, ALU.min))
                    nc.vector.tensor_tensor(ektv[:, :], ekt, v_ps, ALU.mult)
                    nc.vector.tensor_tensor(ekv[:, :], ek, v_ps, ALU.mult).then_inc(v_used, 1)
                    dve.wait_ge(v_used, c + 1)
                    link(nc.vector.tensor_tensor_scan(a_now, ew[:, 2:3].broadcast_to([P, CH]), ekv[:, :],
                                                      a_before[:, 0:1], ALU.mult, ALU.add))
                    link(nc.vector.tensor_tensor_scan(b_now, ew[:, 2:3].broadcast_to([P, CH]), ek,
                                                      b_before[:, 0:1], ALU.mult, ALU.add))
                    link(nc.vector.scalar_tensor_tensor(out=den[:, :], in0=b_before, scalar=WKV_EPS, in1=ekt,
                                                        op0=ALU.add, op1=ALU.add))
                    link(nc.vector.tensor_tensor(ektv[:, :], ektv[:, :], a_before, ALU.add))
                    link(nc.vector.reciprocal(rden[:, :], den[:, :]))
                    link(nc.vector.tensor_tensor(ektv[:, :], ektv[:, :], rden[:, :], ALU.mult))
                    if c >= 2:
                        dve.wait_ge(out_ready, c - 1)
                    nc.vector.scalar_tensor_tensor(out=yT[:, c % 2, :], in0=th, scalar=1.0, in1=ektv[:, :],
                                                   op0=ALU.add, op1=ALU.mult).then_inc(y_ready, 1)
                    dve.wait_ge(y_ready, c + 1)
                if phase == 4:
                    dve.wait_ge(out_ready, c + 1)
                    nc.vector.scalar_tensor_tensor(
                        out=g.x1[:, c * TPC:(c + 1) * TPC, :].rearrange("p t c -> p (t c)"), in0=out_bank(c), scalar=0.5,
                        in1=g.x0[:, c * TPC:(c + 1) * TPC, :].rearrange("p t c -> p (t c)"),
                        op0=ALU.mult, op1=ALU.add).then_inc(x1_ready, 1)
                if phase == 5 and c < NC - 1:
                    t = slice(c * TPC, (c + 1) * TPC)
                    dve.wait_ge(ss2_ready, TPC * (c + 1))
                    nc.vector.tensor_scalar(ms2[:, t], ss2[:, t], 1.0 / C, RMS_EPS, ALU.mult, ALU.add).then_inc(ms2_ready, 1)

        @block.tensor
        def _(pe):
            pe.wait_ge(ident_ready, 2)
            pe.wait_ge(rows_in, 16 * 10)
            nc.tensor.transpose(pb[:, 7, 0:NCOLS], rows[0:NCOLS, :], g.ident[0:NCOLS, 0:NCOLS]).then_inc(cols_turned, 1)
            for c, phase in plan:
                if phase == 1:
                    pe.wait_ge(hx_ready, c + 1)
                    if c >= 2:
                        pe.wait_ge(hT_ready, c - 1)
                    for i in range(TPC):
                        last = nc.tensor.transpose(tr_bank(c)[:, i * P:(i + 1) * P], hx[:, c % 2, i, :], g.ident[:, :])
                    last.then_inc(turned, 1)
                if phase == 2:
                    if c == 0:
                        pe.wait_ge(w_in, 48)
                    pe.wait_ge(xm_ready, c + 1)
                    if c >= 1:
                        pe.wait_ge(ex_ready, 3 * c)
                        pe.wait_ge(v_used, c)
                    for i, (w, ps) in enumerate(((w_k, k_ps), (w_v, v_ps), (w_r, r_ps))):
                        last = nc.tensor.matmul(ps, w[:, :], xm[:, c % 2, i, :], start=True, stop=True)
                    last.then_inc(kvr_ready, 1)
                if phase == 3:
                    if c == 0:
                        pe.wait_ge(wo_in, 16)
                    pe.wait_ge(y_ready, c + 1)
                    if c >= 2:
                        pe.wait_ge(x1_ready, c - 1)
                    for i in range(TPC):
                        last = nc.tensor.matmul(out_bank(c)[:, i * P:(i + 1) * P], yT[:, c % 2, i * P:(i + 1) * P], w_o[:, :],
                                                start=True, stop=True)
                    last.then_inc(out_ready, 1)


def channel_mix(nc, g, a, m, ctx):
    stage = Shared()

    def sb(name, shape, dt=F32):
        return ctx.enter_context(nc.sbuf_tensor(name, shape, dt))

    def sem(name):
        return ctx.enter_context(nc.semaphore(name))

    w_k = sb("w_k2", [P, H])
    w_v = sb("w_v2", [P, HC, P])
    w_r = sb("w_r2", [P, P])
    junk = sb("junk2", [P, P])
    ss = sb("ss2", [P, NT])
    ms = sb("ms2", [P, NT])
    rstd = g.rstd2
    hx = sb("hx2", [P, 2, TPC, P])
    hT = sb("hT2", [P, B, 1 + T])
    diff = sb("diff2", [P, CH])
    xm = sb("xm2", [P, 2, 2, CH])
    relu, th = m.relu, m.th
    sq = m.sq
    z = sb("z2", [P, 2, CH])
    stats = sb("stats2", [P, TPC, 6])
    mv = sb("mv2", [P, 2, TPC, 2])
    vare = sb("vare2", [P, 2, TPC])
    rs = sb("rs2", [P, 2, TPC])
    pb = g.pb
    tr_bank = lambda c: pb[:, c % 2, :]
    key_bank = lambda n: pb[:, 2 + n % 2, :]
    r_ps = pb[:, 4, :]
    val_bank = lambda c: pb[:, 5 + c % 2, :]

    w_in = sem("cm_w_in")
    ss_ready = sem("cm_ss_ready")
    zero_ready = sem("cm_zero_ready")
    ms_ready = sem("cm_ms_ready")
    rstd_ready = sem("cm_rstd_ready")
    hx_ready = sem("cm_hx_ready")
    turned = sem("cm_turned")
    hT_ready = sem("cm_hT_ready")
    xm_ready = sem("cm_xm_ready")
    key_ready = sem("cm_key_ready")
    relu_ready = sem("cm_relu_ready")
    sq_ready = sem("cm_sq_ready")
    r_ready = sem("cm_r_ready")
    stage.th_ready = th_ready = sem("cm_th_ready")
    val_ready = sem("cm_val_ready")
    val_used = sem("cm_val_used")
    vare_ready = sem("cm_vare_ready")
    rs_ready = sem("cm_rs_ready")
    stage.normed = normed = sem("cm_normed")
    dve_step = sem("cm_dve_step")

    plan = schedule(NC, (3, 2, 4, 5, 1, 0))

    def sync(sp):
        sp.dma_start(w_k[:, :], a.W_key2).then_inc(w_in, 16)
        sp.dma_start(w_v[:, :, :], a.W_value2.rearrange("(k p) c -> p k c", p=P)).then_inc(w_in, 16)
        sp.dma_start(w_r[:, :], a.W_recept2).then_inc(w_in, 16)

    def gpsimd(pool):
        for c, phase in plan:
            if phase == 0:
                if c == NC - 1:
                    t = slice(c * TPC, (c + 1) * TPC)
                    pool.wait_ge(ms_ready, 1)
                    nc.gpsimd.tensor_tensor(rstd[:, t], ms[:, t], g.minus_half[:, 0:TPC], ALU.pow).then_inc(rstd_ready, 1)
                scale_raw(nc, pool, g, NC + c)
            if phase == 4:
                pool.wait_ge(vare_ready, c + 1)
                nc.gpsimd.tensor_tensor(rs[:, c % 2, :], vare[:, c % 2, :], g.minus_half[:, 0:TPC], ALU.pow).then_inc(rs_ready, 1)
        scale_raw(nc, pool, g, E)

    def scalar(act):
        for c, phase in plan:
            if phase == 0 and c == NC - 1:
                for i in range(TPC):
                    t = c * TPC + i
                    nc.scalar.activation(junk[:, :], g.x1[:, t, :], ACT.Square, accum_out=ss[:, t:t + 1]).then_inc(ss_ready, 1)
                    act.wait_ge(ss_ready, i + 1)
            if phase == 1:
                high_part(nc, act, g, NC + c)
            if phase == 2:
                act.wait_ge(turned, c + 1)
                nc.scalar.activation(shifted(hT, c)[0], tr_bank(c), ACT.Copy,
                                     scale=g.cols[:, LN2:LN2 + 1]).then_inc(hT_ready, 1)
            if phase == 3:
                for k in range(HC):
                    n = c * HC + k
                    act.wait_ge(key_ready, n + 1)
                    if n >= 2:
                        act.wait_ge(sq_ready, n - 1)
                    nc.scalar.activation(relu[:, n % 2, :], key_bank(n), ACT.Relu).then_inc(relu_ready, 1)
                act.wait_ge(r_ready, c + 1)
                if c >= 2:
                    act.wait_ge(val_used, c - 1)
                nc.scalar.activation(th[:, c % 2, :], r_ps, ACT.Tanh, scale=0.5).then_inc(th_ready, 1)

    def vector(dve):
        link = chain(dve, dve_step)
        nc.vector.memset(hT[:, :, 0:1], 0.0).then_inc(zero_ready, 1)
        dve.wait_ge(zero_ready, 1)
        for c, phase in plan:
            h, sh = shifted(hT, c)
            rows = slice(c * TPC, (c + 1) * TPC)
            if phase == 0 and c == NC - 1:
                dve.wait_ge(ss_ready, TPC)
                nc.vector.tensor_scalar(ms[:, rows], ss[:, rows], 1.0 / C, RMS_EPS, ALU.mult, ALU.add).then_inc(ms_ready, 1)
            if phase == 1:
                if c == NC - 1:
                    dve.wait_ge(rstd_ready, 1)
                if c >= 2:
                    dve.wait_ge(turned, c - 1)
                for i in range(TPC):
                    t = c * TPC + i
                    last = nc.vector.tensor_scalar(hx[:, c % 2, i, :], g.x1[:, t, :], rstd[:, t:t + 1], None, ALU.mult)
                last.then_inc(hx_ready, 1)
            if phase == 2:
                dve.wait_ge(hT_ready, c + 1)
                if c >= 2:
                    dve.wait_ge(r_ready, c - 1)
                link(nc.vector.tensor_tensor(diff[:, :], h, sh, ALU.subtract))
                for i, m in enumerate((MIXK2, MIXR2)):
                    last = nc.vector.scalar_tensor_tensor(out=xm[:, c % 2, i, :], in0=diff[:, :], scalar=g.cols[:, m:m + 1],
                                                          in1=sh, op0=ALU.mult, op1=ALU.add)
                last.then_inc(xm_ready, 1)
                dve.wait_ge(xm_ready, c + 1)
            if phase == 3:
                if c >= 2:
                    dve.wait_ge(val_ready, c - 1)
                for k in range(HC):
                    n = c * HC + k
                    dve.wait_ge(relu_ready, n + 1)
                    nc.vector.tensor_tensor(sq[c % 2][:, k, :], relu[:, n % 2, :], relu[:, n % 2, :], ALU.mult).then_inc(sq_ready, 1)
            if phase == 4:
                zc = z[:, c % 2, :]
                dve.wait_ge(th_ready, c + 1)
                dve.wait_ge(val_ready, c + 1)
                nc.vector.scalar_tensor_tensor(out=zc, in0=th[:, c % 2, :], scalar=1.0, in1=val_bank(c),
                                               op0=ALU.add, op1=ALU.mult).then_inc(val_used, 1)
                dve.wait_ge(val_used, c + 1)
                link(nc.vector.scalar_tensor_tensor(out=zc, in0=zc, scalar=0.5, in1=g.x1[:, rows, :].rearrange("p t c -> p (t c)"),
                                                    op0=ALU.mult, op1=ALU.add))
                link(nc.vector.tensor_tensor(zc, zc, g.x0[:, rows, :].rearrange("p t c -> p (t c)"), ALU.add))
                for i in range(TPC):
                    last = nc.vector.bn_stats(stats[:, i, :], zc[:, i * C:(i + 1) * C])
                link(last)
                for i in range(TPC):
                    last = nc.vector.bn_aggr(mv[:, c % 2, i, :], stats[:, i, :])
                link(last)
                if c >= 2:
                    dve.wait_ge(rs_ready, c - 1)
                nc.vector.tensor_scalar(vare[:, c % 2, :], mv[:, c % 2, :, 1], LN_EPS, None, ALU.add).then_inc(vare_ready, 1)
            if phase == 5:
                dve.wait_ge(rs_ready, c + 1)
                for i in range(TPC):
                    last = nc.vector.tensor_scalar(g.x0[:, c * TPC + i, :], z[:, c % 2, i * C:(i + 1) * C],
                                                   mv[:, c % 2, i, 0:1], rs[:, c % 2, i:i + 1], ALU.subtract, ALU.mult)
                last.then_inc(normed, 1)
                dve.wait_ge(normed, c + 1)

    def tensor(pe):
        for c, phase in plan:
            if phase == 1:
                pe.wait_ge(hx_ready, c + 1)
                if c >= 2:
                    pe.wait_ge(hT_ready, c - 1)
                for i in range(TPC):
                    last = nc.tensor.transpose(tr_bank(c)[:, i * P:(i + 1) * P], hx[:, c % 2, i, :], g.ident[:, :])
                last.then_inc(turned, 1)
            if phase == 2:
                if c == 0:
                    pe.wait_ge(w_in, 48)
                pe.wait_ge(xm_ready, c + 1)
                for k in range(HC):
                    n = c * HC + k
                    if n >= 2:
                        pe.wait_ge(relu_ready, n - 1)
                    nc.tensor.matmul(key_bank(n), w_k[:, k * P:(k + 1) * P], xm[:, c % 2, 0, :],
                                     start=True, stop=True).then_inc(key_ready, 1)
                if c >= 1:
                    pe.wait_ge(th_ready, c)
                for i in range(TPC):
                    last = nc.tensor.matmul(r_ps[:, i * P:(i + 1) * P], xm[:, c % 2, 1, i * P:(i + 1) * P], w_r[:, :],
                                            start=True, stop=True)
                last.then_inc(r_ready, 1)
            if phase == 3:
                if c >= 2:
                    pe.wait_ge(val_used, c - 1)
                pe.wait_ge(sq_ready, HC * (c + 1))
                for i in range(TPC):
                    for k in range(HC):
                        last = nc.tensor.matmul(val_bank(c)[:, i * P:(i + 1) * P], sq[c % 2][:, k, i * P:(i + 1) * P],
                                                w_v[:, k, :], start=(k == 0), stop=(k == HC - 1))
                last.then_inc(val_ready, 1)

    stage.sync = sync
    stage.gpsimd = gpsimd
    stage.scalar = scalar
    stage.vector = vector
    stage.tensor = tensor
    return stage


def route(nc, g, a, m, ctx, before, following):
    stage = Shared()

    def sb(name, shape, dt=F32):
        return ctx.enter_context(nc.sbuf_tensor(name, shape, dt))

    def sem(name):
        return ctx.enter_context(nc.semaphore(name))

    xT = sb("xT", [P, N])
    w_g = sb("w_g", [P, E])
    b2 = sb("b2", [E, C])
    logit = sb("logit", [P, NT, E])
    rest = sb("rest", [P, NT, E])
    rank = sb("rank", [P, NT, E])
    tied = sb("tied", [P, NT, E])
    top = sb("top", [P, TOPK, NT])
    topr = sb("topr", [P, NT])
    onehot = sb("onehot", [P, E, TOPK, NT])
    keep = sb("keep", [P, E, TOPK, NT])
    upper = sb("upper", [P, P])
    ones = sb("ones", [P, P])
    resets = sb("resets", [P, E, TOPK * NT])
    upto = sb("upto", [P, E, TOPK, NT])
    gap = sb("gap", [P, NT])
    egap = sb("egap", [P, NT])
    esum = sb("esum", [P, NT])
    wk = sb("wk", [P, TOPK, NT])
    gT = sb("gT", [E, N])
    pb = g.pb
    tr_bank = lambda c: pb[:, 4 if c % 2 else 7, :]
    logit_ps = pb[:, 6, 0:NT * E].rearrange("p (t e) -> p t e", e=E)
    within_ps = pb[:, 5, 0:E * TOPK * NT]
    total_ps = pb[:, 5, 256:256 + E * TOPK * NT]

    w_in = sem("ro_w_in")
    turned = sem("ro_turned")
    xT_ready = sem("ro_xT_ready")
    xh_ready = sem("ro_xh_ready")
    logit_ready = sem("ro_logit_ready")
    consts_ready = sem("ro_consts_ready")
    onehot_ready = sem("ro_onehot_ready")
    counts_ready = sem("ro_counts_ready")
    gap_ready = sem("ro_gap_ready")
    egap_ready = sem("ro_egap_ready")
    gate_ready = sem("ro_gate_ready")
    gate_turned = sem("ro_gate_turned")
    gT_ready = sem("ro_gT_ready")
    bias_ready = sem("ro_bias_ready")
    bias_used = sem("ro_bias_used")
    xl_ready = sem("ro_xl_ready")
    dve_step = sem("ro_dve_step")

    def sync(sp):
        sp.dma_start(w_g[:, :], a.wg).then_inc(w_in, 16)
        sp.dma_start(b2[:, :], a.b2).then_inc(w_in, 16)

    def gpsimd(pool):
        nc.gpsimd.memset(upper[:, :], 1.0).then_inc(consts_ready, 1)
        nc.gpsimd.memset(ones[:, :], 1.0).then_inc(consts_ready, 1)
        nc.gpsimd.memset(resets[:, :, :], 1.0).then_inc(consts_ready, 1)
        nc.gpsimd.iota(rank[:, :, :], pattern=[[0, NT], [-1, E]], base=E, channel_multiplier=0,
                       allow_small_or_imprecise_dtypes=True).then_inc(consts_ready, 1)
        pool.wait_ge(consts_ready, 4)
        nc.gpsimd.affine_select(out=upper[:, :], in_=upper[:, :], compare_op=ALU.is_ge, fill=0.0,
                                base=0, pattern=[[1, P]], channel_multiplier=-1).then_inc(consts_ready, 1)
        nc.gpsimd.memset(resets[:, :, 0:1], 0.0).then_inc(consts_ready, 1)

    def scalar(act):
        for c in range(NC):
            cols = slice(c * CH, (c + 1) * CH)
            act.wait_ge(turned, c + 1)
            nc.scalar.activation(xT[:, cols], tr_bank(c), ACT.Copy).then_inc(xT_ready, 1)
            nc.scalar.activation(g.xh[:, cols], tr_bank(c), ACT.Copy).then_inc(xh_ready, 1)
        following.begin_scalar(act)
        act.wait_ge(gap_ready, 1)
        nc.scalar.activation(egap[:, :], gap[:, :], ACT.Exp).then_inc(egap_ready, 1)

    def vector(dve):
        link = chain(dve, dve_step)
        following.begin_vector(dve)
        for c in range(NC):
            cols = slice(c * CH, (c + 1) * CH)
            dve.wait_ge(xh_ready, c + 1)
            nc.vector.tensor_tensor(g.xl[:, cols], xT[:, cols], g.xh[:, cols], ALU.subtract).then_inc(xl_ready, 1)
        dve.wait_ge(consts_ready, 6)
        dve.wait_ge(logit_ready, 1)
        link(nc.vector.tensor_copy(logit[:, :, :], logit_ps))
        src = logit
        for k in range(TOPK):
            oh = onehot[:, :, k, :].rearrange("p e t -> p t e")
            link(nc.vector.tensor_reduce(top[:, k, :], src[:, :, :], AX.X, ALU.max))
            link(nc.vector.tensor_tensor(tied[:, :, :], src[:, :, :], top[:, k, :].rearrange("p (t o) -> p t o", o=1)
                                         .broadcast_to([P, NT, E]), ALU.is_equal))
            link(nc.vector.tensor_tensor(tied[:, :, :], tied[:, :, :], rank[:, :, :], ALU.mult))
            link(nc.vector.tensor_reduce(topr[:, :], tied[:, :, :], AX.X, ALU.max))
            link(nc.vector.tensor_tensor(oh, tied[:, :, :], topr[:, :].rearrange("p (t o) -> p t o", o=1)
                                         .broadcast_to([P, NT, E]), ALU.is_equal))
            if k == 0:
                link(nc.vector.scalar_tensor_tensor(out=rest[:, :, :], in0=oh, scalar=-3e38, in1=logit[:, :, :],
                                                    op0=ALU.mult, op1=ALU.add))
                src = rest
        nc.vector.tensor_tensor(gap[:, :], top[:, 1, :], top[:, 0, :], ALU.subtract).then_inc(gap_ready, 1)
        dve.sem_inc(onehot_ready, 1)
        dve.wait_ge(counts_ready, 1)
        flat = lambda buf: buf[:, :, :, :].rearrange("p e k t -> p (e k t)")
        link(nc.vector.tensor_tensor_scan(flat(upto), resets[:, :, :].rearrange("p e n -> p (e n)"), total_ps, 0.0,
                                          ALU.mult, ALU.add))
        link(nc.vector.tensor_tensor(flat(upto), flat(upto), total_ps, ALU.subtract))
        link(nc.vector.tensor_tensor(flat(upto), flat(upto), within_ps, ALU.add))
        link(nc.vector.scalar_tensor_tensor(out=flat(keep), in0=flat(upto), scalar=float(CAP), in1=flat(onehot),
                                            op0=ALU.is_le, op1=ALU.mult))
        dve.wait_ge(egap_ready, 1)
        link(nc.vector.tensor_scalar(esum[:, :], egap[:, :], 1.0, None, ALU.add))
        link(nc.vector.reciprocal(wk[:, 0, :], esum[:, :]))
        link(nc.vector.tensor_tensor(wk[:, 1, :], egap[:, :], wk[:, 0, :], ALU.mult))
        for k in range(TOPK):
            last = nc.vector.tensor_tensor(keep[:, :, k, :], keep[:, :, k, :],
                                           wk[:, k, :].rearrange("p (o t) -> p o t", o=1).broadcast_to([P, E, NT]), ALU.mult)
        link(last)
        nc.vector.tensor_tensor(g.gate[:, :, :], keep[:, :, 0, :], keep[:, :, 1, :], ALU.add).then_inc(gate_ready, 1)
        dve.wait_ge(gate_ready, 1)
        link(nc.vector.tensor_scalar(g.gate_down[:, :, :], g.gate[:, :, :], 1.0 / W_SCALE, None, ALU.mult))

    def tensor(pe):
        for c in range(NC):
            pe.wait_ge(before.normed, c + 1)
            if c == 1:
                pe.wait_ge(before.th_ready, NC)
            if c >= 2:
                pe.wait_ge(xh_ready, c - 1)
            for i in range(TPC):
                last = nc.tensor.transpose(tr_bank(c)[:, i * P:(i + 1) * P], g.x0[:, c * TPC + i, :], g.ident[:, :])
            last.then_inc(turned, 1)
        pe.wait_ge(w_in, 32)
        for t in range(NT):
            pe.wait_ge(xT_ready, t // TPC + 1)
            last = nc.tensor.matmul(logit_ps[:, t, :], xT[:, t * P:(t + 1) * P], w_g[:, :], start=True, stop=True)
        last.then_inc(logit_ready, 1)
        pe.wait_ge(xl_ready, 1)
        following.begin_tensor(pe)
        pe.wait_ge(consts_ready, 6)
        pe.wait_ge(onehot_ready, 1)
        oh = onehot[:, :, :, :].rearrange("p e k t -> p (e k t)")
        nc.tensor.matmul(within_ps, upper[:, :], oh, start=True, stop=True)
        nc.tensor.matmul(total_ps, ones[:, :], oh, start=True, stop=True).then_inc(counts_ready, 1)

    gate_bank, bias_ps = pb[:, 7, :], pb[:, 6, :]

    def turn_gate(pe, c):
        pe.wait_ge(gate_ready, 1)
        for i in range(TPC):
            last = nc.tensor.transpose(gate_bank[0:E, i * P:(i + 1) * P], g.gate[:, :, c * TPC + i], g.ident[:, :])
        last.then_inc(gate_turned, 1)

    def take_gate(act, c):
        act.wait_ge(gate_turned, c + 1)
        nc.scalar.activation(gT[:, c * CH:(c + 1) * CH], gate_bank[0:E, :], ACT.Copy).then_inc(gT_ready, 1)

    def bias(pe, c):
        pe.wait_ge(gT_ready, c + 1)
        if c >= 1:
            pe.wait_ge(bias_used, c)
        for i in range(TPC):
            t = c * TPC + i
            last = nc.tensor.matmul(bias_ps[:, i * P:(i + 1) * P], gT[:, t * P:(t + 1) * P], b2[:, :], start=True, stop=True)
        last.then_inc(bias_ready, 1)

    def take_bias(dve, c):
        rows = slice(c * TPC, (c + 1) * TPC)
        dve.wait_ge(bias_ready, c + 1)
        nc.vector.tensor_tensor(g.moe[:, rows, :].rearrange("p t c -> p (t c)"), bias_ps,
                                g.x0[:, rows, :].rearrange("p t c -> p (t c)"), ALU.add).then_inc(bias_used, 1)
        dve.wait_ge(bias_used, c + 1)

    def beside_tensor(pe, c, part):
        if part == 0 and c == 0:
            turn_gate(pe, 0)
        if part == 1:
            bias(pe, c)
            if c < NC - 1:
                turn_gate(pe, c + 1)

    def beside_scalar(act, c, part):
        if part == 0 and c == 0:
            take_gate(act, 0)
        if part == 1 and c < NC - 1:
            take_gate(act, c + 1)

    def beside_vector(dve, c, part):
        if part == 0:
            take_bias(dve, c)

    stage.beside_tensor = beside_tensor
    stage.beside_scalar = beside_scalar
    stage.beside_vector = beside_vector
    stage.sync = sync
    stage.gpsimd = gpsimd
    stage.scalar = scalar
    stage.vector = vector
    stage.tensor = tensor
    return stage



def experts(nc, g, a, m, ctx):
    stage = Shared()

    def sb(name, shape, dt=F32):
        return ctx.enter_context(nc.sbuf_tensor(name, shape, dt))

    def sem(name):
        return ctx.enter_context(nc.semaphore(name))

    RING = 4
    h32 = sb("h32", [P, RING, CH])
    hh = sb("hh", [P, 2, HC, CH], F16)
    b1_now = sb("b1_now", [P, HC])
    hl = sb("hl", [P, 2, HC, CH], F16)
    pb = g.pb
    hid_bank = lambda n: pb[:, n % RING, :]
    out_bank = lambda c: pb[:, 4 + c % 2, :]
    hid_ready = sem("ex_hid_ready")
    b1_ready = sem("ex_b1_ready")
    hh_ready = sem("ex_hh_ready")
    hl_ready = sem("ex_hl_ready")
    out_ready = sem("ex_out_ready")
    out_used = sem("ex_out_used")

    def chunks(step, e, final, beside=None):
        for c in range(NC):
            if c < NC - 1:
                step(0, e, c + 1)
            elif not final:
                step(0, e + 1, 0)
            if beside:
                beside(c, 0)
            step(1, e, c)
            if beside:
                beside(c, 1)

    def every_expert(eng, step, beside):
        chunks(step, 0, False, beside)
        with eng.Fori(1, E - 1) as e:
            chunks(step, e, False)
        chunks(step, E - 1, True)

    def step_tensor(pe, layer, e, c):
        q = e * NC + c
        if layer == 0:
            x = slice(c * CH, (c + 1) * CH)
            for k in range(HC):
                pe.wait_ge(hh_ready, q * HC + k + 1)
                w = slice(k * P, (k + 1) * P)
                for i, (lhs, rhs) in enumerate(((g.w0h, g.xh), (g.w0h, g.xl), (g.w0l, g.xh))):
                    last = nc.tensor.matmul(hid_bank(k), lhs[:, bass.ds(e, 1), w], rhs[:, x], start=(i == 0), stop=(i == 2))
                last.then_inc(hid_ready, 1)
        else:
            pe.wait_ge(hl_ready, q * HC + (RING + HC))
            pe.wait_ge(out_used, q + 1)
            for i in range(TPC):
                tok = slice(i * P, (i + 1) * P)
                for k in range(HC):
                    w2 = slice(H + k * P, H + (k + 1) * P)
                    for j, (lhs, rhs) in enumerate(((hh, g.w0h), (hh, g.w0l), (hl, g.w0h))):
                        last = nc.tensor.matmul(out_bank(c)[:, tok], lhs[:, c % 2, k, tok], rhs[:, bass.ds(e, 1), w2],
                                                start=(k == 0 and j == 0), stop=(k == HC - 1 and j == 2))
            last.then_inc(out_ready, 1)

    def begin_tensor(pe):
        pe.sem_inc(out_ready, 2)
        step_tensor(pe, 0, 0, 0)

    def tensor(pe, before):
        every_expert(pe, lambda layer, e, c: step_tensor(pe, layer, e, c), lambda c, part: before.beside_tensor(pe, c, part))

    def step_scalar(act, layer, e, c):
        if layer == 0:
            q = e * NC + c
            act.wait_ge(b1_ready, e + 1)
            act.wait_ge(out_ready, q + 1)
            for k in range(HC):
                n = q * HC + k
                b1 = b1_now[:, k:k + 1]
                act.wait_ge(hid_ready, n + 1)
                act.wait_ge(hl_ready, n + 1)
                nc.scalar.activation(h32[:, k, :], hid_bank(k), ACT.Relu, scale=1.0 / W_SCALE, bias=b1)
                nc.scalar.activation(hh[:, c % 2, k, :], hid_bank(k), ACT.Relu, scale=1.0 / W_SCALE,
                                     bias=b1).then_inc(hh_ready, 1)

    def begin_scalar(act):
        act.sem_inc(hh_ready, RING)
        step_scalar(act, 0, 0, 0)

    def scalar(act, before):
        every_expert(act, lambda layer, e, c: step_scalar(act, layer, e, c), lambda c, part: before.beside_scalar(act, c, part))

    def vector(dve, before):
        def step(layer, e, c):
            q = e * NC + c
            if layer == 0:
                if c == 0 and not (isinstance(e, int) and e == 0):
                    dve.wait_ge(hh_ready, q * HC + RING)
                    nc.vector.tensor_scalar(b1_now[:, :], g.cols[:, bass.ds(e * HC + B1, HC)], 1.0, None, ALU.mult).then_inc(b1_ready, 1)
                for k in range(HC):
                    dve.wait_ge(hh_ready, q * HC + (k + 1 + RING))
                    nc.vector.tensor_tensor(hl[:, c % 2, k, :], h32[:, k, :], hh[:, c % 2, k, :], ALU.subtract).then_inc(hl_ready, 1)
            else:
                dve.wait_ge(out_ready, q + 3)
                for i in range(TPC):
                    t = c * TPC + i
                    last = nc.vector.scalar_tensor_tensor(
                        out=g.moe[:, t, :], in0=out_bank(c)[:, i * C:(i + 1) * C], scalar=g.gate_down_flat[:, bass.ds(e * NT + t, 1)],
                        in1=g.moe[:, t, :], op0=ALU.mult, op1=ALU.add)
                last.then_inc(out_used, 1)

        step(0, 0, 0)
        every_expert(dve, step, lambda c, part: before.beside_vector(dve, c, part))

    def begin_vector(dve):
        dve.sem_inc(hl_ready, RING)
        dve.sem_inc(out_used, 2)
        nc.vector.tensor_scalar(b1_now[:, :], g.cols[:, B1:B1 + HC], 1.0, None, ALU.mult).then_inc(b1_ready, 1)

    stage.begin_scalar = begin_scalar
    stage.begin_vector = begin_vector
    stage.begin_tensor = begin_tensor
    stage.scalar = scalar
    stage.vector = vector
    stage.tensor = tensor
    return stage


def layer0_rest(nc, g, a):
    with ExitStack() as ctx:
        m = Shared()
        m.sq = [buf[:, :, :, :, :].rearrange("p g t h d -> p (g t h d)").rearrange("p (k n) -> p k n", k=HC) for buf in (g.q, g.v)]
        m.relu, m.th = (g.ctx[:, i * NG // 2:(i + 1) * NG // 2, :, :, :].rearrange("p g t h d -> p (g t h d)")
                        .rearrange("p (a n) -> p a n", a=2) for i in range(2))
        cm = channel_mix(nc, g, a, m, ctx)
        ex = experts(nc, g, a, m, ctx)
        ro = route(nc, g, a, m, ctx, cm, ex)
        block = ctx.enter_context(nc.Block())

        @block.sync
        def _(sp):
            cm.sync(sp)
            ro.sync(sp)

        @block.gpsimd
        def _(pool):
            cm.gpsimd(pool)
            ro.gpsimd(pool)

        @block.scalar
        def _(act):
            cm.scalar(act)
            ro.scalar(act)
            ex.scalar(act, ro)

        @block.vector
        def _(dve):
            cm.vector(dve)
            ro.vector(dve)
            ex.vector(dve, ro)

        @block.tensor
        def _(pe):
            cm.tensor(pe)
            ro.tensor(pe)
            ex.tensor(pe, ro)


def project(nc, g, a, m, ctx):
    stage = Shared()

    def sb(name, shape, dt=F32):
        return ctx.enter_context(nc.sbuf_tensor(name, shape, dt))

    def sem(name):
        return ctx.enter_context(nc.semaphore(name))

    NB = 2 * C + HASH
    w_raw, w_T = m.w_raw, m.w_T
    brow = sb("pj_brow", [1, NB])
    one_row = sb("pj_one_row", [1, P])
    ones = sb("pj_ones", [P, P])
    bcast = sb("pj_bcast", [P, NB])
    stats = sb("pj_stats", [P, TPC, 6])
    mv = sb("pj_mv", [P, 2, TPC, 2])
    vare = sb("pj_vare", [P, 2, TPC])
    rs = sb("pj_rs", [P, 2, TPC])
    xT = m.xT_project
    squares = m.squares
    hashed = g.ctx
    half = sb("pj_half", [P, NG * HPG])
    nsq = sb("pj_nsq", [P, NG, GT, HPG])
    qa = sb("pj_qa", [P, NG, GT, HPG])
    tmp = sb("pj_tmp", [P, NG, GT, HPG])
    nsq2 = sb("pj_nsq2", [P, NG, GT, HPG])
    pk = sb("pj_pk", [P, NG, GT, HPG])
    hq = sb("pj_hq", [P, NG, GT, HPG])
    hk = sb("pj_hk", [P, NG, GT, HPG])
    mx = sb("pj_mx", [P, NG, HPG])
    mxall = sb("pj_mxall", [P, NG, HPG])
    sc = sb("pj_sc", [P, 3, NG, HPG])
    longest = sb("pj_longest", [P, 1])
    n1 = sb("pj_n1", [P, NG, HPG])
    none = sb("pj_none", [P, 3, NG, HPG])
    pb = g.pb
    tr_bank = lambda c: pb[:, c % 2, :]
    qkv_ps = lambda c: pb[:, 2 + 2 * (c % 2):4 + 2 * (c % 2), :].rearrange("p a n -> p (a n)").rearrange("p (t m) -> p t m", m=2 * C)

    w_in = sem("pj_w_in")
    brow_in = sem("pj_brow_in")
    ones_ready = sem("pj_ones_ready")
    w_turned = sem("pj_w_turned")
    bcast_done = sem("pj_bcast_done")
    consts_ready = sem("pj_consts_ready")
    vare_ready = sem("pj_vare_ready")
    rs_ready = sem("pj_rs_ready")
    x_ready = sem("pj_x_ready")
    turned = sem("pj_turned")
    xT_ready = sem("pj_xT_ready")
    qkv_ready = sem("pj_qkv_ready")
    qkv_used = sem("pj_qkv_used")
    mx_ready = sem("pj_mx_ready")
    mxall_ready = sem("pj_mxall_ready")
    s2_ready = sem("pj_s2_ready")
    squares_ready = sem("pj_squares_ready")
    hashed_ready = sem("pj_hashed_ready")
    s_ready = sem("pj_s_ready")
    hk_ready = sem("pj_hk_ready")
    counts_ready = sem("pj_counts_ready")
    dve_step = sem("pj_dve_step")

    plan = schedule(NC, (3, 2, 1, 0))
    late_plan = schedule(NC, (2, 0, 3, 1))

    def of_chunk(buf, c):
        b, t0 = c // CPB, (c % CPB) * TPC
        part = buf[:, b * HG:(b + 1) * HG, t0:t0 + TPC]
        return part.rearrange("p g t h d -> p g (t h) d") if len(buf.shape) == 5 else part.rearrange("p g t h -> p g (t h)")

    def sync(sp):
        sp.dma_start(w_raw[:, 0, :], a.qk_w).then_inc(w_in, 16)
        sp.dma_start(w_raw[:, 1, :], a.v_w).then_inc(w_in, 16)
        for lo, v in ((0, a.qk_b), (C, a.v_b), (2 * C, a.hash_a)):
            sp.dma_start(brow[:, lo:lo + v.shape[0]], v.rearrange("(a n) -> a n", a=1)).then_inc(brow_in, 16)

    def gpsimd(pool):
        nc.gpsimd.memset(one_row[:, :], 1.0).then_inc(ones_ready, 1)
        nc.gpsimd.memset(ones[:, :], 1.0).then_inc(ones_ready, 1)
        nc.gpsimd.memset(half[:, :], 0.5).then_inc(ones_ready, 1)
        pool.wait_ge(ones_ready, 3)
        for c, phase in late_plan:
            if phase == 0:
                pool.wait_ge(vare_ready, c + 1)
                nc.gpsimd.tensor_tensor(rs[:, c % 2, :], vare[:, c % 2, :], g.minus_half[:, 0:TPC], ALU.pow).then_inc(rs_ready, 1)
            if phase == 3:
                pool.wait_ge(qkv_used, c + 1)
                weights = bcast[:, 2 * C:2 * C + DH].rearrange("p (g n d) -> p g n d", g=1, n=1)
                nc.gpsimd.tensor_tensor(of_chunk(hashed, c), of_chunk(g.q, c), weights.broadcast_to([P, HG, TPC * HPG, DH]),
                                        ALU.mult).then_inc(hashed_ready, 1)
        heads = lambda buf: buf.rearrange("p g h -> p (g h)")
        clear_sides(nc, pool, m)
        pool.wait_ge(mx_ready, 1)
        nc.gpsimd.partition_all_reduce(heads(mxall[:, :, :]), heads(mx[:, :, :]), P,
                                       bass.bass_isa.ReduceOp.max).then_inc(mxall_ready, 1)
        pool.wait_ge(s2_ready, 1)
        nc.gpsimd.tensor_tensor(heads(sc[:, 0, :, :]), heads(sc[:, 1, :, :]), half[:, :], ALU.pow).then_inc(s_ready, 1)

    def scalar(act):
        for c, phase in late_plan:
            if phase == 2:
                act.wait_ge(turned, c + 1)
                if c >= 2:
                    act.wait_ge(qkv_ready, c - 1)
                nc.scalar.activation(xT[:, c % 2, :], tr_bank(c), ACT.Copy).then_inc(xT_ready, 1)
            if phase == 3:
                act.wait_ge(qkv_used, c + 1)
                nc.scalar.activation(of_chunk(squares, c), of_chunk(g.q, c), ACT.Square).then_inc(squares_ready, 1)

    def vector(dve):
        link = chain(dve, dve_step)
        for c, phase in plan:
            if phase == 0:
                for i in range(TPC):
                    last = nc.vector.bn_stats(stats[:, i, :], g.moe[:, c * TPC + i, :])
                link(last)
                for i in range(TPC):
                    last = nc.vector.bn_aggr(mv[:, c % 2, i, :], stats[:, i, :])
                link(last)
                nc.vector.tensor_scalar(vare[:, c % 2, :], mv[:, c % 2, :, 1], LN_EPS, None, ALU.add).then_inc(vare_ready, 1)
            if phase == 1:
                dve.wait_ge(rs_ready, c + 1)
                for i in range(TPC):
                    t = c * TPC + i
                    last = nc.vector.tensor_scalar(g.x0[:, t, :], g.moe[:, t, :], mv[:, c % 2, i, 0:1], rs[:, c % 2, i:i + 1],
                                                   ALU.subtract, ALU.mult)
                last.then_inc(x_ready, 1)
                dve.wait_ge(x_ready, c + 1)
                if c == 0:
                    dve.wait_ge(w_turned, 1)
                    nc.vector.tensor_copy(w_T[:, :], pb[:, 6, 0:2 * C]).then_inc(consts_ready, 1)
                    dve.wait_ge(bcast_done, 1)
                    nc.vector.tensor_copy(bcast[:, :], pb[:, 7, 0:NB]).then_inc(consts_ready, 1)
                    dve.wait_ge(consts_ready, 2)
            if phase == 3:
                b, t0 = c // CPB, (c % CPB) * TPC
                dve.wait_ge(qkv_ready, c + 1)
                for i in range(TPC):
                    for j, dst in enumerate((g.q, g.v)):
                        last = nc.vector.tensor_tensor(
                            dst[:, b * HG:(b + 1) * HG, t0 + i, :, :].rearrange("p g h d -> p g (h d)"),
                            qkv_ps(c)[:, i, j * C:(j + 1) * C].rearrange("p (g n) -> p g n", g=HG),
                            bcast[:, j * C:(j + 1) * C].rearrange("p (g n) -> p g n", g=HG), ALU.add)
                last.then_inc(qkv_used, 1)
        every = lambda buf: buf[:, :, :, :].rearrange("p g t h -> p (g t h)")
        rowsof = lambda buf: buf[:, :, :, :, :].rearrange("p g t h d -> p (g t h) d")
        per_head = lambda buf: buf.rearrange("p g (o h) -> p g o h", o=1).broadcast_to([P, NG, GT, HPG])
        dve.wait_ge(squares_ready, NC)
        link(nc.vector.tensor_reduce(every(nsq), rowsof(squares), AX.X, ALU.add))
        nc.vector.tensor_reduce(mx[:, :, :], nsq[:, :, :, :].rearrange("p g t h -> p g h t"), AX.X, ALU.max).then_inc(mx_ready, 1)
        dve.wait_ge(hashed_ready, NC)
        link(nc.vector.tensor_reduce(every(qa), rowsof(hashed), AX.X, ALU.add))
        dve.wait_ge(mxall_ready, 1)
        link(nc.vector.tensor_scalar(sc[:, 0, :, :], mxall[:, :, :], 1e-24, None, ALU.max))
        link(nc.vector.reciprocal(sc[:, 2, :, :], sc[:, 0, :, :]))
        nc.vector.tensor_scalar(sc[:, 1, :, :], sc[:, 2, :, :], U_HASH ** 2, None, ALU.mult).then_inc(s2_ready, 1)
        link(nc.vector.tensor_reduce(longest[:, :], mxall[:, :, :].rearrange("p g h -> p (g h)"), AX.X, ALU.max))
        nc.vector.tensor_scalar(g.large[:, :], longest[:, :], SAFE_SCORE * DH ** 0.5, None, ALU.is_gt).then_inc(m.large_ready, 1)
        link(nc.vector.tensor_scalar(every(hq), every(qa), 0.0, None, ALU.is_ge))
        link(nc.vector.tensor_scalar(every(g.qbit), every(hq), 2.0, -1.0, ALU.mult, ALU.add))
        dve.wait_ge(s2_ready, 1)
        link(nc.vector.tensor_tensor(nsq2[:, :, :, :], nsq[:, :, :, :], per_head(sc[:, 1, :, :]), ALU.mult))
        link(nc.vector.tensor_tensor(every(tmp), every(nsq2), every(nsq2), ALU.mult))
        for i, part in enumerate((nsq2, tmp)):
            link(nc.vector.tensor_scalar(every(part), every(part), -1.0, 0.5, ALU.mult, ALU.add))
            link(nc.vector.tensor_scalar(every(part), every(part), bcast[:, 2 * C + DH + i:2 * C + DH + i + 1], None, ALU.mult))
        link(nc.vector.tensor_tensor(every(tmp), every(tmp), every(nsq2), ALU.add))
        dve.wait_ge(s_ready, 1)
        link(nc.vector.tensor_tensor(pk[:, :, :, :], qa[:, :, :, :], per_head(sc[:, 0, :, :]), ALU.mult))
        link(nc.vector.tensor_tensor(every(pk), every(pk), every(tmp), ALU.add))
        nc.vector.tensor_scalar(every(hk), every(pk), 0.0, None, ALU.is_ge).then_inc(hk_ready, 1)
        dve.wait_ge(hk_ready, 1)
        link(nc.vector.tensor_scalar(every(g.kbit), every(hk), MASK, -MASK / 2, ALU.mult, ALU.add))
        dve.wait_ge(counts_ready, 1)
        link(nc.vector.tensor_reduce(n1[:, :, :], pb[:, 5, 0:NG * GT * HPG].rearrange("p (g t h) -> p g h t", g=NG, t=GT), AX.X, ALU.add))
        link(nc.vector.tensor_scalar(none[:, 0, :, :], n1[:, :, :], 0.0, MASK, ALU.is_equal, ALU.mult))
        link(nc.vector.tensor_scalar(none[:, 1, :, :], n1[:, :, :], float(T), MASK, ALU.is_equal, ALU.mult))
        link(nc.vector.tensor_tensor(none[:, 2, :, :], none[:, 0, :, :], none[:, 1, :, :], ALU.subtract))
        link(nc.vector.tensor_tensor(tmp[:, :, :, :], hq[:, :, :, :], per_head(none[:, 2, :, :]), ALU.mult))
        link(nc.vector.tensor_tensor(g.lift[:, :, :, :], tmp[:, :, :, :], per_head(none[:, 1, :, :]), ALU.add))

    def tensor(pe):
        pe.wait_ge(w_in, 32)
        nc.tensor.transpose(pb[:, 6, 0:C], w_raw[:, 0, :], g.ident[:, :])
        nc.tensor.transpose(pb[:, 6, C:2 * C], w_raw[:, 1, :], g.ident[:, :]).then_inc(w_turned, 1)
        pe.wait_ge(ones_ready, 3)
        pe.wait_ge(brow_in, 48)
        nc.tensor.matmul(pb[:, 7, 0:NB], one_row[:, :], brow[:, :], start=True, stop=True).then_inc(bcast_done, 1)
        for c, phase in plan:
            if phase == 1:
                pe.wait_ge(x_ready, c + 1)
                if c >= 2:
                    pe.wait_ge(xT_ready, c - 1)
                for i in range(TPC):
                    last = nc.tensor.transpose(tr_bank(c)[:, i * P:(i + 1) * P], g.x0[:, c * TPC + i, :], g.ident[:, :])
                last.then_inc(turned, 1)
            if phase == 2:
                pe.wait_ge(consts_ready, 2)
                pe.wait_ge(xT_ready, c + 1)
                if c >= 2:
                    pe.wait_ge(qkv_used, c - 1)
                for i in range(TPC):
                    last = nc.tensor.matmul(qkv_ps(c)[:, i, :], xT[:, c % 2, i * P:(i + 1) * P], w_T[:, :], start=True, stop=True)
                last.then_inc(qkv_ready, 1)
        pe.wait_ge(hk_ready, 1)
        nc.tensor.matmul(pb[:, 5, 0:NG * GT * HPG], ones[:, :], hk[:, :, :, :].rearrange("p g t h -> p (g t h)"),
                         start=True, stop=True).then_inc(counts_ready, 1)
    stage.sync = sync
    stage.gpsimd = gpsimd
    stage.scalar = scalar
    stage.vector = vector
    stage.tensor = tensor
    return stage



def one_group(buf, G):
    if len(buf.shape) == 5:
        return buf[:, bass.ds(G, 1), :, :, :].rearrange("p o t h d -> p (o t h) d")
    return buf[:, bass.ds(G, 1), :, :].rearrange("p o t (h d) -> p (o t h) d", d=1)


def side_rows(buf, lo, n):
    return buf[:, :, :, lo:lo + n].rearrange("p t h d -> p (t h) d")


def clear_sides(nc, pool, m):
    nc.gpsimd.memset(m.qs[:, :, :, :], 0.0).then_inc(m.cleared, 1)
    nc.gpsimd.memset(m.ks[:, :, :, :], 0.0).then_inc(m.cleared, 1)
    nc.gpsimd.memset(m.va[:, :, :, :, :], 0.0).then_inc(m.cleared, 1)
    pool.wait_ge(m.cleared, 3)
    nc.gpsimd.memset(m.qs[:, :, :, 0:1], 1.0).then_inc(m.cleared, 1)
    nc.gpsimd.memset(m.ks[:, :, :, 0:1], -MASK / 2).then_inc(m.cleared, 1)
    nc.gpsimd.memset(m.ks[:, :, :, 2:4], 1.0).then_inc(m.cleared, 1)
    nc.gpsimd.memset(m.va[:, :, :, :, DH:DH + 1], 1.0).then_inc(m.cleared, 1)


def write_sides(nc, dve, g, G, qs, ks, scaled, step, ready, with_lift):
    flat = scaled[:, :, :, :].rearrange("p t h d -> p (t h) d")
    nc.vector.tensor_copy(side_rows(ks, 1, 1), one_group(g.kbit, G))
    nc.vector.tensor_copy(side_rows(qs, 1, 1), one_group(g.qbit, G))
    nc.vector.tensor_scalar(flat, one_group(g.q, G), DH ** -0.5, None, ALU.mult)
    if with_lift:
        nc.vector.tensor_copy(side_rows(qs, 2, 1).bitcast(F32R), one_group(g.lift, G))
    nc.vector.tensor_copy(side_rows(ks, 4, DH).bitcast(F32R), one_group(g.q, G)).then_inc(step, 1)
    dve.wait_ge(step, 2 * G + 1)
    nc.vector.tensor_copy(side_rows(ks, 4 + DH, DH), side_rows(ks, 4, DH))
    nc.vector.tensor_tensor(side_rows(ks, 4 + 2 * DH, DH), one_group(g.q, G), side_rows(ks, 4, DH), ALU.subtract)
    if with_lift:
        nc.vector.tensor_tensor(side_rows(qs, 3, 1), one_group(g.lift, G), side_rows(qs, 2, 1), ALU.subtract)
    nc.vector.tensor_copy(side_rows(qs, 4, DH).bitcast(F32R), flat).then_inc(step, 1)
    dve.wait_ge(step, 2 * G + 2)
    nc.vector.tensor_tensor(side_rows(qs, 4 + DH, DH), flat, side_rows(qs, 4, DH), ALU.subtract)
    nc.vector.tensor_copy(side_rows(qs, 4 + 2 * DH, DH), side_rows(qs, 4, DH)).then_inc(ready, 1)


def maxima(nc, g, a, m, ctx):
    stage = Shared()

    def sb(name, shape, dt=F32):
        return ctx.enter_context(nc.sbuf_tensor(name, shape, dt))

    def sem(name):
        return ctx.enter_context(nc.semaphore(name))

    qs, ks, scaled = m.qs, m.ks, m.scaled
    qT, kT = m.qT[:, 0, :], m.kT[:, 0, :]
    peak = sb("mx_peak", [P, GT, HPG])
    pb = g.pb
    place = lambda i: pb[:, 2 * i:2 * i + 2, :].rearrange("p a n -> p (a n)")
    USES = GT * HPG

    step = sem("mx_step")
    sides_ready = sem("mx_sides_ready")
    turned = sem("mx_turned")
    taken = sem("mx_taken")
    s_ready = sem("mx_s_ready")
    peak_ready = sem("mx_peak_ready")
    lift_ready = sem("mx_lift_ready")

    def vector(dve):
        dve.wait_ge(m.cleared, 7)
        dve.wait_ge(m.large_ready, 1)
        large = dve.value_load(g.large[0:1, 0:1])
        with dve.If(large > 0):
            with dve.Fori(0, NG) as G:
                write_sides(nc, dve, g, G, qs, ks, scaled, step, sides_ready, False)
                dve.wait_ge(turned, 2 * G + 2)
                nc.vector.tensor_copy(qT, place(2))
                nc.vector.tensor_copy(kT, place(3)).then_inc(taken, 1)
                for t in range(GT):
                    for h in range(HPG):
                        n = t * HPG + h
                        dve.wait_ge(s_ready, G * USES + (n + 1))
                        nc.vector.tensor_reduce(peak[:, t, h:h + 1], place(n % 2), AX.X, ALU.max).then_inc(peak_ready, 1)
                dve.wait_ge(peak_ready, G * USES + USES)
                nc.vector.tensor_scalar(one_group(g.lift, G), peak[:, :, :].rearrange("p t (h d) -> p (t h) d", d=1),
                                        -1.0, None, ALU.mult).then_inc(lift_ready, 1)
                dve.wait_ge(lift_ready, G + 1)

    def tensor(pe):
        pe.wait_ge(m.large_ready, 1)
        large = pe.value_load(g.large[0:1, 0:1])
        with pe.If(large > 0):
            with pe.Fori(0, NG) as G:
                pe.wait_ge(sides_ready, G + 1)
                for i, side in enumerate((qs, ks)):
                    for t in range(GT):
                        last = nc.tensor.transpose(place(2 + i)[:, t * P:(t + 1) * P],
                                                   side[:, t, :, :].rearrange("p h r -> p (h r)"), g.ident[:, :])
                    last.then_inc(turned, 1)
                pe.wait_ge(taken, G + 1)
                for t in range(GT):
                    for h in range(HPG):
                        n = t * HPG + h
                        if n >= 2:
                            pe.wait_ge(peak_ready, G * USES + (n - 1))
                        part = slice(h * AUG, (h + 1) * AUG)
                        for half in range(2):
                            cols = slice(half * CH, (half + 1) * CH)
                            last = nc.tensor.matmul(place(n % 2)[:, cols], qT[part, t * P:(t + 1) * P], kT[part, cols],
                                                    start=True, stop=True)
                        last.then_inc(s_ready, 1)
    stage.vector = vector
    stage.tensor = tensor
    return stage



def attend(nc, g, a, m, ctx, following):
    stage = Shared()

    def sb(name, shape, dt=F32):
        return ctx.enter_context(nc.sbuf_tensor(name, shape, dt))

    def sem(name):
        return ctx.enter_context(nc.semaphore(name))

    qs, ks, scaled, qT, kT, va, ex = m.qs, m.ks, m.scaled, m.qT, m.kT, m.va, m.ex
    oT = m.oT
    rden = sb("at_rden", [P, GT, HPG])
    raw1 = sb("at_raw1", [P, 2, 3 * H])
    pb = g.pb
    ring = lambda pos: pb[:, 2 * (pos % 3):2 * (pos % 3) + 2, :].rearrange("p a n -> p (a n)")
    pv_ps = pb[:, 6:8, :].rearrange("p a n -> p (a n)")

    prep_ready = sem("at_prep_ready")
    q_turned = sem("at_q_turned")
    k_turned = sem("at_k_turned")
    qT_ready = sem("at_qT_ready")
    kT_ready = sem("at_kT_ready")
    s_ready = sem("at_s_ready")
    exp_done = sem("at_exp_done")
    pv_done = sem("at_pv_done")
    oT_ready = sem("at_oT_ready")
    o_turned = sem("at_o_turned")
    o_ready = sem("at_o_ready")
    raw1_in = [sem(f"at_raw1_in{i}") for i in range(2)]
    raw1_used = sem("at_raw1_used")
    prep_step = sem("at_prep_step")
    rden_ready = sem("at_rden_ready")
    high_ready = sem("at_high_ready")

    uses = [("S", n) for n in range(GT * HPG)]
    uses.insert(8, ("O", 0))
    uses.insert(25, ("Q", 0))
    uses.insert(26, ("K", 0))
    assert len(uses) == 35
    POS = {kind: pos for pos, (kind, n) in enumerate(uses) if kind != "S"}
    LEN = 36

    def place_free(eng, G, pos, first, last):
        back = pos - 3
        if back < 0:
            if first:
                return
            back += LEN
            G = G - 1
            if back == LEN - 1:
                back -= 3
        kind, n = uses[back]
        if kind == "S":
            eng.wait_ge(exp_done, G * (GT * HPG) + (n + 1))
        if kind == "O" and not first:
            eng.wait_ge(o_ready, G)
        if kind == "Q" and not last:
            eng.wait_ge(qT_ready, G + 2)
        if kind == "Q" and last:
            eng.wait_ge(following.xh_ready, 1)
        if kind == "K" and not last:
            eng.wait_ge(kT_ready, G + 2)

    def take_out(dve, G, turned_ps):
        out = turned_ps.rearrange("p (t h r) -> p t h r", t=GT, h=HPG)
        dve.wait_ge(o_turned, G + 1)
        nc.vector.reciprocal(rden[:, :, :].rearrange("p t (h o) -> p t h o", o=1), out[:, :, :, DH:DH + 1]).then_inc(rden_ready, 1)
        dve.wait_ge(rden_ready, G + 1)
        rows = lambda buf: buf.rearrange("p t h d -> p (t h) d")
        nc.vector.tensor_tensor(
            g.ctx[:, bass.ds(G, 1), :, :, :].rearrange("p o t h d -> p (o t h) d"),
            rows(out[:, :, :, 0:DH]),
            rden[:, :, :].rearrange("p t (h o) -> p (t h) o", o=1).broadcast_to([P, GT * HPG, DH]), ALU.mult).then_inc(o_ready, 1)

    def turn_out(pe, G, to):
        pe.wait_ge(oT_ready, G + 1)
        for t in range(GT):
            last = nc.tensor.transpose(to[:, t * P:(t + 1) * P], oT[:, t * P:(t + 1) * P], g.ident[:, :])
        last.then_inc(o_turned, 1)

    def groups(eng, group):
        group(0, 0, True, False)
        with eng.Fori(0, (NG - 2) // 2) as i:
            group(2 * i + 1, 1, False, False)
            group(2 * i + 2, 0, False, False)
        group(NG - 1, 1, False, True)

    def sync(sp):
        for e in range(E):
            if e >= 2:
                sp.wait_ge(raw1_used, e - 1)
            for i, src in enumerate((a.Wg[e], a.Wu[e])):
                sp.dma_start(raw1[:, e % 2, i * H:(i + 1) * H], src).then_inc(raw1_in[e % 2], 16)
            sp.dma_start(raw1[:, e % 2, 2 * H:3 * H].rearrange("p (k c) -> p k c", k=HC),
                         a.Wd[e].rearrange("(k p) c -> p k c", p=P)).then_inc(raw1_in[e % 2], 16)

    def scalar(act):
        def group(G, par, first, last):
            for pos, (kind, n) in enumerate(uses):
                if kind == "S":
                    kt = n // HPG
                    act.wait_ge(s_ready, G * (GT * HPG) + (n + 1))
                    if n % HPG == 0 and not (first and kt < 2):
                        act.wait_ge(pv_done, G * GT + (kt - 1))
                    nc.scalar.activation(ex[:, kt % 2, n % HPG, :], ring(pos), ACT.Exp).then_inc(exp_done, 1)
                if kind == "Q" and last:
                    following.take_x(act, 0, ring(pos)[:, 0:CH])

        groups(act, group)

    def vector(dve):
        def prepare(G, par, first):
            if not first:
                dve.wait_ge(k_turned, G)
            nc.vector.tensor_copy(va[:, par, :, :, 0:DH].rearrange("p t h d -> p (t h) d"), one_group(g.v, G))
            write_sides(nc, dve, g, G, qs, ks, scaled, prep_step, prep_ready, True)

        def take_sides(G, par):
            dve.wait_ge(q_turned, G + 1)
            nc.vector.tensor_copy(qT[:, par, :], ring(POS["Q"])).then_inc(qT_ready, 1)
            dve.wait_ge(k_turned, G + 1)
            nc.vector.tensor_copy(kT[:, par, :], ring(POS["K"])).then_inc(kT_ready, 1)

        def take_pv(G):
            dve.wait_ge(pv_done, (G + 1) * GT)
            nc.vector.tensor_copy(oT[:, :], pv_ps).then_inc(oT_ready, 1)

        def split(G, par):
            raw = raw1[:, par, :]
            high, low = (buf[:, bass.ds(G, 1), :].rearrange("p o n -> p (o n)") for buf in (g.w1h, g.w1l))
            dve.wait_ge(raw1_in[par], (G - par) * 24 + 48)
            nc.vector.tensor_scalar(high, raw, W_SCALE, None, ALU.mult).then_inc(high_ready, 1)
            dve.wait_ge(high_ready, G + 1)
            nc.vector.scalar_tensor_tensor(out=low, in0=raw, scalar=W_SCALE, in1=high, op0=ALU.mult,
                                           op1=ALU.subtract).then_inc(raw1_used, 1)

        def group(G, par, first, last):
            if not first:
                take_pv(G - 1)
                take_out(dve, G - 1, ring(POS["O"]))
            if not last:
                prepare(G + 1, 1 - par, False)
                take_sides(G + 1, 1 - par)
            split(G, par)
            if last:
                following.norm_in_stats(dve, 0)
                following.norm_in(dve, 0)
                following.norm_in_stats(dve, 1)
                following.low_x(dve, 0)

        prepare(0, 0, True)
        take_sides(0, 0)
        groups(dve, group)
        take_pv(NG - 1)

    def last_out(dve):
        take_out(dve, NG - 1, pv_ps)

    def tensor(pe):
        def warm(count):
            for _ in range(count):
                nc.tensor.matmul(pv_ps[:, 0:CH], g.ident[:, :], g.x0[:, 0:TPC, :].rearrange("p t c -> p (t c)"), start=True, stop=True)

        def turn(src, kind, done):
            for t in range(GT):
                last = nc.tensor.transpose(ring(POS[kind])[:, t * P:(t + 1) * P],
                                           src[:, t, :, :].rearrange("p h r -> p (h r)"), g.ident[:, :])
            last.then_inc(done, 1)

        def values(G, par, kt, half, first):
            if half == 0:
                pe.wait_ge(exp_done, G * (GT * HPG) + (kt + 1) * HPG)
                if kt == 0 and not first:
                    pe.wait_ge(oT_ready, G)
            for h in range(HPG):
                cols = slice(half * CH, (half + 1) * CH)
                last = nc.tensor.matmul(pv_ps[h * AUG:(h + 1) * AUG, cols], va[:, par, kt, h, :], ex[:, kt % 2, h, cols],
                                        start=(kt == 0), stop=(kt == GT - 1))
            if half == 1:
                last.then_inc(pv_done, 1)

        def group(G, par, first, last_group):
            pe.wait_ge(kT_ready, G + 1)
            pe.wait_ge(qT_ready, G + 1)
            for pos, (kind, n) in enumerate(uses):
                if kind == "S":
                    kt, h = n // HPG, n % HPG
                    place_free(pe, G, pos, first, last_group)
                    part = slice(h * AUG, (h + 1) * AUG)
                    for half in range(2):
                        cols = slice(half * CH, (half + 1) * CH)
                        last = nc.tensor.matmul(ring(pos)[:, cols], kT[part, par, kt * P:(kt + 1) * P], qT[part, par, cols],
                                                start=True, stop=True)
                    last.then_inc(s_ready, 1)
                    if h in (1, 3):
                        if kt >= 1:
                            values(G, par, kt - 1, h // 2, first)
                        elif not first:
                            values(G - 1, 1 - par, GT - 1, h // 2, False)
                        else:
                            warm(1)
                if kind == "O" and not first:
                    place_free(pe, G, pos, first, last_group)
                    turn_out(pe, G - 1, ring(POS["O"]))
                if kind in "QK" and not last_group:
                    place_free(pe, G, pos, first, last_group)
                    if kind == "Q":
                        pe.wait_ge(prep_ready, G + 2)
                    turn(qs if kind == "Q" else ks, kind, q_turned if kind == "Q" else k_turned)
                if kind == "Q" and last_group:
                    place_free(pe, G, pos, first, last_group)
                    following.turn_x(pe, 0, ring(pos)[:, 0:CH])

        warm(5)
        pe.wait_ge(prep_ready, 1)
        turn(qs, "Q", q_turned)
        turn(ks, "K", k_turned)
        warm(1)
        groups(pe, group)
        values(NG - 1, 1, GT - 1, 0, False)
        values(NG - 1, 1, GT - 1, 1, False)

    def turn_last(pe):
        turn_out(pe, NG - 1, pv_ps)
    stage.sync = sync
    stage.scalar = scalar
    stage.last_out = last_out
    stage.turn_last = turn_last
    stage.vector = vector
    stage.tensor = tensor
    return stage


def feed(nc, g, a, m, ctx):
    stage = Shared()

    def sb(name, shape, dt=F32):
        return ctx.enter_context(nc.sbuf_tensor(name, shape, dt))

    def sem(name):
        return ctx.enter_context(nc.semaphore(name))

    LAG = 2
    STEPS = E * HC
    silu, h32, hh, hl, sums = m.silu, m.h32, m.hh, m.hl, m.sums
    eye = sb("fd_eye", [P, P], F16)
    xT, xn, z, y = m.xT, m.xn, m.z, m.y
    stats = sb("fd_stats", [P, TPC, 6])
    mv_in = sb("fd_mv_in", [P, TPC, 2])
    mv_out = sb("fd_mv_out", [P, TPC, 2])
    vare = sb("fd_vare", [P, 2, TPC])
    rs = sb("fd_rs", [P, 2, TPC])
    steps = [0]
    pb = g.pb
    gate_ps = lambda k: pb[:, 2 * (k % 2), :]
    up_ps = lambda k: pb[:, 2 * (k % 2) + 1, :]
    sum_ps = lambda c: pb[:, 4 + c % 2, :]
    turn_ps = pb[:, 6, :]

    eye_ready = sem("fd_eye_ready")
    in_vare_ready = sem("fd_in_vare_ready")
    in_rs_ready = sem("fd_in_rs_ready")
    x_ready = sem("fd_x_ready")
    x_turned = sem("fd_x_turned")
    xT_ready = sem("fd_xT_ready")
    xh_ready = sem("fd_xh_ready")
    xl_ready = sem("fd_xl_ready")
    gate_ready = sem("fd_gate_ready")
    up_ready = sem("fd_up_ready")
    silu_ready = sem("fd_silu_ready")
    h_ready = sem("fd_h_ready")
    hh_ready = sem("fd_hh_ready")
    hl_ready = sem("fd_hl_ready")
    added = sem("fd_added")
    summed = sem("fd_summed")
    sums_ready = sem("fd_sums_ready")
    sums_turned = sem("fd_sums_turned")
    out_vare_ready = sem("fd_out_vare_ready")
    out_rs_ready = sem("fd_out_rs_ready")
    y_ready = sem("fd_y_ready")
    stored = [sem(f"fd_stored{i}") for i in range(2)]
    dve_step = sem("fd_dve_step")

    def whole(eng, step, beside):
        for c in range(NC):
            for k in range(HC):
                step(c, 0, k)
            for part in range(3):
                beside(c, part)
                with eng.Fori(1 + 2 * part, 3 + 2 * part) as e:
                    for k in range(HC):
                        step(c, e, k)
            beside(c, 3)
            for k in range(HC):
                step(c, E - 1, k)

    def wait(eng, sem, value):
        if not (isinstance(value, int) and value <= 0):
            eng.wait_ge(sem, value)

    def take_x(act, c, ps):
        cols = slice(c * CH, (c + 1) * CH)
        act.wait_ge(x_turned, c + 1)
        if c >= 1:
            act.wait_ge(xl_ready, c)
        nc.scalar.activation(xT[:, :], ps, ACT.Copy).then_inc(xT_ready, 1)
        nc.scalar.activation(g.xh[:, cols], ps, ACT.Copy).then_inc(xh_ready, 1)

    def norm_stats(link, mv, of):
        for i in range(TPC):
            last = nc.vector.bn_stats(stats[:, i, :], of[:, i * C:(i + 1) * C])
        link(last)
        for i in range(TPC):
            last = nc.vector.bn_aggr(mv[:, i, :], stats[:, i, :])
        link(last)

    def norm_in_stats(dve, c):
        link = chain(dve, dve_step, steps)
        b, t0, rows = c // CPB, (c % CPB) * TPC, slice(c * TPC, (c + 1) * TPC)
        zc = z[:, c % 2, :]
        link(nc.vector.tensor_tensor(
            zc.rearrange("p (t g n) -> p t g n", t=TPC, g=HG),
            g.x0[:, rows, :].rearrange("p t (g n) -> p t g n", g=HG),
            g.ctx[:, b * HG:(b + 1) * HG, t0:t0 + TPC, :, :].rearrange("p g t h d -> p t g (h d)"), ALU.add))
        norm_stats(link, mv_in, zc)
        nc.vector.tensor_scalar(vare[:, 0, :], mv_in[:, :, 1], LN_EPS, None, ALU.add).then_inc(in_vare_ready, 1)

    def norm_in(dve, c):
        dve.wait_ge(in_rs_ready, c + 1)
        for i in range(TPC):
            last = nc.vector.tensor_scalar(xn[:, i, :], z[:, c % 2, i * C:(i + 1) * C], mv_in[:, i, 0:1], rs[:, 0, i:i + 1],
                                           ALU.subtract, ALU.mult)
        last.then_inc(x_ready, 1)

    def low_x(dve, c):
        dve.wait_ge(xh_ready, c + 1)
        nc.vector.tensor_tensor(g.xl[:, c * CH:(c + 1) * CH], xT[:, :], g.xh[:, c * CH:(c + 1) * CH],
                                ALU.subtract).then_inc(xl_ready, 1)

    def turn_x(pe, c, ps):
        pe.wait_ge(x_ready, c + 1)
        for i in range(TPC):
            last = nc.tensor.transpose(ps[:, i * P:(i + 1) * P], xn[:, i, :], g.ident[:, :])
        last.then_inc(x_turned, 1)

    def sync(sp):
        for c in range(NC):
            sp.wait_ge(y_ready, c + 1)
            sp.dma_start(a.out_tiles[:, c * TPC:(c + 1) * TPC, :], y[:, c % 2, :, :]).then_inc(stored[c % 2], 16)
        sp.wait_ge(stored[0], 16 * (NC // 2))
        sp.wait_ge(stored[1], 16 * (NC // 2))

    def gpsimd(pool):
        nc.gpsimd.memset(eye[:, :], 0.0).then_inc(eye_ready, 1)
        pool.wait_ge(eye_ready, 1)
        nc.gpsimd.affine_select(out=eye[:, :], in_=eye[:, :], compare_op=ALU.not_equal, fill=W_SCALE,
                                base=0, pattern=[[-1, P]], channel_multiplier=1).then_inc(eye_ready, 1)

        def rsqrt_in(c):
            pool.wait_ge(in_vare_ready, c + 1)
            nc.gpsimd.tensor_tensor(rs[:, 0, :], vare[:, 0, :], g.minus_half[:, 0:TPC], ALU.pow).then_inc(in_rs_ready, 1)

        def rsqrt_out(c):
            pool.wait_ge(out_vare_ready, c + 1)
            nc.gpsimd.tensor_tensor(rs[:, 1, :], vare[:, 1, :], g.minus_half[:, 0:TPC], ALU.pow).then_inc(out_rs_ready, 1)

        rsqrt_in(0)
        rsqrt_in(1)
        for c in range(NC):
            if c >= 1:
                rsqrt_out(c - 1)
            if c < NC - 2:
                rsqrt_in(c + 2)
        rsqrt_out(NC - 1)

    def scalar(act):
        def take_sums(c):
            act.wait_ge(summed, c + 1)
            if c >= 1:
                act.wait_ge(sums_turned, c)
            nc.scalar.activation(sums[:, :], sum_ps(c), ACT.Copy, scale=1.0 / W_SCALE).then_inc(sums_ready, 1)

        def high(n, k):
            act.wait_ge(h_ready, n + 1)
            wait(act, added, n - 2)
            nc.scalar.activation(hh[:, k, :], h32[:, k % 2, :], ACT.Copy).then_inc(hh_ready, 1)

        def step(c, e, k):
            n = c * STEPS + e * HC + k
            act.wait_ge(gate_ready, n + 1)
            wait(act, h_ready, n - 1)
            nc.scalar.activation(silu[:, k % 2, :], gate_ps(k), ACT.Silu, scale=1.0 / W_SCALE).then_inc(silu_ready, 1)
            if not (isinstance(n, int) and n == 0):
                high(n - 1, (k - 1) % HC)
            if c >= 1 and isinstance(e, int) and e == 0 and k == LAG:
                take_sums(c - 1)

        whole(act, step, lambda c, part: take_x(act, c + 1, turn_ps) if part == 2 and c < NC - 1 else None)
        high(NC * STEPS - 1, HC - 1)
        take_sums(NC - 1)

    def vector(dve, before):
        link = chain(dve, dve_step, steps)

        def norm_out_stats(c):
            dve.wait_ge(sums_turned, c + 1)
            norm_stats(link, mv_out, sum_ps(c))
            nc.vector.tensor_scalar(vare[:, 1, :], mv_out[:, :, 1], LN_EPS, None, ALU.add).then_inc(out_vare_ready, 1)

        def norm_out(c):
            dve.wait_ge(out_rs_ready, c + 1)
            if c >= 2:
                dve.wait_ge(stored[c % 2], 16)
            for i in range(TPC):
                last = nc.vector.tensor_scalar(y[:, c % 2, i, :], sum_ps(c)[:, i * C:(i + 1) * C], mv_out[:, i, 0:1],
                                               rs[:, 1, i:i + 1], ALU.subtract, ALU.mult)
            last.then_inc(y_ready, 1)

        def low(n, k):
            dve.wait_ge(hh_ready, n + 1)
            wait(dve, added, n - 2)
            nc.vector.tensor_tensor(hl[:, k, :], h32[:, k % 2, :], hh[:, k, :], ALU.subtract).then_inc(hl_ready, 1)

        def step(c, e, k):
            n = c * STEPS + e * HC + k
            dve.wait_ge(up_ready, n + 1)
            dve.wait_ge(silu_ready, n + 1)
            wait(dve, hl_ready, n - 1)
            nc.vector.scalar_tensor_tensor(out=h32[:, k % 2, :], in0=up_ps(k), scalar=1.0 / W_SCALE, in1=silu[:, k % 2, :],
                                           op0=ALU.mult, op1=ALU.mult).then_inc(h_ready, 1)
            if not (isinstance(n, int) and n == 0):
                low(n - 1, (k - 1) % HC)

        def beside(c, part):
            if part == 0 and c == 0:
                before.last_out(dve)
            if part == 0 and c >= 1:
                norm_out_stats(c - 1)
            if part == 1 and c < NC - 1:
                norm_in(dve, c + 1)
            if part == 2 and c >= 1:
                norm_out(c - 1)
            if part == 2 and c < NC - 1:
                low_x(dve, c + 1)
            if part == 3 and c < NC - 2:
                norm_in_stats(dve, c + 2)

        whole(dve, step, beside)
        low(NC * STEPS - 1, HC - 1)
        norm_out_stats(NC - 1)
        norm_out(NC - 1)

    def tensor(pe, before):
        def begin(c):
            if c >= 2:
                pe.wait_ge(y_ready, c - 1)
            nc.tensor.matmul(sum_ps(c), eye[:, :], g.xh[:, c * CH:(c + 1) * CH], start=True, stop=False, skip_group_check=True)

        def end(c):
            nc.tensor.matmul(sum_ps(c), eye[:, :], g.xl[:, c * CH:(c + 1) * CH], start=False, stop=True,
                             skip_group_check=True).then_inc(summed, 1)

        def turn_sums(c):
            pe.wait_ge(sums_ready, c + 1)
            for i in range(TPC):
                last = nc.tensor.transpose(sum_ps(c)[:, i * P:(i + 1) * P], sums[:, i * P:(i + 1) * P], g.ident[:, :])
            last.then_inc(sums_turned, 1)

        def add(c, e, k, n):
            pe.wait_ge(hl_ready, n + 1)
            wd = slice(2 * H + k * P, 2 * H + (k + 1) * P)
            for w, h in ((g.w1h, hh), (g.w1h, hl), (g.w1l, hh)):
                last = nc.tensor.matmul(sum_ps(c), w[:, bass.ds(e, 1), wd], h[:, k, :], start=False, stop=False,
                                        skip_group_check=True)
            last.then_inc(added, 1)

        def step(c, e, k):
            n = c * STEPS + e * HC + k
            x = slice(c * CH, (c + 1) * CH)
            if isinstance(e, int) and e == 0 and k == 0:
                pe.wait_ge(xl_ready, c + 1)
            wait(pe, silu_ready, n - 1)
            wait(pe, h_ready, n - 1)
            for ps, lo, done in ((gate_ps(k), 0, gate_ready), (up_ps(k), H, up_ready)):
                w = slice(lo + k * P, lo + (k + 1) * P)
                for i, (lhs, rhs) in enumerate(((g.w1h, g.xh), (g.w1h, g.xl), (g.w1l, g.xh))):
                    last = nc.tensor.matmul(ps, lhs[:, bass.ds(e, 1), w], rhs[:, x], start=(i == 0), stop=(i == 2))
                last.then_inc(done, 1)
            if k >= LAG:
                add(c, e, k - LAG, n - LAG)
            elif isinstance(e, int) and e == 0:
                if c >= 1:
                    add(c - 1, E - 1, k - LAG + HC, n - LAG)
                    if k == LAG - 1:
                        end(c - 1)
                        begin(c)
            else:
                add(c, e - 1, k - LAG + HC, n - LAG)

        pe.wait_ge(eye_ready, 2)
        pe.wait_ge(xl_ready, 1)
        begin(0)

        def beside(c, part):
            if part == 0 and c == 0:
                before.turn_last(pe)
            if part == 0 and c >= 1:
                turn_sums(c - 1)
            if part == 2 and c < NC - 1:
                turn_x(pe, c + 1, turn_ps)

        whole(pe, step, beside)
        for k in range(HC - LAG, HC):
            add(NC - 1, E - 1, k, NC * STEPS - HC + k)
        end(NC - 1)
        turn_sums(NC - 1)
    stage.sync = sync
    stage.gpsimd = gpsimd
    stage.scalar = scalar
    stage.vector = vector
    stage.tensor = tensor
    stage.take_x = take_x
    stage.norm_in_stats = norm_in_stats
    stage.norm_in = norm_in
    stage.low_x = low_x
    stage.turn_x = turn_x
    stage.xh_ready = xh_ready
    return stage


def layer1(nc, g, a):
    with ExitStack() as ctx:
        def sb(name, shape, dt=F32):
            return ctx.enter_context(nc.sbuf_tensor(name, shape, dt))

        m = Shared()
        m.qs = sb("qs", [P, GT, HPG, AUG])
        m.ks = sb("ks", [P, GT, HPG, AUG])
        m.scaled = sb("scaled", [P, GT, HPG, DH])
        m.qT = sb("qT", [P, 2, T], F32R)
        m.kT = sb("kT", [P, 2, T], F32R)
        m.va = sb("va", [P, 2, GT, HPG, AUG])
        m.ex = sb("ex_scores", [P, 2, HPG, T])
        m.cleared = ctx.enter_context(nc.semaphore("cleared"))
        m.large_ready = ctx.enter_context(nc.semaphore("large_ready"))
        m.hh = sb("fd_hh", [P, HC, CH], F16)
        m.hl = sb("fd_hl", [P, HC, CH], F16)
        idle = m.ex[:, :, :, :].rearrange("p a h t -> p (a h t)")
        m.xT_project, m.silu, m.h32 = (idle[:, i * 2 * CH:(i + 1) * 2 * CH].rearrange("p (a n) -> p a n", a=2) for i in range(3))
        m.sums = idle[:, 6 * CH:7 * CH]
        m.w_raw = idle[:, 7 * CH:7 * CH + 2 * C].rearrange("p (a n) -> p a n", a=2)
        m.w_T = idle[:, 8 * CH:8 * CH + 2 * C]
        m.squares = g.x1[:, :, :].rearrange("p t c -> p (t c)").rearrange("p (g t h d) -> p g t h d", g=NG, t=GT, h=HPG)
        m.oT = g.x1[:, 0:GT, :].rearrange("p t c -> p (t c)")
        m.xn = g.x1[:, GT:GT + TPC, :]
        m.xT = g.x1[:, GT + TPC:GT + 2 * TPC, :].rearrange("p t c -> p (t c)")
        m.z = g.moe[:, 0:2 * TPC, :].rearrange("p (a t) c -> p a (t c)", a=2)
        m.y = g.moe[:, 2 * TPC:4 * TPC, :].rearrange("p (a t) c -> p a t c", a=2)

        pj = project(nc, g, a, m, ctx)
        mx = maxima(nc, g, a, m, ctx)
        fd = feed(nc, g, a, m, ctx)
        at = attend(nc, g, a, m, ctx, fd)
        block = ctx.enter_context(nc.Block())

        @block.sync
        def _(sp):
            pj.sync(sp)
            at.sync(sp)
            fd.sync(sp)

        @block.gpsimd
        def _(pool):
            pj.gpsimd(pool)
            fd.gpsimd(pool)

        @block.scalar
        def _(act):
            pj.scalar(act)
            at.scalar(act)
            fd.scalar(act)

        @block.vector
        def _(dve):
            pj.vector(dve)
            mx.vector(dve)
            at.vector(dve)
            fd.vector(dve, at)

        @block.tensor
        def _(pe):
            pj.tensor(pe)
            mx.tensor(pe)
            at.tensor(pe)
            fd.tensor(pe, at)


def mixture0(nc, ctx, g):
    g.w0h = ctx.enter_context(nc.sbuf_tensor("w0h", [P, E, 2 * H], F16))
    g.w0l = ctx.enter_context(nc.sbuf_tensor("w0l", [P, E, 2 * H], F16))
    g.raw0 = ctx.enter_context(nc.sbuf_tensor("raw0", [P, E, 2 * H], F32))


def mixture1(nc, ctx, g):
    g.w1h = ctx.enter_context(nc.sbuf_tensor("w1h", [P, E, 3 * H], F16))
    g.w1l = ctx.enter_context(nc.sbuf_tensor("w1l", [P, E, 3 * H], F16))


def globals_(nc, ctx, g):
    def sb(name, shape, dt=F32):
        return ctx.enter_context(nc.sbuf_tensor(name, shape, dt))

    def sem(name):
        return ctx.enter_context(nc.semaphore(name))

    g.pb = ctx.enter_context(nc.psum_tensor("pb", [P, 8, CH], F32))
    g.x0 = sb("x0", [P, NT, C])
    g.x1 = sb("x1", [P, NT, C])
    g.ident = sb("ident", [P, P])
    g.minus_half = sb("minus_half", [P, NT])
    g.rstd2 = sb("rstd2", [P, NT])
    g.cols = sb("cols", [P, NCOLS])
    g.gate = sb("gate", [P, E, NT])
    g.gate_down = sb("gate_down", [P, E, NT])
    g.gate_down_flat = g.gate_down[:, :, :].rearrange("p e t -> p (e t)")
    g.moe = sb("moe", [P, NT, C])
    g.xh = sb("xh", [P, N], F16)
    g.xl = sb("xl", [P, N], F16)
    g.raw0_scaled = sem("raw0_scaled")
    g.w0h_ready = sem("w0h_ready")
    g.q = sb("q", [P, NG, GT, HPG, DH])
    g.v = sb("v", [P, NG, GT, HPG, DH])
    g.ctx = sb("ctx", [P, NG, GT, HPG, DH])
    g.qbit = sb("qbit", [P, NG, GT, HPG])
    g.kbit = sb("kbit", [P, NG, GT, HPG])
    g.lift = sb("lift", [P, NG, GT, HPG])
    g.large = sb("large", [P, 1], mybir.dt.int32)
    g.raw0_in = [sem(f"raw0_in{i}") for i in range(E // 2)]
    g.cols_ready = sem("cols_ready")
    g.junk_done = sem("junk_done")


_INS = ['L0_attn_x', 'L0_attn_ln1_w', 'L0_attn_ln2_w', 'L0_attn_time_decay', 'L0_attn_time_first', 'L0_attn_time_mix_k',
        'L0_attn_time_mix_v', 'L0_attn_time_mix_r', 'L0_attn_W_key', 'L0_attn_W_value', 'L0_attn_W_recept',
        'L0_attn_W_out', 'L0_attn_time_mix_k2', 'L0_attn_time_mix_r2', 'L0_attn_W_key2', 'L0_attn_W_value2',
        'L0_attn_W_recept2', 'L0_ffn_wg', 'L0_ffn_w1', 'L0_ffn_b1', 'L0_ffn_w2', 'L0_ffn_b2', 'L1_attn_qk_w',
        'L1_attn_qk_b', 'L1_attn_v_w', 'L1_attn_v_b', 'L1_attn_hash_a', 'L1_ffn_Wg', 'L1_ffn_Wu', 'L1_ffn_Wd']


def inputs(a, aps):
    (a.x, a.ln1_w, a.ln2_w, a.decay, a.first, a.mix_k, a.mix_v, a.mix_r, a.W_key, a.W_value, a.W_recept, a.W_out,
     a.mix_k2, a.mix_r2, a.W_key2, a.W_value2, a.W_recept2, a.wg, a.w1, a.b1, a.w2, a.b2, a.qk_w, a.qk_b, a.v_w, a.v_b,
     a.hash_a, a.Wg, a.Wu, a.Wd) = aps
    a.x_tiles = a.x.rearrange("b (t p) c -> p (b t) c", p=P)


def program(nc, *aps):
    with ExitStack() as ctx:
        g, a = Shared(), Shared()
        inputs(a, aps[:-1])
        a.out_tiles = aps[-1].rearrange("b (t p) c -> p (b t) c", p=P)
        globals_(nc, ctx, g)
        with ExitStack() as weights:
            mixture0(nc, weights, g)
            time_mix(nc, g, a)
            layer0_rest(nc, g, a)
        with ExitStack() as weights:
            mixture1(nc, weights, g)
            layer1(nc, g, a)


_OUTS = [((B, T, C), 'float32')]


def kernel(**inputs):
    import numpy as _np
    import concourse.bacc as _bacc
    from concourse import mybir as _mybir
    from concourse.bass_utils import run_bass_kernel_spmd as _run

    nc = _bacc.Bacc("TRN2", target_bir_lowering=False, num_devices=1)
    arrays, args = {}, []
    for name in _INS:
        a = _np.ascontiguousarray(inputs[name])
        arrays[f"in_{name}_dram"] = a
        args.append(nc.dram_tensor(f"in_{name}_dram", a.shape, _mybir.dt.from_np(a.dtype), kind="ExternalInput").ap())
    for i, (shape, dtype) in enumerate(_OUTS):
        dt = _mybir.dt.from_np(_np.dtype(dtype))
        args.append(nc.dram_tensor(f"out_{i}_dram", shape, dt, kind="ExternalOutput").ap())
    program(nc, *args)
    r = _run(nc, [arrays], core_ids=[0])
    return r.results[0]["out_0_dram"]
```
